# Optimizing a Trainium2 kernel written in Bass

```python
import numpy as np
import jax
import jax.numpy as jnp

def _softmax(x, axis=-1):
    return jax.nn.softmax(x, axis=axis)

def _gelu(x):
    return jax.nn.gelu(x, approximate=True)

def _silu(x):
    return jax.nn.silu(x)

def _sigmoid(x):
    return jax.nn.sigmoid(x)

def _layernorm(x, axis=-1, eps=1e-05):
    m = jnp.mean(x, axis=axis, keepdims=True)
    v = jnp.var(x, axis=axis, keepdims=True)
    return (x - m) / jnp.sqrt(v + eps)

def _scatter_add(tgt, idx, src, axis=0):
    return tgt.at[idx].add(src)

def _segment_sum(src, seg, n):
    return jax.ops.segment_sum(src, seg, n)
kernel_name = 'mk_seq_preln_d2_jaxref_r8_be0096'

def setup_inputs(seed: int=0):
    np.random.seed(seed)
    _w = jnp.asarray

    def _L0_attn_setup():
        import jax, jax.numpy as jnp
        import numpy as np
        HIDDEN_DIM = 128
        NUM_HEADS = 16
        LN_EPS = 1e-06

        def _layernorm(x, scale, bias):
            mu = jnp.mean(x, axis=-1, keepdims=True)
            var = jnp.mean(jnp.square(x - mu), axis=-1, keepdims=True)
            return (x - mu) * jax.lax.rsqrt(var + LN_EPS) * scale + bias
        key = jax.random.key(seed)
        ks = jax.random.split(key, 4)
        B, S, D = (2, 256, HIDDEN_DIM)
        x = jax.random.normal(ks[0], (B, S, D), dtype=jnp.float32)
        scale = 1.0 / np.sqrt(D)
        wq = jax.random.normal(ks[1], (D, HIDDEN_DIM), dtype=jnp.float32) * scale
        wk = jax.random.normal(ks[2], (D, HIDDEN_DIM), dtype=jnp.float32) * scale
        wv = jax.random.normal(ks[3], (D, HIDDEN_DIM), dtype=jnp.float32) * scale
        ln_scale = jnp.ones((D,), dtype=jnp.float32)
        ln_bias = jnp.zeros((D,), dtype=jnp.float32)
        return {'x': x, 'ln_scale': ln_scale, 'ln_bias': ln_bias, 'wq': wq, 'wk': wk, 'wv': wv}
    _L0_attn_in = _L0_attn_setup()

    def _L0_ffn_setup():
        import jax, jax.numpy as jnp
        import numpy as np
        B, S, D, E, H, K = (4, 256, 128, 8, 64, 2)
        key = jax.random.key(seed)
        ks = jax.random.split(key, 11)
        sc = 0.02
        return {'x': jax.random.normal(ks[0], (B, S, D), dtype=jnp.float32), 'gate_W': jax.random.normal(ks[1], (D, E), dtype=jnp.float32) * sc, 'W1': jax.random.normal(ks[2], (E, D, H), dtype=jnp.float32) * sc, 'b1': jnp.zeros((E, H), dtype=jnp.float32), 'W2': jax.random.normal(ks[3], (E, H, D), dtype=jnp.float32) * sc, 'b2': jnp.zeros((E, D), dtype=jnp.float32), 'Ws1': jax.random.normal(ks[4], (D, H), dtype=jnp.float32) * sc, 'bs1': jnp.zeros((H,), dtype=jnp.float32), 'Ws2': jax.random.normal(ks[5], (H, D), dtype=jnp.float32) * sc, 'bs2': jnp.zeros((D,), dtype=jnp.float32), 'route_scale': jnp.ones((), dtype=jnp.float32)}
    _L0_ffn_in = _L0_ffn_setup()

    def _L1_attn_setup():
        import jax, jax.numpy as jnp
        import numpy as np
        B, T, HID = (16, 64, 128)
        NH, NKV, D = (8, 4, 128)
        THETA = 10000.0

        def _rotate_half(x):
            x1, x2 = (x[..., :x.shape[-1] // 2], x[..., x.shape[-1] // 2:])
            return jnp.concatenate((-x2, x1), axis=-1)
        key = jax.random.key(seed)
        k0, k1, k2, k3, k4 = jax.random.split(key, 5)
        s = 0.02
        return {'hidden_states': jax.random.normal(k0, (B, T, HID), dtype=jnp.float32), 'Wq': s * jax.random.normal(k1, (HID, NH * D), dtype=jnp.float32), 'Wk': s * jax.random.normal(k2, (HID, NKV * D), dtype=jnp.float32), 'Wv': s * jax.random.normal(k3, (HID, NKV * D), dtype=jnp.float32), 'Wo': s * jax.random.normal(k4, (NH * D, HID), dtype=jnp.float32)}
    _L1_attn_in = _L1_attn_setup()

    def _L1_ffn_setup():
        import jax, jax.numpy as jnp
        import numpy as np
        ALPHA = 1.702
        LIMIT = 7.0
        EPS = 1e-05
        E = 16
        K = 4

        def _swiglu(h):
            x_glu = jnp.minimum(h[..., ::2], LIMIT)
            x_lin = jnp.clip(h[..., 1::2], LIMIT, LIMIT)
            return x_glu * jax.nn.sigmoid(ALPHA * x_glu) * (x_lin + 1.0)
        key = jax.random.key(seed)
        ks = jax.random.split(key, 7)
        B, T, H, I = (1, 256, 128, 128)
        x = jax.random.normal(ks[0], (B, T, H), jnp.float32)
        scale = jnp.ones((H,), jnp.float32)
        gate_w = jax.random.normal(ks[1], (E, H), jnp.float32) * 0.02
        gate_b = jnp.zeros((E,), jnp.float32)
        mlp1_w = jax.random.normal(ks[2], (E, 2 * I, H), jnp.float32) * 0.02
        mlp1_b = jax.random.normal(ks[3], (E, 2 * I), jnp.float32) * 0.02
        mlp2_w = jax.random.normal(ks[4], (E, H, I), jnp.float32) * 0.02
        mlp2_b = jax.random.normal(ks[5], (E, H), jnp.float32) * 0.02
        return dict(x=x, scale=scale, gate_w=gate_w, gate_b=gate_b, mlp1_w=mlp1_w, mlp1_b=mlp1_b, mlp2_w=mlp2_w, mlp2_b=mlp2_b)
    _L1_ffn_in = _L1_ffn_setup()
    _d = {'L0_attn_x': _L0_attn_in['x'], 'L0_attn_ln_scale': _L0_attn_in['ln_scale'], 'L0_attn_ln_bias': _L0_attn_in['ln_bias'], 'L0_attn_wq': _L0_attn_in['wq'], 'L0_attn_wk': _L0_attn_in['wk'], 'L0_attn_wv': _L0_attn_in['wv'], 'L0_ffn_gate_W': _L0_ffn_in['gate_W'], 'L0_ffn_W1': _L0_ffn_in['W1'], 'L0_ffn_b1': _L0_ffn_in['b1'], 'L0_ffn_W2': _L0_ffn_in['W2'], 'L0_ffn_b2': _L0_ffn_in['b2'], 'L0_ffn_Ws1': _L0_ffn_in['Ws1'], 'L0_ffn_bs1': _L0_ffn_in['bs1'], 'L0_ffn_Ws2': _L0_ffn_in['Ws2'], 'L0_ffn_bs2': _L0_ffn_in['bs2'], 'L0_ffn_route_scale': _L0_ffn_in['route_scale'], 'L1_attn_Wq': _L1_attn_in['Wq'], 'L1_attn_Wk': _L1_attn_in['Wk'], 'L1_attn_Wv': _L1_attn_in['Wv'], 'L1_attn_Wo': _L1_attn_in['Wo'], 'L1_ffn_scale': _L1_ffn_in['scale'], 'L1_ffn_gate_w': _L1_ffn_in['gate_w'], 'L1_ffn_gate_b': _L1_ffn_in['gate_b'], 'L1_ffn_mlp1_w': _L1_ffn_in['mlp1_w'], 'L1_ffn_mlp1_b': _L1_ffn_in['mlp1_b'], 'L1_ffn_mlp2_w': _L1_ffn_in['mlp2_w'], 'L1_ffn_mlp2_b': _L1_ffn_in['mlp2_b']}
    _x0 = _d['L0_attn_x']
    _d['L0_attn_x'] = jax.random.normal(jax.random.fold_in(jax.random.key(seed), 1), (2, 1024, 128), dtype=_x0.dtype)
    del _x0
    return _d

def reference(L0_attn_x, L0_attn_ln_scale, L0_attn_ln_bias, L0_attn_wq, L0_attn_wk, L0_attn_wv, L0_ffn_gate_W, L0_ffn_W1, L0_ffn_b1, L0_ffn_W2, L0_ffn_b2, L0_ffn_Ws1, L0_ffn_bs1, L0_ffn_Ws2, L0_ffn_bs2, L0_ffn_route_scale, L1_attn_Wq, L1_attn_Wk, L1_attn_Wv, L1_attn_Wo, L1_ffn_scale, L1_ffn_gate_w, L1_ffn_gate_b, L1_ffn_mlp1_w, L1_ffn_mlp1_b, L1_ffn_mlp2_w, L1_ffn_mlp2_b):

    def _L0_attn_ref(x, ln_scale, ln_bias, wq, wk, wv):
        import jax, jax.numpy as jnp
        import numpy as np
        HIDDEN_DIM = 128
        NUM_HEADS = 16
        LN_EPS = 1e-06

        def _layernorm(x, scale, bias):
            mu = jnp.mean(x, axis=-1, keepdims=True)
            var = jnp.mean(jnp.square(x - mu), axis=-1, keepdims=True)
            return (x - mu) * jax.lax.rsqrt(var + LN_EPS) * scale + bias
        bs, sl, fdim = x.shape
        h, hd = (NUM_HEADS, HIDDEN_DIM // NUM_HEADS)
        xn = _layernorm(x, ln_scale, ln_bias)
        q = (xn @ wq).reshape(bs, sl, h, hd).transpose(0, 2, 1, 3)
        k = (xn @ wk).reshape(bs, sl, h, hd).transpose(0, 2, 1, 3)
        v = (xn @ wv).reshape(bs, sl, h, hd).transpose(0, 2, 1, 3)
        scores = jnp.einsum('bhid,bhjd->bhij', q, k)
        probs = jax.nn.softmax(scores / jnp.sqrt(jnp.float32(HIDDEN_DIM)), axis=-1)
        out = jnp.einsum('bhij,bhjd->bhid', probs, v)
        out = out.transpose(0, 2, 1, 3).reshape(bs, sl, -1) + xn
        return out

    def _L0_ffn_ref(x, gate_W, W1, b1, W2, b2, Ws1, bs1, Ws2, bs2, route_scale):
        import jax, jax.numpy as jnp
        import numpy as np
        B, S, D, E, H, K = (4, 256, 128, 8, 64, 2)
        scores = jax.nn.sigmoid(x @ gate_W) * route_scale
        topk_scores, topk_idx = jax.lax.top_k(scores, K)
        topk_w = topk_scores / topk_scores.sum(-1, keepdims=True)
        onehot = jax.nn.one_hot(topk_idx, E, dtype=x.dtype)
        gate_full = jnp.einsum('bsk,bske->bse', topk_w, onehot)
        h = jax.nn.gelu(jnp.einsum('bsd,edh->bseh', x, W1) + b1, approximate=False)
        y = jnp.einsum('bseh,ehd->bsed', h, W2) + b2
        expert_out = jnp.einsum('bse,bsed->bsd', gate_full, y)
        shared = jax.nn.gelu(x @ Ws1 + bs1, approximate=False) @ Ws2 + bs2
        return expert_out + shared

    def _L1_attn_ref(hidden_states, Wq, Wk, Wv, Wo):
        import jax, jax.numpy as jnp
        import numpy as np
        B, T, HID = (16, 64, 128)
        NH, NKV, D = (8, 4, 128)
        THETA = 10000.0

        def _rotate_half(x):
            x1, x2 = (x[..., :x.shape[-1] // 2], x[..., x.shape[-1] // 2:])
            return jnp.concatenate((-x2, x1), axis=-1)
        b, t, _ = hidden_states.shape
        q = (hidden_states @ Wq).reshape(b, t, NH, D).transpose(0, 2, 1, 3)
        k = (hidden_states @ Wk).reshape(b, t, NKV, D).transpose(0, 2, 1, 3)
        v = (hidden_states @ Wv).reshape(b, t, NKV, D).transpose(0, 2, 1, 3)
        inv_freq = 1.0 / THETA ** (jnp.arange(0, D, 2, dtype=jnp.float32) / D)
        freqs = jnp.outer(jnp.arange(t, dtype=jnp.float32), inv_freq)
        emb = jnp.concatenate((freqs, freqs), axis=-1)
        cos, sin = (jnp.cos(emb), jnp.sin(emb))
        q = q * cos + _rotate_half(q) * sin
        k = k * cos + _rotate_half(k) * sin
        groups = NH // NKV
        k = jnp.repeat(k, groups, axis=1)
        v = jnp.repeat(v, groups, axis=1)
        scale = 1.0 / jnp.sqrt(jnp.float32(D))
        attn = jnp.einsum('bhtd,bhsd->bhts', q, k) * scale
        causal = jnp.triu(jnp.ones((t, t), dtype=bool), k=1)
        attn = jnp.where(causal, -jnp.inf, attn)
        attn = jax.nn.softmax(attn, axis=-1)
        out = jnp.einsum('bhts,bhsd->bhtd', attn, v)
        out = out.transpose(0, 2, 1, 3).reshape(b, t, NH * D)
        return out @ Wo

    def _L1_ffn_ref(x, scale, gate_w, gate_b, mlp1_w, mlp1_b, mlp2_w, mlp2_b):
        import jax, jax.numpy as jnp
        import numpy as np
        ALPHA = 1.702
        LIMIT = 7.0
        EPS = 1e-05
        E = 16
        K = 4

        def _swiglu(h):
            x_glu = jnp.minimum(h[..., ::2], LIMIT)
            x_lin = jnp.clip(h[..., 1::2], LIMIT, LIMIT)
            return x_glu * jax.nn.sigmoid(ALPHA * x_glu) * (x_lin + 1.0)
        t = x * jax.lax.rsqrt(jnp.mean(x * x, axis=-1, keepdims=True) + EPS) * scale
        g = jnp.einsum('bth,eh->bte', t, gate_w) + gate_b
        vals, idx = jax.lax.top_k(g, K)
        w = jax.nn.softmax(vals, axis=-1)
        route = jnp.sum(jax.nn.one_hot(idx, E, dtype=t.dtype) * w[..., None], axis=-2)
        route_e = jnp.moveaxis(route, -1, 0)

        def step(acc, p):
            w1, b1, w2, b2, r = p
            h = jnp.einsum('bth,ih->bti', t, w1) + b1
            s = _swiglu(h)
            y = jnp.einsum('bti,hi->bth', s, w2) + b2
            return (acc + r[..., None] * y, None)
        acc, _ = jax.lax.scan(step, jnp.zeros_like(x), (mlp1_w, mlp1_b, mlp2_w, mlp2_b, route_e))
        return x + acc
    x = L0_attn_x
    x = x + _L0_attn_ref(_layernorm(x, axis=-1), L0_attn_ln_scale, L0_attn_ln_bias, L0_attn_wq, L0_attn_wk, L0_attn_wv)
    x = x + _L0_ffn_ref(_layernorm(x, axis=-1), L0_ffn_gate_W, L0_ffn_W1, L0_ffn_b1, L0_ffn_W2, L0_ffn_b2, L0_ffn_Ws1, L0_ffn_bs1, L0_ffn_Ws2, L0_ffn_bs2, L0_ffn_route_scale)
    x = x + _L1_attn_ref(_layernorm(x, axis=-1), L1_attn_Wq, L1_attn_Wk, L1_attn_Wv, L1_attn_Wo)
    x = x + _L1_ffn_ref(_layernorm(x, axis=-1), L1_ffn_scale, L1_ffn_gate_w, L1_ffn_gate_b, L1_ffn_mlp1_w, L1_ffn_mlp1_b, L1_ffn_mlp2_w, L1_ffn_mlp2_b)
    return x

_drawn_inputs = setup_inputs


def setup_inputs(seed=0):
    import zlib

    import numpy as np

    out = dict(_drawn_inputs(seed))
    spreads = {'L0_attn_ln_scale': (1.0, 0.2),
     'L0_attn_ln_bias': (0.0, 0.1),
     'L0_ffn_b1': (0.0, 0.8),
     'L0_ffn_b2': (0.0, 0.1),
     'L0_ffn_bs1': (0.0, 0.8),
     'L0_ffn_bs2': (0.0, 0.1),
     'L1_ffn_scale': (1.0, 0.6),
     'L1_ffn_gate_b': (0.0, 0.361)}
    factors = {'L0_attn_wq': 4.023,
     'L0_attn_wk': 3.959,
     'L0_ffn_W1': 7.964,
     'L0_ffn_W2': 7.369,
     'L0_ffn_Ws1': 5.63,
     'L0_ffn_Ws2': 5.073,
     'L1_attn_Wq': 8.0,
     'L1_attn_Wk': 8.0,
     'L1_attn_Wv': 6.576,
     'L1_attn_Wo': 6.353,
     'L1_ffn_mlp1_b': 24.996,
     'L1_ffn_mlp2_b': 25.868}
    for name, (base, spread) in spreads.items():
        noise = np.random.default_rng([zlib.crc32(name.encode()), seed]).standard_normal(out[name].shape)
        drawn = base * np.exp(spread * noise) if base else spread * noise
        out[name] = jnp.asarray(drawn.astype(out[name].dtype))
    for name, factor in factors.items():
        out[name] = (out[name] * factor).astype(out[name].dtype)
    return out
```

```python
from contextlib import ExitStack

import concourse.bass as bass
from concourse import mybir

F32 = mybir.dt.float32
BF16 = mybir.dt.bfloat16
ALU = mybir.AluOpType
ACT = mybir.ActivationFunctionType
AX_X = mybir.AxisListType.X

P = 128
B, S, D = 2, 1024, 128
T = B * S
NT = T // P
TB = S // P
CH = 512
NCH = T // CH

H0, HD0 = 16, 8
NPAIR = B * H0 // 2
SLOT = 64
NST = 6 * HD0
VW = 32

H1, KV1, D1 = 8, 4, 128
GQ = H1 // KV1

E0, K0, F0 = 8, 2, 64
E1, K1, F1 = 16, 4, 128
ALPHA, LIMIT = 1.702, 7.0
LOW, HIGH = -3.0e38, 3.0e38
SCALE0 = 1.0 / 128.0 ** 0.5


class Tensors:
    pass


class Chain:

    def __init__(self, engine, sem):
        self.engine, self.sem, self.n = engine, sem, 0

    def after(self, instruction):
        self.n += 1
        instruction.then_inc(self.sem, 1)
        self.engine.wait_ge(self.sem, self.n)


def over_features(column):
    return column.unsqueeze(2).broadcast_to([P, NT, D])


def normalise(dve, chain, dst, src, work, stat, eps, root_asked, root_given, turn):
    total, square_total, variance, root, inverse = (stat[:, i, :] for i in range(5))
    centred, squares = work
    chain.after(dve.reduce_sum(total, src, AX_X))
    chain.after(dve.scalar_tensor_tensor(out=centred, in0=over_features(total), scalar=-1.0 / D, in1=src,
                                         op0=ALU.mult, op1=ALU.add))
    chain.after(dve.tensor_tensor(squares, centred, centred, ALU.mult))
    chain.after(dve.reduce_sum(square_total, squares, AX_X))
    dve.tensor_scalar(variance, square_total, 1.0 / D, eps, ALU.mult, ALU.add).then_inc(root_asked, 1)
    dve.wait_ge(root_given, turn + 1)
    chain.after(dve.reciprocal(inverse, root))
    chain.after(dve.tensor_tensor(dst, centred, over_features(inverse), ALU.mult))


def take_root(act, stat, root_asked, root_given, turn):
    act.wait_ge(root_asked, turn + 1)
    act.activation(stat[:, 3, :], stat[:, 2, :], ACT.Sqrt).then_inc(root_given, 1)


def transpose_tiles(pe, dst_bank, src, identity, chunk):
    for c in range(CH // P):
        last = pe.transpose(dst_bank[:, c * P:(c + 1) * P], src[:, chunk * (CH // P) + c, :], identity)
    return last


def layer0_project(nc, t, d):
    ctx = ExitStack()
    with ctx:
        def sb(name, shape, dt=F32):
            return ctx.enter_context(nc.sbuf_tensor(name, shape, dt))

        def sem(name):
            return ctx.enter_context(nc.semaphore(name))

        normed = sb("l0_normed", [P, NT, D])
        centred = sb("l0_centred", [P, NT, D])
        squares = sb("l0_squares", [P, NT, D])
        normedT = sb("l0_normedT", [P, T])
        stat = sb("l0_stat", [P, 5, NT])
        w_qkv = sb("l0_w_qkv", [P, 3, D])
        affine = sb("l0_affine", [P, 2, D])
        parts = [sb("l0_q_parts", [P, 3, T], BF16), sb("l0_k_parts", [P, 3, T], BF16)]
        rest = sb("l0_rest", [P, 2, CH])
        banks = [ctx.enter_context(nc.psum_tensor(f"l0_bank{i}", [P, CH], F32)) for i in range(4)]

        x_in, w_in = sem("x_in"), sem("w_in")
        dve_step, root_asked, root_given = sem("dve_step"), sem("root_asked"), sem("root_given")
        normed_ready, tr_ready, tr_out = sem("normed_ready"), sem("tr_ready"), sem("tr_out")
        qk_ready, hi_ready, rest_ready = sem("qk_ready"), sem("hi_ready"), sem("rest_ready")
        mid_ready, lo_ready = sem("mid_ready"), sem("lo_ready")
        v_ready, v_out, parts_out = sem("v_ready"), sem("v_out"), sem("parts_out")
        consts_in = sem("consts_in")

        with nc.Block() as block:
            @block.sync
            def _(sp):
                sp.dma_start(t.x[:, :, :], d["L0_attn_x"].rearrange("b (t p) d -> p (b t) d", p=P)).then_inc(x_in, 16)
                for i, name in enumerate(("L0_attn_wq", "L0_attn_wk", "L0_attn_wv")):
                    sp.dma_start(w_qkv[:, i, :], d[name]).then_inc(w_in, 16)
                for i, name in enumerate(("L0_attn_ln_scale", "L0_attn_ln_bias")):
                    sp.dma_start(affine[:, i, :], d[name].partition_broadcast(P)).then_inc(w_in, 16)
                sp.dma_start(t.identity[:, :], d["identity"]).then_inc(w_in, 16)
                for which in range(2):
                    for b in range(B):
                        sp.wait_ge(lo_ready, which * NCH + (b + 1) * (NCH // B))
                        sp.dma_start(t.parts_dram[which][:, b * P:(b + 1) * P, :].rearrange("a r s -> r a s"),
                                     parts[which][:, :, b * S:(b + 1) * S]).then_inc(parts_out, 16)
                sp.wait_ge(parts_out, 16 * 2 * B)

            @block.gpsimd
            def _(pool):
                pool.dma_start(t.rope[:, :, :], d["rope"].rearrange("a p s -> p a s")).then_inc(consts_in, 16)
                pool.wait_ge(consts_in, 16)

            @block.vector
            def _(dve):
                chain = Chain(dve, dve_step)
                dve.wait_ge(x_in, 16)
                work = (centred[:, :, :], squares[:, :, :])
                normalise(dve, chain, normed[:, :, :], t.x[:, :, :], work, stat, 1e-5, root_asked, root_given, 0)
                normalise(dve, chain, normed[:, :, :], normed[:, :, :], work, stat, 1e-6, root_asked, root_given, 1)
                dve.wait_ge(w_in, 16 * 6)
                scale, bias = (affine[:, i, :].unsqueeze(1).broadcast_to([P, NT, D]) for i in range(2))
                chain.after(dve.tensor_tensor(centred[:, :, :], normed[:, :, :], scale, ALU.mult))
                dve.tensor_tensor(normed[:, :, :], centred[:, :, :], bias, ALU.add).then_inc(normed_ready, 1)
                for c in range(NCH):
                    dve.wait_ge(tr_ready, c + 1)
                    dve.tensor_copy(normedT[:, c * CH:(c + 1) * CH], banks[c][:, :]).then_inc(tr_out, 1)
                dve.wait_ge(normed_ready, 1)
                dve.tensor_tensor(t.x[:, :, :], t.x[:, :, :], normed[:, :, :], ALU.add)
                for u in range(2 * NCH):
                    which, c = u // NCH, u % NCH
                    cols = slice(c * CH, (c + 1) * CH)
                    dve.wait_ge(hi_ready, u + 1)
                    dve.tensor_tensor(rest[:, u % 2, :], banks[u % 4][:, :], parts[which][:, 0, cols],
                                      ALU.subtract).then_inc(rest_ready, 1)
                    dve.wait_ge(mid_ready, u + 1)
                    dve.tensor_tensor(parts[which][:, 2, cols], rest[:, u % 2, :], parts[which][:, 1, cols],
                                      ALU.subtract).then_inc(lo_ready, 1)
                for c in range(NCH):
                    b, first = c // (NCH // B), (c % (NCH // B)) * 4
                    dve.wait_ge(v_ready, c + 1)
                    dst = t.values0[:, b * H0 * S // P * HD0:(b + 1) * H0 * S // P * HD0].rearrange(
                        "p (h t w) -> p t h w", h=H0, w=HD0)[:, first:first + 4, :, :]
                    dve.tensor_copy(dst, banks[c][:, :].rearrange("p (t h w) -> p t h w", t=4, w=HD0)).then_inc(v_out, 1)

            @block.scalar
            def _(act):
                take_root(act, stat, root_asked, root_given, 0)
                take_root(act, stat, root_asked, root_given, 1)
                for u in range(2 * NCH):
                    which, c = u // NCH, u % NCH
                    cols = slice(c * CH, (c + 1) * CH)
                    act.wait_ge(qk_ready, u + 1)
                    act.activation(parts[which][:, 0, cols], banks[u % 4][:, :], ACT.Copy).then_inc(hi_ready, 1)
                    act.wait_ge(rest_ready, u + 1)
                    act.activation(parts[which][:, 1, cols], rest[:, u % 2, :], ACT.Copy).then_inc(mid_ready, 1)

            @block.tensor
            def _(pe):
                pe.wait_ge(w_in, 16 * 6)
                pe.wait_ge(normed_ready, 1)
                for c in range(NCH):
                    transpose_tiles(pe, banks[c], normed, t.identity[:, :], c).then_inc(tr_ready, 1)
                for u in range(2 * NCH):
                    which, c = u // NCH, u % NCH
                    if u < NCH:
                        pe.wait_ge(tr_out, NCH if u == 0 else NCH)
                    else:
                        pe.wait_ge(rest_ready, u - 3)
                    pe.matmul(banks[u % 4][:, :], w_qkv[:, which, :], normedT[:, c * CH:(c + 1) * CH],
                              start=True, stop=True).then_inc(qk_ready, 1)
                for c in range(NCH):
                    pe.wait_ge(rest_ready, NCH + c + 1)
                    for k in range(4):
                        tile = 4 * c + k
                        last = pe.matmul(banks[c][:, k * P:(k + 1) * P], normedT[:, tile * P:(tile + 1) * P],
                                         w_qkv[:, 2, :], start=True, stop=True)
                    last.then_inc(v_ready, 1)


def layer0_attention(nc, t, exact):
    rows = NST + 2 if exact else NST
    SLOTS = 8
    ctx = ExitStack()
    with ctx:
        def sb(name, shape, dt=F32):
            return ctx.enter_context(nc.sbuf_tensor(name, shape, dt))

        def ps(name, shape):
            return ctx.enter_context(nc.psum_tensor(name, shape, F32))

        def sem(name):
            return ctx.enter_context(nc.semaphore(name))

        q_stack = [sb(f"q_stack{i}", [P, S], BF16) for i in range(2)]
        k_stack = [sb(f"k_stack{i}", [P, S], BF16) for i in range(2)]
        v_tile = [sb(f"v_tile{i}", [P, 2, TB, VW]) for i in range(2)]
        probs = sb("probs", [P, SLOTS, S])
        heads = [sb(f"heads{i}", [P, CH]) for i in range(2)]
        inverse = sb("inverse", [P, 2, P // 8])
        maxima = sb("maxima", [P, 2 * TB])
        shift = sb("shift", [2 * TB, 2, P], BF16)
        scores = [ps(f"scores{i}", [P, S]) for i in range(2)]
        summed = ps("summed", [P, CH])
        turned = ps("turned", [P, CH])

        loaded = [sem(f"loaded{i}") for i in range(2)]
        staged, ones_set = sem("staged"), sem("ones_set")
        score_ready, prob_ready = sem("score_ready"), sem("prob_ready")
        prob_free, summed_free = sem("prob_free"), sem("summed_free")
        heads_ready, turned_ready, written, dve_step = sem("heads_ready"), sem("turned_ready"), sem("written"), sem("dve_step")
        plain_ready, max_ready, maxT_ready, shift_ready = sem("plain_ready"), sem("max_ready"), sem("maxT_ready"), sem("shift_ready")
        shift_in = [sem(f"shift_in{i}") for i in range(2)]

        with nc.Block() as block:
            @block.sync
            def _(sp):
                q_dram, k_dram = t.parts_dram

                def load(pair, par):
                    for x in range(2):
                        head = bass.ds(pair * (2 * HD0) + x * HD0, HD0)
                        for n, (q_part, k_part) in enumerate(((0, 0), (0, 1), (0, 2), (1, 0), (1, 1), (2, 0))):
                            rows_n = slice(x * SLOT + n * HD0, x * SLOT + (n + 1) * HD0)
                            sp.dma_start(q_stack[par][rows_n, :], q_dram[q_part, head, :]).then_inc(loaded[par], 16)
                            sp.dma_start(k_stack[par][rows_n, :], k_dram[k_part, head, :]).then_inc(loaded[par], 16)

                sp.wait_ge(ones_set, 4)
                for par in range(2):
                    load(par, par)
                with sp.Fori(0, NPAIR // 2 - 1) as i:
                    for par in range(2):
                        sp.wait_ge(score_ready, i * 32 + (par * 16 + 16))
                        load(i * 2 + (par + 2), par)

            @block.gpsimd
            def _(pool):
                for i in range(2):
                    for r in (32, 96):
                        pool.memset(k_stack[i][r:r + 32, :], 1.0).then_inc(ones_set, 1)
                pool.wait_ge(ones_set, 4)
                for i in range(2):
                    pool.memset(v_tile[i][:, :, :, :], 0.0).then_inc(ones_set, 1)
                pool.wait_ge(ones_set, 6)
                for i in range(2):
                    pool.memset(v_tile[i][:, :, :, HD0:HD0 + 1], 1.0).then_inc(ones_set, 1)

            @block.vector
            def _(dve):
                dve.wait_ge(ones_set, 8)

                def stage(pair, par):
                    for x in range(2):
                        src = t.values0[:, bass.ds(pair * (2 * TB * HD0) + x * TB * HD0, TB * HD0)]
                        dve.tensor_scalar(v_tile[par][:, x, :, 0:HD0], src.rearrange("p (t w) -> p t w", w=HD0), 1.0, None,
                                          ALU.mult).then_inc(staged, 1)

                with dve.Fori(0, NPAIR // 2) as i:
                    for par in range(2):
                        pair = i * 2 + par
                        dve.wait_ge(prob_free, i * 32 + (par * 16 + SLOTS))
                        stage(pair, par)
                        if exact:
                            for n in range(2 * TB):
                                dve.wait_ge(plain_ready, i * 32 + (par * 16 + n + 1))
                                dve.reduce_max(maxima[:, n:n + 1], scores[n % 2][:, :], AX_X).then_inc(max_ready, 1)
                            dve.wait_ge(maxT_ready, i * 2 + (par + 1))
                            mT = turned[0:2 * TB, 0:P]
                            dve.tensor_scalar(shift[:, 0, :], mT, -1.0, None, ALU.mult).then_inc(dve_step, 1)
                            dve.wait_ge(dve_step, i * 4 + (par * 2 + 1))
                            dve.scalar_tensor_tensor(out=shift[:, 1, :], in0=mT, scalar=-1.0, in1=shift[:, 0, :],
                                                     op0=ALU.mult, op1=ALU.subtract).then_inc(shift_ready, 1)
                        dve.wait_ge(prob_free, i * 32 + (par * 16 + 16 + SLOTS))
                        dve.tensor_copy(heads[par][:, :], summed[:, :]).then_inc(heads_ready, 1)
                        dve.wait_ge(turned_ready, i * 2 + (par + 1))
                        tv = turned[:, :].rearrange("p (c h w) -> p c h w", c=4, w=VW)
                        inv = inverse[:, par, :].rearrange("p (c h) -> p c h", c=4)
                        dve.reciprocal(inv, tv[:, :, :, HD0]).then_inc(dve_step, 1)
                        if exact:
                            dve.wait_ge(dve_step, i * 4 + (par * 2 + 2))
                        else:
                            dve.wait_ge(dve_step, i * 2 + (par + 1))
                        dst = t.attn0[:, bass.ds(pair * P, P)].rearrange("p (h c w) -> p c h w", h=4, w=HD0)
                        dve.tensor_tensor(dst, tv[:, :, :, 0:HD0], inv.unsqueeze(3).broadcast_to([P, 4, 4, HD0]),
                                          ALU.mult).then_inc(written, 1)

            @block.scalar
            def _(act):
                with act.Fori(0, NPAIR // 2) as i:
                    for par in range(2):
                        if exact:
                            act.wait_ge(shift_ready, i * 2 + (par + 1))
                            for x in range(2):
                                for part in range(2):
                                    row = x * SLOT + NST + part
                                    act.dma_start(q_stack[par][row:row + 1, :], shift[x * TB:(x + 1) * TB, part, :]).then_inc(shift_in[par], 16)
                        for n in range(2 * TB):
                            act.wait_ge(score_ready, i * 32 + (par * 16 + n + 1))
                            act.wait_ge(prob_free, i * 32 + (par * 16 + n + 1))
                            act.activation(probs[:, n % SLOTS, :], scores[n % 2][:, :], ACT.Exp, scale=SCALE0).then_inc(prob_ready, 1)

            @block.tensor
            def _(pe):
                pe.sem_inc(prob_free, SLOTS)

                def score(par, k, x, n):
                    r = x * SLOT
                    for half in range(2):
                        last = pe.matmul(scores[x][:, half * CH:(half + 1) * CH],
                                         k_stack[par][r:r + rows, k * P:(k + 1) * P],
                                         q_stack[par][r:r + rows, half * CH:(half + 1) * CH], start=True, stop=True)
                    last.then_inc(score_ready, 1)

                with pe.Fori(0, NPAIR // 2) as i:
                    for par in range(2):
                        pe.wait_ge(loaded[par], (i + 1) * (24 * 16))
                        if exact:
                            for n in range(2 * TB):
                                x, qt = n // TB, n % TB
                                r = x * SLOT
                                if n < 2:
                                    pe.wait_ge(prob_ready, i * 32 + par * 16)
                                else:
                                    pe.wait_ge(max_ready, i * 32 + (par * 16 + n - 1))
                                for half in range(2):
                                    last = pe.matmul(scores[n % 2][:, half * CH:(half + 1) * CH],
                                                     q_stack[par][r:r + NST, qt * P:(qt + 1) * P],
                                                     k_stack[par][r:r + NST, half * CH:(half + 1) * CH], start=True, stop=True)
                                last.then_inc(plain_ready, 1)
                            pe.wait_ge(max_ready, i * 32 + (par * 16 + 16))
                            pe.wait_ge(written, i * 2 + par)
                            pe.transpose(turned[0:2 * TB, 0:P], maxima[:, :], t.identity[:, :]).then_inc(maxT_ready, 1)
                            pe.wait_ge(shift_in[par], (i + 1) * 64)
                        for k in range(TB + 1):
                            if k < TB:
                                for x in range(2):
                                    if k == 0:
                                        pe.wait_ge(prob_ready, i * 32 + par * 16)
                                    else:
                                        pe.wait_ge(prob_ready, i * 32 + (par * 16 + 2 * k + x - 1))
                                    score(par, k, x, 2 * k + x)
                            if k == 0:
                                pe.wait_ge(staged, i * 4 + (par * 2 + 2))
                                pe.wait_ge(heads_ready, i * 2 + par)
                            if k > 0:
                                pe.wait_ge(prob_ready, i * 32 + (par * 16 + 2 * k))
                                for x in range(2):
                                    for half in range(2):
                                        g = 32 * (2 * x + half)
                                        last = pe.matmul(summed[g:g + VW, :], v_tile[par][:, x, k - 1, :],
                                                         probs[:, (2 * (k - 1) + x) % SLOTS, half * CH:(half + 1) * CH],
                                                         start=(k == 1), stop=(k == TB), tile_position=(0, g))
                                    last.then_inc(prob_free, 1)
                        pe.wait_ge(heads_ready, i * 2 + (par + 1))
                        pe.wait_ge(written, i * 2 + par)
                        for c in range(4):
                            last = pe.transpose(turned[:, c * P:(c + 1) * P], heads[par][:, c * P:(c + 1) * P], t.identity[:, :])
                        last.then_inc(turned_ready, 1)


def choose(dve, chain, padded, experts, chosen, top, wanted, marked):
    for tile in range(NT):
        last = dve.max(out=top[:, tile, :], in_=padded[:, tile, 0:experts])
    chain.after(last)
    chain.after(dve.tensor_copy(wanted[:, :, 0:chosen], top[:, :, 0:chosen]))
    for tile in range(NT):
        last = dve.match_replace(out=marked[:, tile, :], in_to_replace=wanted[:, tile, :],
                                 in_values=padded[:, tile, :], imm_value=HIGH)
    chain.after(last)
    chain.after(dve.tensor_scalar(marked[:, :, 0:experts], marked[:, :, 0:experts], HIGH, None, ALU.is_equal))


def split_weights(dve, chain, weight, parts, rest):
    chain.after(dve.tensor_copy(parts[:, :, 0, :], weight))
    chain.after(dve.tensor_tensor(rest[0], weight, parts[:, :, 0, :], ALU.subtract))
    chain.after(dve.tensor_copy(parts[:, :, 1, :], rest[0]))
    return dve.tensor_tensor(parts[:, :, 2, :], rest[0], parts[:, :, 1, :], ALU.subtract)


def layer0_mixture(nc, t, d):
    NP0 = E0 * F0 // P
    NU = NP0 + 1
    pad = E0 + 8 - K0
    ctx = ExitStack()
    with ctx:
        def sb(name, shape, dt=F32):
            return ctx.enter_context(nc.sbuf_tensor(name, shape, dt))

        def ps(name, shape, dt=F32):
            return ctx.enter_context(nc.psum_tensor(name, shape, dt))

        def sem(name):
            return ctx.enter_context(nc.semaphore(name))

        normed = sb("m0_normed", [P, NT, D])
        centred = sb("m0_centred", [P, NT, D])
        squares = sb("m0_squares", [P, NT, D])
        inT = sb("m0_inT", [P, T])
        stat = sb("m0_stat", [P, 5, NT])
        gate_w = sb("m0_gate_w", [P, E0])
        route = sb("m0_route", [P, 1])
        w1 = sb("m0_w1", [P, NP0, 2, F0])
        ws1 = sb("m0_ws1", [P, P])
        w2 = sb("m0_w2", [P, NP0, D])
        ws2 = sb("m0_ws2", [P, D])
        b1 = sb("m0_b1", [P, NU])
        b2x3 = sb("m0_b2x3", [3 * E0, D])
        bs2 = sb("m0_bs2", [P, 1])
        spread32 = sb("m0_spread32", [3 * E0, NP0, P])
        spread = sb("m0_spread", [3 * E0, NP0, P], BF16)
        padded = sb("m0_padded", [P, NT, pad])
        marked = sb("m0_marked", [P, NT, pad])
        top, wanted = sb("m0_top", [P, NT, 8]), sb("m0_wanted", [P, NT, 8])
        weight = sb("m0_weight", [P, NT, E0])
        rest = sb("m0_rest", [P, NT, E0])
        total = sb("m0_total", [P, 2, NT])
        parts = sb("m0_parts", [P, NT, 3, E0], BF16)
        weightT = sb("m0_weightT", [3 * E0, T], BF16)
        weightT32 = sb("m0_weightT32", [3 * E0, T])
        hidden = sb("m0_hidden", [P, NU, CH])
        weighed = sb("m0_weighed", [P, NP0, CH])
        outT = sb("m0_outT", [P, CH])
        identity16 = sb("m0_identity16", [P, P], BF16)
        hid_bank = [ps(f"m0_hid{i}", [P, CH]) for i in range(2)]
        wgt_bank = [ps(f"m0_wgt{i}", [P, CH]) for i in range(2)]
        sum_bank, turn_bank = ps("m0_sum", [P, CH]), ps("m0_turn", [P, NT // 4, D])
        gate_bank = ps("m0_gate", [P, NT, E0])
        part_bank = ps("m0_part", [3 * E0, CH], BF16)

        w_in, dve_step, root_asked, root_given = sem("w_in"), sem("dve_step"), sem("root_asked"), sem("root_given")
        low_set, normed_ready, tr_ready, tr_out = sem("low_set"), sem("normed_ready"), sem("tr_ready"), sem("tr_out")
        gate_ready, prob_ready, cast_ready = sem("gate_ready"), sem("prob_ready"), sem("cast_ready")
        parts_ready, partT_ready, partT_out = sem("parts_ready"), sem("partT_ready"), sem("partT_out")
        hid_ready, act_ready, wgt_ready, weighed_ready = sem("hid_ready"), sem("act_ready"), sem("wgt_ready"), sem("weighed_ready")
        sum_ready, out_ready, turn_ready, added = sem("sum_ready"), sem("out_ready"), sem("turn_ready"), sem("added")
        NW = 15

        with nc.Block() as block:
            @block.sync
            def _(sp):
                def load(dst, src):
                    sp.dma_start(dst, src).then_inc(w_in, 16)

                sp.wait_ge(low_set, 5)
                load(gate_w[:, :], d["L0_ffn_gate_W"])
                load(route[:, :], d["L0_ffn_route_scale"].partition_broadcast(P))
                load(w1[:, :, :, :].rearrange("p m e f -> p (m e) f"), d["L0_ffn_W1"].rearrange("e d f -> d e f"))
                load(ws1[:, 0:F0], d["L0_ffn_Ws1"])
                load(w2[:, :, :], d["L0_ffn_W2"].rearrange("(m e) f d -> (e f) m d", e=2))
                load(ws2[0:F0, :], d["L0_ffn_Ws2"])
                load(b1[:, 0:NP0], d["L0_ffn_b1"])
                load(b1[0:F0, NP0:NU], d["L0_ffn_bs1"])
                for i in range(3):
                    load(b2x3[i * E0:(i + 1) * E0, :], d["L0_ffn_b2"])
                load(bs2[:, :], d["L0_ffn_bs2"])
                load(spread32[:, :, :], d["spread0"])
                load(t.mask32[:, :], d["mask"])
                load(t.seen[:, :], d["seen"])

            @block.gpsimd
            def _(pool):
                pool.memset(padded[:, :, E0:pad], LOW).then_inc(low_set, 1)
                pool.memset(wanted[:, :, K0:8], LOW).then_inc(low_set, 1)
                pool.memset(ws1[:, F0:P], 0.0).then_inc(low_set, 1)
                pool.wait_ge(low_set, 3)
                pool.memset(ws2[F0:P, :], 0.0).then_inc(low_set, 1)
                pool.memset(b1[F0:P, NP0:NU], 0.0).then_inc(low_set, 1)
                pool.wait_ge(w_in, 16 * NW)
                pool.tensor_copy(spread[:, :, :], spread32[:, :, :]).then_inc(cast_ready, 1)
                pool.tensor_copy(identity16[:, :], t.identity[:, :]).then_inc(cast_ready, 1)

            @block.vector
            def _(dve):
                chain = Chain(dve, dve_step)
                for b in range(B):
                    half = t.x[:, b * TB:(b + 1) * TB, :].rearrange("p t (h w) -> p h t w", w=HD0)
                    src = t.attn0[:, b * S:(b + 1) * S].rearrange("p (h t w) -> p h t w", h=H0, w=HD0)
                    last = dve.tensor_tensor(half, half, src, ALU.add)
                chain.after(last)
                normalise(dve, chain, normed[:, :, :], t.x[:, :, :], (centred[:, :, :], squares[:, :, :]), stat, 1e-5,
                          root_asked, root_given, 0)
                dve.engine_nop().then_inc(normed_ready, 1)
                for c in range(NCH):
                    dve.wait_ge(tr_ready, c + 1)
                    bank = (hid_bank + wgt_bank)[c]
                    dve.tensor_copy(inT[:, c * CH:(c + 1) * CH], bank[:, :]).then_inc(tr_out, 1)
                dve.wait_ge(w_in, 16 * NW)
                dve.wait_ge(low_set, 2)
                dve.wait_ge(prob_ready, 1)
                chain.after(dve.tensor_scalar(padded[:, :, 0:E0], weight[:, :, :], route[:, 0:1], None, ALU.mult))
                choose(dve, chain, padded, E0, K0, top, wanted, marked)
                chain.after(dve.tensor_tensor(weight[:, :, :], padded[:, :, 0:E0], marked[:, :, 0:E0], ALU.mult))
                chain.after(dve.tensor_tensor(total[:, 0, :], top[:, :, 0], top[:, :, 1], ALU.add))
                chain.after(dve.reciprocal(total[:, 1, :], total[:, 0, :]))
                chain.after(dve.tensor_tensor(weight[:, :, :], weight[:, :, :],
                                              total[:, 1, :].unsqueeze(2).broadcast_to([P, NT, E0]), ALU.mult))
                split_weights(dve, chain, weight[:, :, :], parts, [rest[:, :, :]]).then_inc(parts_ready, 1)
                for c in range(NCH):
                    cols = slice(c * CH, (c + 1) * CH)
                    dve.wait_ge(partT_ready, c + 1)
                    chain.after(dve.tensor_copy(weightT[:, cols], part_bank[:, :]))
                    dve.tensor_copy(weightT32[:, cols], weightT[:, cols]).then_inc(partT_out, 1)
                with dve.Fori(0, NCH) as c:
                    for m in range(NP0):
                        dve.wait_ge(act_ready, c * NU + (m + 1))
                        dve.wait_ge(wgt_ready, c * NP0 + (m + 1))
                        dve.wait_ge(sum_ready, c)
                        dve.tensor_tensor(weighed[:, m, :], hidden[:, m, :], wgt_bank[m % 2][:, :], ALU.mult).then_inc(weighed_ready, 1)
                    dve.wait_ge(turn_ready, c + 1)
                    xs = t.x[:, :, :].rearrange("p t d -> p (t d)")[:, bass.ds(c * CH, CH)]
                    dve.tensor_tensor(xs, turn_bank[:, :, :].rearrange("p t d -> p (t d)"), xs, ALU.add).then_inc(added, 1)

            @block.scalar
            def _(act):
                take_root(act, stat, root_asked, root_given, 0)
                act.wait_ge(gate_ready, 1)
                act.activation(weight[:, :, :], gate_bank[:, :, :], ACT.Sigmoid).then_inc(prob_ready, 1)
                act.wait_ge(w_in, 16 * NW)
                with act.Fori(0, NCH) as c:
                    for m in range(NU):
                        act.wait_ge(hid_ready, c * NU + (m + 1))
                        if m < NP0:
                            act.wait_ge(weighed_ready, c * NP0)
                        else:
                            act.wait_ge(sum_ready, c)
                        act.activation(hidden[:, m, :], hid_bank[m % 2][:, :], ACT.Gelu, bias=b1[:, m:m + 1]).then_inc(act_ready, 1)
                    act.wait_ge(sum_ready, c + 1)
                    act.wait_ge(turn_ready, c)
                    act.activation(outT[:, :], sum_bank[:, :], ACT.Identity, bias=bs2[:, 0:1]).then_inc(out_ready, 1)

            @block.tensor
            def _(pe):
                pe.wait_ge(normed_ready, 1)
                for c in range(NCH):
                    transpose_tiles(pe, (hid_bank + wgt_bank)[c], normed, t.identity[:, :], c).then_inc(tr_ready, 1)
                pe.wait_ge(w_in, 16 * NW)
                pe.wait_ge(tr_out, NCH)
                for tile in range(NT):
                    last = pe.matmul(gate_bank[:, tile, :], inT[:, tile * P:(tile + 1) * P], gate_w[:, :], start=True, stop=True)
                last.then_inc(gate_ready, 1)
                pe.wait_ge(cast_ready, 2)
                pe.wait_ge(parts_ready, 1)
                for c in range(NCH):
                    if c:
                        pe.wait_ge(partT_out, c)
                    for k in range(4):
                        last = pe.transpose(part_bank[:, k * P:(k + 1) * P],
                                            parts[:, 4 * c + k, :, :].rearrange("p a e -> p (a e)"), identity16[:, :])
                    last.then_inc(partT_ready, 1)
                pe.wait_ge(partT_out, NCH)
                with pe.Fori(0, NCH) as c:
                    cols = bass.ds(c * CH, CH)

                    def up(m):
                        if m < NP0:
                            pe.wait_ge(weighed_ready, c * NP0 + max(m - 1, 0))
                        pe.wait_ge(act_ready, c * NU + max(m - 1, 0))
                        w = w1[:, m, :, :].rearrange("p e f -> p (e f)") if m < NP0 else ws1[:, :]
                        pe.matmul(hid_bank[m % 2][:, :], w, inT[:, cols], start=True, stop=True).then_inc(hid_ready, 1)
                        if m < NP0:
                            pe.matmul(wgt_bank[m % 2][:, :], spread[:, m, :], weightT[:, cols], start=True, stop=True).then_inc(wgt_ready, 1)

                    pe.wait_ge(out_ready, c)
                    up(0)
                    up(1)
                    pe.matmul(sum_bank[:, :], b2x3[:, :], weightT32[:, cols], start=True, stop=False)
                    for m in range(NU):
                        if m + 2 < NU:
                            up(m + 2)
                        if m < NP0:
                            pe.wait_ge(weighed_ready, c * NP0 + (m + 1))
                            pe.matmul(sum_bank[:, :], w2[:, m, :], weighed[:, m, :], start=False, stop=False)
                        else:
                            pe.wait_ge(act_ready, c * NU + NU)
                            pe.matmul(sum_bank[:, :], ws2[:, :], hidden[:, m, :], start=False, stop=True).then_inc(sum_ready, 1)
                    pe.wait_ge(out_ready, c + 1)
                    pe.wait_ge(added, c)
                    for k in range(4):
                        last = pe.transpose(turn_bank[:, k, :], outT[:, k * P:(k + 1) * P], t.identity[:, :])
                    last.then_inc(turn_ready, 1)


NBLK = S // CH
UNITS = [(b, q) for b in range(B) for q in range(GQ)]
TILES = [(b, q, blk, j) for b, q in UNITS for blk in range(NBLK) for j in range(4 * blk + 4)]
NTILE = len(TILES)
UTILE = NTILE // len(UNITS)
BLOCKS = [(b, q, blk) for b, q in UNITS for blk in range(NBLK)]
BLOCK_OF = [BLOCKS.index((b, q, blk)) for b, q, blk, j in TILES]
LAST_OF = [max(n for n in range(NTILE) if BLOCK_OF[n] == k) for k in range(len(BLOCKS))]
DIAGONAL = [j >= 4 * blk for _, _, blk, j in TILES]
SKIPPED = [max(0, j - 4 * blk) * P for _, _, blk, j in TILES]
NDIAG = sum(DIAGONAL)
AHEAD = 2


def attention_order(exact):
    runs = [range(u * UTILE, (u + 1) * UTILE) for u in range(len(UNITS))] if exact else [range(NTILE)]
    for unit, run in enumerate(runs):
        if exact:
            yield "maxima", unit
        for i in range(len(run) + AHEAD):
            if i < len(run):
                yield "score", run[i]
            if i >= AHEAD:
                n = run[i - AHEAD]
                yield "use", n
                if n != run[0] and BLOCK_OF[n - 1] != BLOCK_OF[n]:
                    yield "close", BLOCK_OF[n - 1]
        yield "close", BLOCK_OF[run[-1]]


def layer1_attention(nc, t, d, exact):
    NB, NU = len(BLOCKS), len(UNITS)
    PSLOT, SSLOT = 8, 4
    NR, NV = 2 * (1 + GQ) * B, 2 * B
    ctx = ExitStack()
    with ctx:
        def sb(name, shape, dt=F32):
            return ctx.enter_context(nc.sbuf_tensor(name, shape, dt))

        def ps(name, shape):
            return ctx.enter_context(nc.psum_tensor(name, shape, F32))

        def sem(name):
            return ctx.enter_context(nc.semaphore(name))

        normed = sb("a1_normed", [P, NT, D])
        centred = sb("a1_centred", [P, NT, D])
        squares = sb("a1_squares", [P, NT, D])
        stat = sb("a1_stat", [P, 5, NT])
        inT = sb("a1_inT", [P, T])
        w_q, w_k, w_v = sb("a1_wq", [P, GQ, D1]), sb("a1_wk", [P, D1]), sb("a1_wv", [P, D1])
        w_o = sb("a1_wo", [P, GQ, D])
        kT = sb("a1_kT", [P, B, S])
        qT = sb("a1_qT", [P, B, GQ, S])
        v = sb("a1_v", [P, B, TB, D1])
        straight, crossed = sb("a1_straight", [P, 2, CH]), sb("a1_crossed", [P, 2, CH])
        probs = sb("a1_probs", [P, PSLOT, CH])
        weight = sb("a1_weight", [P, 2, CH])
        headsT = sb("a1_headsT", [P, 2, CH])
        inverse = sb("a1_inverse", [P, 2, 4])
        part = sb("a1_part", [P, 2, 4, D])
        ones = sb("a1_ones", [P, 1])
        maxima = sb("a1_maxima", [P, TB])
        shift = sb("a1_shift", [TB, 2, P], BF16)
        shift_row = sb("a1_shift_row", [2, S], BF16)
        ones2 = sb("a1_ones2", [2, P], BF16)
        mask16, identity16 = sb("a1_mask16", [P, P], BF16), sb("a1_identity16", [P, P], BF16)
        proj_bank = [ps(f"a1_proj{i}", [P, CH]) for i in range(2)]
        out_bank, weight_bank = proj_bank
        scores = ps("a1_scores", [P, SSLOT * CH])
        sum_bank = [ps(f"a1_sum{i}", [P, CH]) for i in range(2)]

        dve_step, root_asked, root_given = sem("dve_step"), sem("root_asked"), sem("root_given")
        normed_ready, tr_ready, tr_out = sem("normed_ready"), sem("tr_ready"), sem("tr_out")
        w_in, wo_in, w_used, wo_used, ones_set = sem("w_in"), sem("wo_in"), sem("w_used"), sem("wo_used"), sem("ones_set")
        rot_ready, rot_taken, rotated = sem("rot_ready"), sem("rot_taken"), sem("rotated")
        v_ready, v_taken = sem("v_ready"), sem("v_taken")
        score_ready, prob_ready, masked = sem("score_ready"), sem("prob_ready"), sem("masked")
        used, weighed = sem("used"), sem("weighed")
        heads_ready, weight_ready, out_ready, out_taken, added = (sem("heads_ready"), sem("weight_ready"), sem("out_ready"),
                                                                  sem("out_taken"), sem("added"))
        plain_ready, max_ready, maxT_ready, shift_ready, shift_in, inverse_ready = (
            sem("plain_ready"), sem("max_ready"), sem("maxT_ready"), sem("shift_ready"), sem("shift_in"), sem("inverse_ready"))

        def slot(n):
            return scores[:, (n % SSLOT) * CH + SKIPPED[n]:(n % SSLOT + 1) * CH]

        def prob(n):
            return probs[:, n % PSLOT, SKIPPED[n]:CH]

        def wait_probs(engine, g, n):
            if DIAGONAL[n] and not exact:
                engine.wait_ge(masked, g * NDIAG + sum(DIAGONAL[:n + 1]))
            else:
                engine.wait_ge(prob_ready, g * NTILE + (n + 1))

        with nc.Block() as block:
            @block.sync
            def _(sp):
                with sp.Fori(0, KV1) as g:
                    sp.wait_ge(w_used, g)
                    sp.dma_start(w_q[:, :, :].rearrange("p q d -> p (q d)"), d["L1_attn_Wq"][:, bass.ds(g * (GQ * D1), GQ * D1)]).then_inc(w_in, 16)
                    sp.dma_start(w_k[:, :], d["L1_attn_Wk"][:, bass.ds(g * D1, D1)]).then_inc(w_in, 16)
                    sp.dma_start(w_v[:, :], d["L1_attn_Wv"][:, bass.ds(g * D1, D1)]).then_inc(w_in, 16)
                    sp.wait_ge(wo_used, g)
                    for q in range(GQ):
                        sp.dma_start(w_o[:, q, :], d["L1_attn_Wo"][bass.ds(g * (GQ * D1) + q * D1, D1), :]).then_inc(wo_in, 16)

            @block.gpsimd
            def _(pool):
                pool.memset(ones[:, :], 1.0).then_inc(ones_set, 1)
                pool.memset(ones2[:, :], 1.0).then_inc(ones_set, 1)
                pool.tensor_copy(mask16[:, :], t.mask32[:, :]).then_inc(ones_set, 1)
                pool.tensor_copy(identity16[:, :], t.identity[:, :]).then_inc(ones_set, 1)
                with pool.Fori(0, KV1) as g:
                    for r in range(NR):
                        b, i = divmod(r, NR // B)
                        dst = (kT[:, b, :] if i < 2 else qT[:, b, (i - 2) // 2, :])[:, (i % 2) * CH:(i % 2 + 1) * CH]
                        pool.wait_ge(rot_taken, g * NR + (r + 1))
                        pool.tensor_tensor(dst, straight[:, r % 2, :], crossed[:, r % 2, :], ALU.add).then_inc(rotated, 1)
                    for what, n in attention_order(exact):
                        if what == "score" and DIAGONAL[n] and not exact:
                            pool.wait_ge(prob_ready, g * NTILE + (n + 1))
                            edge = probs[:, n % PSLOT, SKIPPED[n]:SKIPPED[n] + P]
                            pool.tensor_tensor(edge, edge, t.seen[:, :], ALU.mult).then_inc(masked, 1)
                        if what == "close":
                            b, q, blk = BLOCKS[n]
                            xs = t.x[:, b * TB + blk * 4:b * TB + blk * 4 + 4, :]
                            pool.wait_ge(out_taken, g * NB + (n + 1))
                            pool.wait_ge(added, g * NB + n)
                            pool.tensor_tensor(xs, xs, part[:, n % 2, :, :], ALU.add).then_inc(added, 1)

            @block.vector
            def _(dve):
                chain = Chain(dve, dve_step)
                normalise(dve, chain, normed[:, :, :], t.x[:, :, :], (centred[:, :, :], squares[:, :, :]), stat, 1e-5,
                          root_asked, root_given, 0)
                dve.engine_nop().then_inc(normed_ready, 1)
                for c in range(NCH):
                    dve.wait_ge(tr_ready, c + 1)
                    dve.tensor_copy(inT[:, c * CH:(c + 1) * CH], scores[:, c * CH:(c + 1) * CH]).then_inc(tr_out, 1)
                with dve.Fori(0, KV1) as g:
                    for r in range(NR):
                        b, i = divmod(r, NR // B)
                        u = b * (NR + NV) // B + i
                        bank, table = proj_bank[u % 2], 2 if i < 2 else 0
                        cols = slice((i % 2) * CH, (i % 2 + 1) * CH)
                        dve.wait_ge(rot_ready, g * NR + (r + 1))
                        dve.wait_ge(rotated, g * NR + max(r - 1, 0))
                        dve.tensor_tensor(straight[:, r % 2, :], bank[:, :], t.rope[:, table, cols], ALU.mult)
                        for half in range(2):
                            to, of = slice(half * 64, half * 64 + 64), slice(64 - half * 64, 128 - half * 64)
                            last = dve.tensor_tensor(crossed[to, r % 2, :], bank[of, :], t.rope[to, table + 1, cols], ALU.mult)
                        last.then_inc(rot_taken, 1)
                    for what, n in attention_order(exact):
                        if what == "maxima":
                            for qt in range(TB):
                                dve.wait_ge(plain_ready, g * (NU * TB) + (n * TB + qt + 1))
                                dve.reduce_max(maxima[:, qt:qt + 1], scores[:, (qt % 2) * 2 * CH:(qt % 2) * 2 * CH + (qt + 1) * P],
                                               AX_X).then_inc(max_ready, 1)
                            dve.wait_ge(maxT_ready, g * NU + (n + 1))
                            mT = weight_bank[0:TB, P:2 * P]
                            dve.tensor_scalar(shift[:, 0, :], mT, -1.0, None, ALU.mult).then_inc(inverse_ready, 1)
                            dve.wait_ge(inverse_ready, g * (NU + NB) + (n + 2 * n + 1))
                            dve.scalar_tensor_tensor(out=shift[:, 1, :], in0=mT, scalar=-1.0, in1=shift[:, 0, :],
                                                     op0=ALU.mult, op1=ALU.subtract).then_inc(shift_ready, 1)
                        if what == "use":
                            k = BLOCK_OF[n]
                            wait_probs(dve, g, n)
                            dst = weight[:, k % 2, SKIPPED[n]:CH]
                            if TILES[n][3] == 0:
                                dve.wait_ge(weight_ready, g * NB + max(k - 1, 0))
                                dve.tensor_copy(dst, prob(n)).then_inc(weighed, 1)
                            else:
                                dve.wait_ge(weighed, g * NTILE + n)
                                dve.tensor_tensor(dst, dst, prob(n), ALU.add).then_inc(weighed, 1)
                        if what == "close":
                            dve.wait_ge(weight_ready, g * NB + (n + 1))
                            dve.reciprocal(inverse[:, n % 2, :], weight_bank[:, 0:4]).then_inc(inverse_ready, 1)
                            if exact:
                                dve.wait_ge(inverse_ready, g * (NU + NB) + (n + n // 2 + 2))
                            else:
                                dve.wait_ge(inverse_ready, g * NB + (n + 1))
                            dve.wait_ge(out_ready, g * NB + (n + 1))
                            dve.wait_ge(added, g * NB + max(n - 1, 0))
                            dve.tensor_tensor(part[:, n % 2, :, :], out_bank[:, :].rearrange("p (t d) -> p t d", d=D),
                                              inverse[:, n % 2, :].unsqueeze(2).broadcast_to([P, 4, D]), ALU.mult).then_inc(out_taken, 1)

            @block.scalar
            def _(act):
                take_root(act, stat, root_asked, root_given, 0)
                with act.Fori(0, KV1) as g:
                    for i in range(NV):
                        u = i // 2 * (NR + NV) // B + NR // B + i % 2
                        act.wait_ge(v_ready, g * NV + (i + 1))
                        act.activation(v[:, i // 2, (i % 2) * 4:(i % 2) * 4 + 4, :].rearrange("p t d -> p (t d)"),
                                       proj_bank[u % 2][:, :], ACT.Copy).then_inc(v_taken, 1)
                    for what, n in attention_order(exact):
                        if what == "maxima":
                            act.wait_ge(shift_ready, g * NU + (n + 1))
                            for i in range(2):
                                act.dma_start(shift_row[i:i + 1, :], shift[:, i, :]).then_inc(shift_in, 16)
                        if what == "score":
                            act.wait_ge(score_ready, g * NTILE + (n + 1))
                            act.wait_ge(used, g * NTILE + max(n - PSLOT + 1, 0))
                            act.wait_ge(weighed, g * NTILE + max(n - PSLOT + 1, 0))
                            act.activation(prob(n), slot(n), ACT.Exp).then_inc(prob_ready, 1)
                        if what == "close":
                            act.wait_ge(used, g * NTILE + (LAST_OF[n] + 1))
                            act.wait_ge(out_ready, g * NB + max(n - 1, 0))
                            act.activation(headsT[:, n % 2, :], sum_bank[n % 2][:, :], ACT.Copy).then_inc(heads_ready, 1)

            @block.tensor
            def _(pe):
                pe.wait_ge(normed_ready, 1)
                for c in range(NCH):
                    transpose_tiles(pe, scores[:, c * CH:(c + 1) * CH], normed, t.identity[:, :], c).then_inc(tr_ready, 1)
                pe.wait_ge(tr_out, NCH)
                pe.wait_ge(ones_set, 4)
                with pe.Fori(0, KV1) as g:
                    pe.wait_ge(w_in, (g + 1) * 48)
                    pe.wait_ge(out_taken, g * NB)
                    for b in range(B):
                        for i in range(2 * (1 + GQ)):
                            r = b * (NR // B) + i
                            u = b * (NR + NV) // B + i
                            if i >= 2:
                                pe.wait_ge(rot_taken, g * NR + (r - 1))
                            elif b:
                                pe.wait_ge(v_taken, g * NV + (i + 1))
                            w = w_k[:, :] if i < 2 else w_q[:, (i - 2) // 2, :]
                            pe.matmul(proj_bank[u % 2][:, :], w, inT[:, b * S + (i % 2) * CH:b * S + (i % 2 + 1) * CH],
                                      start=True, stop=True).then_inc(rot_ready, 1)
                        for i in range(2):
                            u = b * (NR + NV) // B + NR // B + i
                            pe.wait_ge(rot_taken, g * NR + ((b + 1) * (NR // B) - 1 + i))
                            for k in range(4):
                                first = b * S + (4 * i + k) * P
                                last = pe.matmul(proj_bank[u % 2][:, k * P:(k + 1) * P], inT[:, first:first + P], w_v[:, :],
                                                 start=True, stop=True)
                            last.then_inc(v_ready, 1)
                    pe.wait_ge(v_taken, (g + 1) * NV)
                    pe.nop().then_inc(w_used, 1)
                    pe.wait_ge(rotated, (g + 1) * NR)
                    pe.wait_ge(wo_in, (g + 1) * 32)
                    for what, n in attention_order(exact):
                        if what == "maxima":
                            b, q = UNITS[n]
                            pe.wait_ge(prob_ready, g * NTILE + n * UTILE)
                            for qt in range(TB):
                                if qt >= 2:
                                    pe.wait_ge(max_ready, g * (NU * TB) + (n * TB + qt - 1))
                                base, width = (qt % 2) * 2 * CH, (qt + 1) * P
                                for first in range(0, width, CH):
                                    cols = min(CH, width - first)
                                    pe.matmul(scores[:, base + first:base + first + cols], qT[:, b, q, qt * P:(qt + 1) * P],
                                              kT[:, b, first:first + cols], start=True, stop=first + cols < width)
                                pe.matmul(scores[:, base + width - P:base + width], identity16[:, :], mask16[:, :],
                                          start=False, stop=True).then_inc(plain_ready, 1)
                            pe.wait_ge(max_ready, g * (NU * TB) + (n + 1) * TB)
                            pe.wait_ge(out_taken, g * NB + 2 * n)
                            pe.transpose(weight_bank[0:TB, P:2 * P], maxima[:, :], t.identity[:, :]).then_inc(maxT_ready, 1)
                            pe.wait_ge(shift_in, g * (NU * 32) + (n + 1) * 32)
                        if what == "score":
                            b, q, blk, j = TILES[n]
                            pe.wait_ge(prob_ready, g * NTILE + max(n - SSLOT + 1, 0))
                            queries = slice(blk * CH + SKIPPED[n], (blk + 1) * CH)
                            last = pe.matmul(slot(n), kT[:, b, j * P:(j + 1) * P], qT[:, b, q, queries], start=True, stop=not exact)
                            if exact:
                                last = pe.matmul(slot(n), ones2[:, :], shift_row[:, queries], start=False, stop=not DIAGONAL[n])
                                if DIAGONAL[n]:
                                    last = pe.matmul(slot(n)[:, 0:P], mask16[:, :], identity16[:, :], start=False, stop=True)
                            last.then_inc(score_ready, 1)
                        if what == "use":
                            b, q, blk, j = TILES[n]
                            k = BLOCK_OF[n]
                            wait_probs(pe, g, n)
                            if j == 0:
                                pe.wait_ge(heads_ready, g * NB + max(k - 1, 0))
                            pe.matmul(sum_bank[k % 2][:, SKIPPED[n]:CH], v[:, b, j, :], prob(n), start=(j == 0),
                                      stop=(n == LAST_OF[k])).then_inc(used, 1)
                        if what == "close":
                            pe.wait_ge(weighed, g * NTILE + (LAST_OF[n] + 1))
                            pe.wait_ge(out_taken, g * NB + n)
                            for c in range(4):
                                last = pe.matmul(weight_bank[:, c:c + 1], weight[:, n % 2, c * P:(c + 1) * P], ones[:, :], start=True, stop=True)
                            last.then_inc(weight_ready, 1)
                            pe.wait_ge(heads_ready, g * NB + (n + 1))
                            for c in range(4):
                                last = pe.matmul(out_bank[:, c * P:(c + 1) * P], headsT[:, n % 2, c * P:(c + 1) * P],
                                                 w_o[:, BLOCKS[n][1], :], start=True, stop=True)
                            last.then_inc(out_ready, 1)
                    pe.wait_ge(out_taken, (g + 1) * NB)
                    pe.nop().then_inc(wo_used, 1)


def layer1_mixture(nc, t, d, out):
    pad = E1 + 8 - K1
    SIDE = LIMIT + 1.0
    ctx = ExitStack()
    with ctx:
        def sb(name, shape, dt=F32):
            return ctx.enter_context(nc.sbuf_tensor(name, shape, dt))

        def ps(name, shape, dt=F32):
            return ctx.enter_context(nc.psum_tensor(name, shape, dt))

        def sem(name):
            return ctx.enter_context(nc.semaphore(name))

        normed = sb("m1_normed", [P, NT, D])
        centred = sb("m1_centred", [P, NT, D])
        squares = sb("m1_squares", [P, NT, D])
        inT = sb("m1_inT", [P, T])
        stat = sb("m1_stat", [P, 5, NT])
        scale = sb("m1_scale", [P, D])
        gate_w, gate_b = sb("m1_gate_w", [P, E1]), sb("m1_gate_b", [P, E1])
        w1 = [sb(f"m1_w1_{i}", [P, F1]) for i in range(2)]
        w2 = [sb(f"m1_w2_{i}", [P, D]) for i in range(2)]
        b1 = sb("m1_b1", [P, E1])
        b2x3 = sb("m1_b2x3", [3 * E1, D])
        spread32 = sb("m1_spread32", [3 * E1, E1 * P])
        spread = [sb(f"m1_spread{i}", [3 * E1, P], BF16) for i in range(2)]
        padded = sb("m1_padded", [P, NT, pad])
        marked = sb("m1_marked", [P, NT, pad])
        top, wanted = sb("m1_top", [P, NT, 8]), sb("m1_wanted", [P, NT, 8])
        weight = sb("m1_weight", [P, NT, E1])
        rest = sb("m1_rest", [P, NT, E1])
        total = sb("m1_total", [P, 2, NT])
        parts = sb("m1_parts", [P, NT, 3, E1], BF16)
        weightT = sb("m1_weightT", [3 * E1, T], BF16)
        weightT32 = sb("m1_weightT32", [3 * E1, T])
        identity16 = sb("m1_identity16", [P, P], BF16)
        linear, sigm = sb("m1_linear", [P, 4, CH]), sb("m1_sigm", [P, 4, CH])
        gated, weighed = sb("m1_gated", [P, 4, CH]), sb("m1_weighed", [P, 4, CH])
        outT = sb("m1_outT", [P, T])
        hid_bank = [ps(f"m1_hid{i}", [P, CH]) for i in range(2)]
        wgt_bank = [ps(f"m1_wgt{i}", [P, CH]) for i in range(2)]
        sum_bank = [ps(f"m1_sum{i}", [P, CH]) for i in range(NCH)]
        gate_bank = hid_bank[0][:, 0:NT * E1].rearrange("p (t e) -> p t e", e=E1)

        w_in, dve_step, root_asked, root_given = sem("w_in"), sem("dve_step"), sem("root_asked"), sem("root_given")
        low_set, normed_ready, tr_ready, tr_out = sem("low_set"), sem("normed_ready"), sem("tr_ready"), sem("tr_out")
        gate_ready, exp_asked, exp_given, cast_ready = sem("gate_ready"), sem("exp_asked"), sem("exp_given"), sem("cast_ready")
        parts_ready, partT_ready, partT_out = sem("parts_ready"), sem("partT_ready"), sem("partT_out")
        expert_in = [sem(f"expert_in{i}") for i in range(2)]
        spread_ready = sem("spread_ready")
        hid_ready, linear_ready, sigm_ready, gated_ready = sem("hid_ready"), sem("linear_ready"), sem("sigm_ready"), sem("gated_ready")
        wgt_ready, weighed_ready, summed = sem("wgt_ready"), sem("weighed_ready"), sem("summed")
        sum_out, turn_ready, added, stored = sem("sum_out"), sem("turn_ready"), sem("added"), sem("stored")
        NW = 8
        N = 2 * NCH

        with nc.Block() as block:
            @block.sync
            def _(sp):
                def load(dst, src):
                    sp.dma_start(dst, src).then_inc(w_in, 16)

                def load_expert(e, par):
                    sp.dma_start(w1[par][:, :], d["L1_ffn_mlp1_w"][bass.ds(e * P, P), :]).then_inc(expert_in[par], 16)
                    sp.dma_start(w2[par][:, :], d["L1_ffn_mlp2_w"][bass.ds(e * P, P), :]).then_inc(expert_in[par], 16)

                load(scale[:, :], d["L1_ffn_scale"].partition_broadcast(P))
                load(gate_w[:, :], d["L1_ffn_gate_w"])
                load(gate_b[:, :], d["L1_ffn_gate_b"].partition_broadcast(P))
                load(b1[:, :], d["L1_ffn_mlp1_b"])
                for i in range(3):
                    load(b2x3[i * E1:(i + 1) * E1, :], d["L1_ffn_mlp2_b"])
                load(spread32[:, :], d["spread1"])
                for par in range(2):
                    load_expert(par, par)
                with sp.Fori(0, E1 // 2 - 1) as i:
                    for par in range(2):
                        sp.wait_ge(summed, i * N + (par + 1) * NCH)
                        load_expert(i * 2 + (par + 2), par)
                for c in range(NCH):
                    sp.wait_ge(added, c + 1)
                    b, first = c // (NCH // B), c % (NCH // B) * CH
                    sp.dma_start(out[b, first:first + CH, :].rearrange("(t p) d -> p t d", p=P), t.x[:, 4 * c:4 * c + 4, :]).then_inc(stored, 16)
                sp.wait_ge(stored, 16 * NCH)

            @block.gpsimd
            def _(pool):
                pool.memset(padded[:, :, E1:pad], LOW).then_inc(low_set, 1)
                pool.memset(wanted[:, :, K1:8], LOW).then_inc(low_set, 1)
                pool.tensor_copy(identity16[:, :], t.identity[:, :]).then_inc(cast_ready, 1)
                with pool.Fori(0, E1 // 2) as i:
                    for n in range(N):
                        pool.wait_ge(sigm_ready, i * N + (n + 1))
                        pool.wait_ge(weighed_ready, i * N + max(n - 3, 0))
                        pool.tensor_tensor(gated[:, n % 4, :], linear[:, n % 4, :], sigm[:, n % 4, :], ALU.mult).then_inc(gated_ready, 1)

            @block.vector
            def _(dve):
                chain = Chain(dve, dve_step)
                normalise(dve, chain, normed[:, :, :], t.x[:, :, :], (centred[:, :, :], squares[:, :, :]), stat, 1e-5,
                          root_asked, root_given, 0)
                chain.after(dve.tensor_tensor(t.x[:, :, :], t.x[:, :, :], normed[:, :, :], ALU.add))
                chain.after(dve.tensor_tensor(squares[:, :, :], normed[:, :, :], normed[:, :, :], ALU.mult))
                chain.after(dve.reduce_sum(stat[:, 1, :], squares[:, :, :], AX_X))
                dve.tensor_scalar(stat[:, 2, :], stat[:, 1, :], 1.0 / D, 1e-5, ALU.mult, ALU.add).then_inc(root_asked, 1)
                dve.wait_ge(root_given, 2)
                chain.after(dve.reciprocal(stat[:, 4, :], stat[:, 3, :]))
                chain.after(dve.tensor_tensor(centred[:, :, :], normed[:, :, :], over_features(stat[:, 4, :]), ALU.mult))
                dve.wait_ge(w_in, 16 * NW)
                dve.tensor_tensor(normed[:, :, :], centred[:, :, :], scale[:, :].unsqueeze(1).broadcast_to([P, NT, D]),
                                  ALU.mult).then_inc(normed_ready, 1)
                for c in range(NCH):
                    dve.wait_ge(tr_ready, c + 1)
                    dve.tensor_copy(inT[:, c * CH:(c + 1) * CH], sum_bank[c][:, :]).then_inc(tr_out, 1)
                dve.wait_ge(low_set, 2)
                dve.wait_ge(gate_ready, 1)
                chain.after(dve.tensor_tensor(padded[:, :, 0:E1], gate_bank, gate_b[:, :].unsqueeze(1).broadcast_to([P, NT, E1]), ALU.add))
                choose(dve, chain, padded, E1, K1, top, wanted, marked)
                dve.tensor_tensor(weight[:, :, :], padded[:, :, 0:E1], top[:, :, 0].unsqueeze(2).broadcast_to([P, NT, E1]),
                                  ALU.subtract).then_inc(exp_asked, 1)
                dve.wait_ge(exp_given, 1)
                chain.after(dve.tensor_tensor(weight[:, :, :], rest[:, :, :], marked[:, :, 0:E1], ALU.mult))
                chain.after(dve.reduce_sum(total[:, 0, :], weight[:, :, :], AX_X))
                chain.after(dve.reciprocal(total[:, 1, :], total[:, 0, :]))
                chain.after(dve.tensor_tensor(weight[:, :, :], weight[:, :, :],
                                              total[:, 1, :].unsqueeze(2).broadcast_to([P, NT, E1]), ALU.mult))
                split_weights(dve, chain, weight[:, :, :], parts, [rest[:, :, :]]).then_inc(parts_ready, 1)
                for c in range(NCH):
                    cols = slice(c * CH, (c + 1) * CH)
                    dve.wait_ge(partT_ready, c + 1)
                    chain.after(dve.tensor_copy(weightT[:, cols], wgt_bank[c % 2][0:3 * E1, 0:CH // 2].bitcast(BF16)))
                    dve.tensor_copy(weightT32[:, cols], weightT[:, cols]).then_inc(partT_out, 1)
                with dve.Fori(0, E1 // 2) as i:
                    dve.wait_ge(wgt_ready, i * N)
                    for par in range(2):
                        dve.tensor_scalar(spread[par][:, :], spread32[:, bass.ds(i * (2 * P) + par * P, P)], 1.0, None,
                                          ALU.mult).then_inc(spread_ready, 1)
                    for n in range(N + 1):
                        if n < N:
                            dve.wait_ge(hid_ready, i * N + (n + 1))
                            dve.wait_ge(gated_ready, i * N + max(n - 3, 0))
                            dve.tensor_scalar(linear[:, n % 4, :], hid_bank[n % 2][:, :], b1[:, bass.ds(i * 2 + n // NCH, 1)], LIMIT,
                                              ALU.add, ALU.min).then_inc(linear_ready, 1)
                        if n:
                            m = n - 1
                            dve.wait_ge(gated_ready, i * N + (m + 1))
                            dve.wait_ge(wgt_ready, i * N + (m + 1))
                            dve.wait_ge(summed, i * N + max(m - 3, 0))
                            dve.scalar_tensor_tensor(out=weighed[:, m % 4, :], in0=gated[:, m % 4, :], scalar=SIDE, in1=wgt_bank[m % 2][:, :],
                                                     op0=ALU.mult, op1=ALU.mult).then_inc(weighed_ready, 1)
                for c in range(NCH):
                    dve.wait_ge(summed, E1 * NCH - NCH + c + 1)
                    dve.tensor_copy(outT[:, c * CH:(c + 1) * CH], sum_bank[c][:, :]).then_inc(sum_out, 1)
                for c in range(NCH):
                    dve.wait_ge(turn_ready, c + 1)
                    xs = t.x[:, 4 * c:4 * c + 4, :]
                    dve.tensor_tensor(xs, (hid_bank + wgt_bank)[c][:, :].rearrange("p (t d) -> p t d", d=D), xs, ALU.add).then_inc(added, 1)

            @block.scalar
            def _(act):
                take_root(act, stat, root_asked, root_given, 0)
                take_root(act, stat, root_asked, root_given, 1)
                act.wait_ge(exp_asked, 1)
                act.activation(rest[:, :, :], weight[:, :, :], ACT.Exp).then_inc(exp_given, 1)
                with act.Fori(0, E1 // 2) as i:
                    for n in range(N):
                        act.wait_ge(linear_ready, i * N + (n + 1))
                        act.wait_ge(gated_ready, i * N + max(n - 3, 0))
                        act.activation(sigm[:, n % 4, :], linear[:, n % 4, :], ACT.Sigmoid, scale=ALPHA).then_inc(sigm_ready, 1)

            @block.tensor
            def _(pe):
                pe.wait_ge(normed_ready, 1)
                for c in range(NCH):
                    transpose_tiles(pe, sum_bank[c], normed, t.identity[:, :], c).then_inc(tr_ready, 1)
                pe.wait_ge(w_in, 16 * NW)
                pe.wait_ge(tr_out, NCH)
                for tile in range(NT):
                    last = pe.matmul(gate_bank[:, tile, :], inT[:, tile * P:(tile + 1) * P], gate_w[:, :], start=True, stop=True)
                last.then_inc(gate_ready, 1)
                pe.wait_ge(cast_ready, 1)
                pe.wait_ge(parts_ready, 1)
                for c in range(NCH):
                    if c >= 2:
                        pe.wait_ge(partT_out, c - 1)
                    half = wgt_bank[c % 2][0:3 * E1, 0:CH // 2].bitcast(BF16)
                    for k in range(4):
                        last = pe.transpose(half[:, k * P:(k + 1) * P], parts[:, 4 * c + k, :, :].rearrange("p a e -> p (a e)"), identity16[:, :])
                    last.then_inc(partT_ready, 1)
                pe.wait_ge(partT_out, NCH)
                for c in range(NCH):
                    pe.matmul(sum_bank[c][:, :], b2x3[:, :], weightT32[:, c * CH:(c + 1) * CH], start=True, stop=True)
                with pe.Fori(0, E1 // 2) as i:
                    def up(n):
                        par, c = divmod(n, NCH)
                        cols = slice(c * CH, (c + 1) * CH)
                        if c == 0:
                            pe.wait_ge(expert_in[par], (i + 1) * 32)
                            pe.wait_ge(spread_ready, i * 2 + 2)
                        pe.wait_ge(linear_ready, i * N + max(n - 1, 0))
                        pe.matmul(hid_bank[n % 2][:, :], w1[par][:, :], inT[:, cols], start=True, stop=True).then_inc(hid_ready, 1)
                        pe.wait_ge(weighed_ready, i * N + max(n - 1, 0))
                        pe.matmul(wgt_bank[n % 2][:, :], spread[par][:, :], weightT[:, cols], start=True, stop=True).then_inc(wgt_ready, 1)

                    up(0)
                    up(1)
                    for n in range(N):
                        if n + 2 < N:
                            up(n + 2)
                        par, c = divmod(n, NCH)
                        pe.wait_ge(weighed_ready, i * N + (n + 1))
                        pe.matmul(sum_bank[c][:, :], w2[par][:, :], weighed[:, n % 4, :], start=False, stop=True,
                                  skip_group_check=True).then_inc(summed, 1)
                for c in range(NCH):
                    pe.wait_ge(sum_out, c + 1)
                    for k in range(4):
                        last = pe.transpose((hid_bank + wgt_bank)[c][:, k * P:(k + 1) * P], outT[:, (4 * c + k) * P:(4 * c + k + 1) * P],
                                            t.identity[:, :])
                    last.then_inc(turn_ready, 1)


def two_layers(nc, d, out):
    t = Tensors()
    ctx = ExitStack()
    with ctx:
        def sb(name, shape, dt=F32):
            return ctx.enter_context(nc.sbuf_tensor(name, shape, dt))

        t.x = sb("x", [P, NT, D])
        t.identity = sb("identity", [P, P])
        t.mask32 = sb("mask32", [P, P])
        t.seen = sb("seen", [P, P])
        t.rope = sb("rope", [P, 4, S])
        t.values0 = sb("values0", [P, B * H0 * TB * HD0])
        t.attn0 = sb("attn0", [P, B * H0 * TB * HD0])
        t.parts_dram = [nc.dram_tensor(f"{name}_parts", (3, B * P, S), BF16, kind="Internal").ap() for name in ("q", "k")]
        layer0_project(nc, t, d)
        layer0_attention(nc, t, True)
        layer0_mixture(nc, t, d)
        layer1_attention(nc, t, d, True)
        layer1_mixture(nc, t, d, out)


def shape_constants():
    import numpy as np
    f32 = np.float32
    half = (np.arange(0, D1, 2, dtype=f32) / f32(D1)).astype(f32)
    inverse_frequency = (f32(1.0) / np.power(f32(10000.0), half)).astype(f32)
    angle = np.outer(np.arange(S, dtype=f32), inverse_frequency).astype(f32)
    cos, sin = np.cos(angle).T, np.sin(angle).T
    cos, sin = np.concatenate([cos, cos]), np.concatenate([-sin, sin])
    scale = f32(1.0) / np.sqrt(f32(D1))
    rope = np.stack([cos * scale, sin * scale, cos, sin]).astype(f32)
    spread0 = np.zeros((3, E0, E0 * F0 // P, P), f32)
    for e in range(E0):
        m, side = divmod(e, 2)
        spread0[:, e, m, side * F0:(side + 1) * F0] = 1.0
    spread1 = np.zeros((3, E1, E1, P), f32)
    for e in range(E1):
        spread1[:, e, e, :] = 1.0
    later = np.triu(np.ones((P, P), bool), 1)
    return {"identity": np.eye(P, dtype=f32), "mask": np.where(later, f32(LOW), f32(0.0)).astype(f32),
            "seen": np.triu(np.ones((P, P), f32)), "rope": rope,
            "spread0": spread0.reshape(3 * E0, -1, P), "spread1": spread1.reshape(3 * E1, -1)}


def kernel(**inputs):
    import numpy as np
    import concourse.bacc as bacc
    from concourse import mybir as my
    from concourse.bass_utils import run_bass_kernel_spmd as run

    arrays = {name: np.asarray(a) for name, a in inputs.items()}
    arrays["L1_ffn_gate_w"] = arrays["L1_ffn_gate_w"].T
    arrays["L1_ffn_mlp1_w"] = arrays["L1_ffn_mlp1_w"][:, ::2, :].transpose(0, 2, 1).reshape(E1 * P, F1)
    arrays["L1_ffn_mlp1_b"] = arrays["L1_ffn_mlp1_b"][:, ::2].T
    arrays["L1_ffn_mlp2_w"] = arrays["L1_ffn_mlp2_w"].transpose(0, 2, 1).reshape(E1 * F1, D)
    arrays["L0_ffn_b1"] = arrays["L0_ffn_b1"].reshape(E0 * F0 // P, P).T
    arrays["L0_ffn_bs1"] = arrays["L0_ffn_bs1"].reshape(F0, 1)
    arrays["L0_ffn_bs2"] = arrays["L0_ffn_bs2"].reshape(D, 1)
    arrays["L0_ffn_route_scale"] = arrays["L0_ffn_route_scale"].reshape(1)
    arrays.update(shape_constants())

    nc = bacc.Bacc("TRN2", target_bir_lowering=False, num_devices=1)
    given, d = {}, {}
    for name, a in arrays.items():
        a = np.ascontiguousarray(a)
        given[f"in_{name}"] = a
        d[name] = nc.dram_tensor(f"in_{name}", a.shape, my.dt.from_np(a.dtype), kind="ExternalInput").ap()
    out = nc.dram_tensor("out_0", (B, S, D), F32, kind="ExternalOutput").ap()
    two_layers(nc, d, out)
    r = run(nc, [given], core_ids=[0])
    return r.results[0]["out_0"]
```

```python
from contextlib import ExitStack

import concourse.bass as bass
from concourse import mybir

F32 = mybir.dt.float32
BF16 = mybir.dt.bfloat16
ALU = mybir.AluOpType
ACT = mybir.ActivationFunctionType
AX_X = mybir.AxisListType.X

P = 128
B, S, D = 2, 1024, 128
T = B * S
NT = T // P
TB = S // P
CH = 512
NCH = T // CH

H0, HD0 = 16, 8
NPAIR = B * H0 // 2
NST = 6 * HD0
SHIFTS = 2 * NST
VW = 32

H1, KV1, D1 = 8, 4, 128
GQ = H1 // KV1

E0, K0, F0 = 8, 2, 64
E1, K1, F1 = 16, 4, 128
ALPHA, LIMIT = 1.702, 7.0
LOW, HIGH = -3.0e38, 3.0e38
SCALE0 = 1.0 / 128.0 ** 0.5


class Tensors:
    pass


class Chain:

    def __init__(self, engine, sem):
        self.engine, self.sem, self.n = engine, sem, 0

    def after(self, instruction):
        self.n += 1
        instruction.then_inc(self.sem, 1)
        self.engine.wait_ge(self.sem, self.n)


def over_features(column):
    return column.unsqueeze(2).broadcast_to([P, NT, D])


def normalise(dve, chain, dst, src, work, stat, eps, root_asked, root_given, turn):
    total, square_total, variance, root, inverse = (stat[:, i, :] for i in range(5))
    centred, squares = work
    chain.after(dve.reduce_sum(total, src, AX_X))
    chain.after(dve.scalar_tensor_tensor(out=centred, in0=over_features(total), scalar=-1.0 / D, in1=src,
                                         op0=ALU.mult, op1=ALU.add))
    chain.after(dve.tensor_tensor(squares, centred, centred, ALU.mult))
    chain.after(dve.reduce_sum(square_total, squares, AX_X))
    dve.tensor_scalar(variance, square_total, 1.0 / D, eps, ALU.mult, ALU.add).then_inc(root_asked, 1)
    dve.wait_ge(root_given, turn + 1)
    chain.after(dve.reciprocal(inverse, root))
    chain.after(dve.tensor_tensor(dst, centred, over_features(inverse), ALU.mult))


def take_root(act, stat, root_asked, root_given, turn):
    act.wait_ge(root_asked, turn + 1)
    act.activation(stat[:, 3, :], stat[:, 2, :], ACT.Sqrt).then_inc(root_given, 1)


def transpose_tiles(pe, dst_bank, src, identity, chunk):
    for c in range(CH // P):
        last = pe.transpose(dst_bank[:, c * P:(c + 1) * P], src[:, chunk * (CH // P) + c, :], identity)
    return last


def layer0_project(nc, t, d):
    ctx = ExitStack()
    with ctx:
        def sb(name, shape, dt=F32):
            return ctx.enter_context(nc.sbuf_tensor(name, shape, dt))

        def sem(name):
            return ctx.enter_context(nc.semaphore(name))

        normed = sb("l0_normed", [P, NT, D])
        centred = sb("l0_centred", [P, NT, D])
        squares = sb("l0_squares", [P, NT, D])
        normedT = sb("l0_normedT", [P, T])
        stat = sb("l0_stat", [P, 5, NT])
        w_qkv = sb("l0_w_qkv", [P, 3, D])
        affine = sb("l0_affine", [P, 2, D])
        parts = [sb("l0_q_parts", [P, 3, T], BF16), sb("l0_k_parts", [P, 3, T], BF16)]
        rest = sb("l0_rest", [P, 2, CH])
        banks = [ctx.enter_context(nc.psum_tensor(f"l0_bank{i}", [P, CH], F32)) for i in range(4)]

        x_in, w_in = sem("x_in"), sem("w_in")
        dve_step, root_asked, root_given = sem("dve_step"), sem("root_asked"), sem("root_given")
        normed_ready, tr_ready, tr_out = sem("normed_ready"), sem("tr_ready"), sem("tr_out")
        qk_ready, hi_ready, rest_ready = sem("qk_ready"), sem("hi_ready"), sem("rest_ready")
        mid_ready, lo_ready = sem("mid_ready"), sem("lo_ready")
        v_ready, v_out, parts_out = sem("v_ready"), sem("v_out"), sem("parts_out")
        consts_in = sem("consts_in")

        with nc.Block() as block:
            @block.sync
            def _(sp):
                sp.dma_start(t.x[:, :, :], d["L0_attn_x"].rearrange("b (t p) d -> p (b t) d", p=P)).then_inc(x_in, 16)
                for i, name in enumerate(("L0_attn_wq", "L0_attn_wk", "L0_attn_wv")):
                    sp.dma_start(w_qkv[:, i, :], d[name]).then_inc(w_in, 16)
                for i, name in enumerate(("L0_attn_ln_scale", "L0_attn_ln_bias")):
                    sp.dma_start(affine[:, i, :], d[name].partition_broadcast(P)).then_inc(w_in, 16)
                sp.dma_start(t.identity[:, :], d["identity"]).then_inc(w_in, 16)
                for which in range(2):
                    for b in range(B):
                        sp.wait_ge(lo_ready, which * NCH + (b + 1) * (NCH // B))
                        sp.dma_start(t.parts_dram[which][:, b * P:(b + 1) * P, :].rearrange("a r s -> r a s"),
                                     parts[which][:, :, b * S:(b + 1) * S]).then_inc(parts_out, 16)
                sp.wait_ge(parts_out, 16 * 2 * B)

            @block.gpsimd
            def _(pool):
                pool.dma_start(t.rope[:, :, :], d["rope"].rearrange("a p s -> p a s")).then_inc(consts_in, 16)
                pool.wait_ge(consts_in, 16)

            @block.vector
            def _(dve):
                chain = Chain(dve, dve_step)
                dve.wait_ge(x_in, 16)
                work = (centred[:, :, :], squares[:, :, :])
                normalise(dve, chain, normed[:, :, :], t.x[:, :, :], work, stat, 1e-5, root_asked, root_given, 0)
                normalise(dve, chain, normed[:, :, :], normed[:, :, :], work, stat, 1e-6, root_asked, root_given, 1)
                dve.wait_ge(w_in, 16 * 6)
                scale, bias = (affine[:, i, :].unsqueeze(1).broadcast_to([P, NT, D]) for i in range(2))
                chain.after(dve.tensor_tensor(centred[:, :, :], normed[:, :, :], scale, ALU.mult))
                dve.tensor_tensor(normed[:, :, :], centred[:, :, :], bias, ALU.add).then_inc(normed_ready, 1)
                for c in range(NCH):
                    dve.wait_ge(tr_ready, c + 1)
                    dve.tensor_copy(normedT[:, c * CH:(c + 1) * CH], banks[c][:, :]).then_inc(tr_out, 1)
                dve.wait_ge(normed_ready, 1)
                dve.tensor_tensor(t.x[:, :, :], t.x[:, :, :], normed[:, :, :], ALU.add)
                for u in range(2 * NCH):
                    which, c = u // NCH, u % NCH
                    cols = slice(c * CH, (c + 1) * CH)
                    dve.wait_ge(hi_ready, u + 1)
                    dve.tensor_tensor(rest[:, u % 2, :], banks[u % 4][:, :], parts[which][:, 0, cols],
                                      ALU.subtract).then_inc(rest_ready, 1)
                    dve.wait_ge(mid_ready, u + 1)
                    dve.tensor_tensor(parts[which][:, 2, cols], rest[:, u % 2, :], parts[which][:, 1, cols],
                                      ALU.subtract).then_inc(lo_ready, 1)
                for c in range(NCH):
                    b, first = c // (NCH // B), (c % (NCH // B)) * 4
                    dve.wait_ge(v_ready, c + 1)
                    dst = t.values0[:, b * H0 * S // P * HD0:(b + 1) * H0 * S // P * HD0].rearrange(
                        "p (h t w) -> p t h w", h=H0, w=HD0)[:, first:first + 4, :, :]
                    dve.tensor_copy(dst, banks[c][:, :].rearrange("p (t h w) -> p t h w", t=4, w=HD0)).then_inc(v_out, 1)

            @block.scalar
            def _(act):
                take_root(act, stat, root_asked, root_given, 0)
                take_root(act, stat, root_asked, root_given, 1)
                for u in range(2 * NCH):
                    which, c = u // NCH, u % NCH
                    cols = slice(c * CH, (c + 1) * CH)
                    act.wait_ge(qk_ready, u + 1)
                    act.activation(parts[which][:, 0, cols], banks[u % 4][:, :], ACT.Copy).then_inc(hi_ready, 1)
                    act.wait_ge(rest_ready, u + 1)
                    act.activation(parts[which][:, 1, cols], rest[:, u % 2, :], ACT.Copy).then_inc(mid_ready, 1)

            @block.tensor
            def _(pe):
                pe.wait_ge(w_in, 16 * 6)
                pe.wait_ge(normed_ready, 1)
                for c in range(NCH):
                    transpose_tiles(pe, banks[c], normed, t.identity[:, :], c).then_inc(tr_ready, 1)
                for u in range(2 * NCH):
                    which, c = u // NCH, u % NCH
                    if u < NCH:
                        pe.wait_ge(tr_out, NCH if u == 0 else NCH)
                    else:
                        pe.wait_ge(rest_ready, u - 3)
                    pe.matmul(banks[u % 4][:, :], w_qkv[:, which, :], normedT[:, c * CH:(c + 1) * CH],
                              start=True, stop=True).then_inc(qk_ready, 1)
                for c in range(NCH):
                    pe.wait_ge(rest_ready, NCH + c + 1)
                    for k in range(4):
                        tile = 4 * c + k
                        last = pe.matmul(banks[c][:, k * P:(k + 1) * P], normedT[:, tile * P:(tile + 1) * P],
                                         w_qkv[:, 2, :], start=True, stop=True)
                    last.then_inc(v_ready, 1)


MAX_LEAD = 22
STACKS = 4
PROB_STEPS = 4


def layer0_attention(nc, t):
    assert 16 <= MAX_LEAD <= 24 and MAX_LEAD % 2 == 0
    TILES = 2 * TB
    TURN_AT = (TILES - MAX_LEAD % TILES) // 2
    ctx = ExitStack()
    with ctx:
        def sb(name, shape, dt=F32):
            return ctx.enter_context(nc.sbuf_tensor(name, shape, dt))

        def ps(name, shape):
            return ctx.enter_context(nc.psum_tensor(name, shape, F32))

        def sem(name):
            return ctx.enter_context(nc.semaphore(name))

        q_stack = [sb(f"q_stack{i}", [P, S], BF16) for i in range(STACKS)]
        k_stack = [[sb(f"k_stack{i}_{x}", [P, S], BF16) for x in range(2)] for i in range(STACKS)]
        v_tile = [sb(f"v_tile{i}", [P, 2, TB, VW]) for i in range(2)]
        probs = sb("probs", [P, PROB_STEPS, 4, CH])
        heads = [sb(f"heads{i}", [P, CH]) for i in range(2)]
        inverse = sb("inverse", [P, 2, P // 8])
        maxima = sb("maxima", [P, 2, TILES])
        shift = sb("shift", [TILES, 2, P], BF16)
        score_bank = [ps(f"score_bank{i}", [P, CH]) for i in range(2)]
        max_bank = [ps(f"max_bank{i}", [P, S]) for i in range(2)]
        summed = ps("summed", [P, CH])
        turned = ps("turned", [P, CH])

        loaded = [sem(f"loaded{i}") for i in range(STACKS)]
        shift_in = [sem(f"shift_in{i}") for i in range(STACKS)]
        staged, ones_set, zeros_set, rows_set = sem("staged"), sem("ones_set"), sem("zeros_set"), sem("rows_set")
        score_ready, prob_ready, used = sem("score_ready"), sem("prob_ready"), sem("used")
        plain_ready, max_ready = sem("plain_ready"), sem("max_ready")
        maxT_ready, high_ready, shift_ready = sem("maxT_ready"), sem("high_ready"), sem("shift_ready")
        heads_ready, turned_ready = sem("heads_ready"), sem("turned_ready")
        inverse_ready, written = sem("inverse_ready"), sem("written")

        def each_pair(engine, body):
            body(0, 0)
            with engine.Fori(0, NPAIR // 4 - 1) as g:
                for s in range(1, 5):
                    body(g, s)
            for s in range(1, 4):
                body(NPAIR // 4 - 1, s)

        def ahead(g, s, n):
            return not isinstance(g, int) or 4 * g + s + n < NPAIR

        def first(g, s):
            return isinstance(g, int) and 4 * g + s == 0

        def searched_at(k):
            return [divmod(MAX_LEAD + 2 * k + i, TILES) for i in range(2)]

        with nc.Block() as block:
            @block.sync
            def _(sp):
                q_dram, k_dram = t.parts_dram

                def load(pair, stack):
                    for x in range(2):
                        head = bass.ds(pair * (2 * HD0) + x * HD0, HD0)
                        for n, (q_part, k_part) in enumerate(((0, 0), (0, 1), (0, 2), (1, 0), (1, 1), (2, 0))):
                            rows_n = slice(x * NST + n * HD0, x * NST + (n + 1) * HD0)
                            sp.dma_start(q_stack[stack][rows_n, :], q_dram[q_part, head, :]).then_inc(loaded[stack], 16)
                            sp.dma_start(k_stack[stack][x][rows_n, :], k_dram[k_part, head, :]).then_inc(loaded[stack], 16)

                def subtract(stack):
                    for x in range(2):
                        for part in range(2):
                            row = SHIFTS + 2 * x + part
                            sp.dma_start(q_stack[stack][row:row + 1, :], shift[x * TB:(x + 1) * TB, part, :]).then_inc(shift_in[stack], 16)

                for pair in range(3):
                    sp.wait_ge(zeros_set, 2 * (pair + 1))
                    load(pair, pair)
                sp.wait_ge(shift_ready, 1)
                subtract(0)

                def body(g, s):
                    if ahead(g, s, 1):
                        sp.wait_ge(shift_ready, g * 4 + (s + 2))
                        subtract((s + 1) % STACKS)
                    if ahead(g, s, 3):
                        if not first(g, s):
                            sp.wait_ge(score_ready, g * (4 * 32) + s * 32)
                        load(g * 4 + (s + 3), (s + 3) % STACKS)

                each_pair(sp, body)

            @block.gpsimd
            def _(pool):
                for i in range(STACKS):
                    for x in range(2):
                        pool.memset(k_stack[i][x][0:SHIFTS, :], 0.0).then_inc(zeros_set, 1)
                for i in range(2):
                    pool.memset(v_tile[i][:, :, :, :], 0.0).then_inc(ones_set, 1)
                pool.wait_ge(ones_set, 2)
                for i in range(2):
                    pool.memset(v_tile[i][:, :, :, HD0:HD0 + 1], 1.0).then_inc(ones_set, 1)

            @block.vector
            def _(dve):
                def search(g, s, away, n):
                    m = (s + away) * TILES + n
                    dve.wait_ge(plain_ready, g * (4 * TILES) + (m + 1))
                    dve.reduce_max(maxima[:, (s + away) % 2, n:n + 1], max_bank[n % 2][:, :], AX_X).then_inc(max_ready, 1)

                def split(g, s):
                    dve.wait_ge(maxT_ready, g * 4 + (s + 1))
                    if not first(g, s):
                        dve.wait_ge(shift_in[(s - 1) % STACKS], g * 64 + ((s - 1) // STACKS + 1) * 64)
                    mT = turned[0:TILES, 0:P]
                    dve.tensor_scalar(shift[:, 0, :], mT, -1.0, None, ALU.mult).then_inc(high_ready, 1)
                    dve.wait_ge(high_ready, g * 4 + (s + 1))
                    dve.scalar_tensor_tensor(out=shift[:, 1, :], in0=mT, scalar=-1.0, in1=shift[:, 0, :],
                                             op0=ALU.mult, op1=ALU.subtract).then_inc(shift_ready, 1)

                def stage(g, s):
                    for x in range(2):
                        src = t.values0[:, bass.ds(g * (8 * TB * HD0) + (2 * s + x) * TB * HD0, TB * HD0)]
                        dve.tensor_scalar(v_tile[s % 2][:, x, :, 0:HD0], src.rearrange("p (t w) -> p t w", w=HD0), 1.0, None,
                                          ALU.mult).then_inc(staged, 1)

                def divide(g, s):
                    dve.wait_ge(turned_ready, g * 4 + (s + 1))
                    tv = turned[:, :].rearrange("p (c h w) -> p c h w", c=4, w=VW)
                    inv = inverse[:, s % 2, :].rearrange("p (c h) -> p c h", c=4)
                    dve.reciprocal(inv, tv[:, :, :, HD0]).then_inc(inverse_ready, 1)
                    dve.wait_ge(inverse_ready, g * 4 + (s + 1))
                    dst = t.attn0[:, bass.ds(g * (4 * P) + s * P, P)].rearrange("p (h c w) -> p c h w", h=4, w=HD0)
                    dve.tensor_tensor(dst, tv[:, :, :, 0:HD0], inv.unsqueeze(3).broadcast_to([P, 4, 4, HD0]),
                                      ALU.mult).then_inc(written, 1)

                for i in range(STACKS):
                    for x in range(2):
                        own = [t.identity[SHIFTS:P, SHIFTS + 2 * x + part:SHIFTS + 2 * x + part + 1].broadcast_to([P - SHIFTS, S])
                               for part in range(2)]
                        dve.tensor_tensor(k_stack[i][x][SHIFTS:P, :], own[0], own[1], ALU.add).then_inc(rows_set, 1)
                dve.wait_ge(ones_set, 4)
                stage(0, 0)
                for m in range(MAX_LEAD):
                    if m == TILES + 2:
                        split(0, 0)
                    search(0, 0, *divmod(m, TILES))

                def body(g, s):
                    for k in range(TB):
                        for away, n in searched_at(k):
                            if ahead(g, s, away):
                                search(g, s, away, n)
                        if k == 3 and not first(g, s):
                            divide(g, s - 1)
                        if k == TURN_AT and ahead(g, s, 1):
                            split(g, s + 1)
                        if k == 6 and ahead(g, s, 1):
                            if not first(g, s):
                                dve.wait_ge(used, g * (4 * TB) + s * TB)
                            stage(g, s + 1)

                each_pair(dve, body)
                divide(NPAIR // 4 - 1, 3)

            @block.scalar
            def _(act):
                def take(g, s):
                    act.wait_ge(used, g * (4 * TB) + (s + 1) * TB)
                    act.activation(heads[s % 2][:, :], summed[:, :], ACT.Copy).then_inc(heads_ready, 1)

                def body(g, s):
                    for k in range(TB):
                        for j in range(4):
                            act.wait_ge(score_ready, g * (4 * 32) + (s * 32 + 4 * k + j + 1))
                            if j == 0 and (k >= PROB_STEPS or not first(g, s)):
                                act.wait_ge(used, g * (4 * TB) + (s * TB + k - PROB_STEPS + 1))
                            act.activation(probs[:, k % PROB_STEPS, j, :], score_bank[j % 2][:, :], ACT.Exp, scale=SCALE0).then_inc(prob_ready, 1)
                            if k == 0 and j == 1 and not first(g, s):
                                take(g, s - 1)

                each_pair(act, body)
                take(NPAIR // 4 - 1, 3)

            @block.tensor
            def _(pe):
                def search(g, s, away, n):
                    m = (s + away) * TILES + n
                    x, qt = divmod(n, TB)
                    stack = (s + away) % STACKS
                    if n == 0:
                        pe.wait_ge(loaded[stack], g * (24 * 16) + ((s + away) // STACKS + 1) * (24 * 16))
                    if m >= 2:
                        pe.wait_ge(max_ready, g * (4 * TILES) + (m - 1))
                    for half in range(2):
                        last = pe.matmul(max_bank[n % 2][:, half * CH:(half + 1) * CH], q_stack[stack][0:SHIFTS, qt * P:(qt + 1) * P],
                                         k_stack[stack][x][0:SHIFTS, half * CH:(half + 1) * CH], start=True, stop=True)
                    last.then_inc(plain_ready, 1)

                def turn_maxima(g, s):
                    pe.wait_ge(max_ready, g * (4 * TILES) + (s + 1) * TILES)
                    if 4 * (g if isinstance(g, int) else 1) + s >= 2:
                        pe.wait_ge(written, g * 4 + (s - 1))
                    pe.transpose(turned[0:TILES, 0:P], maxima[:, s % 2, :], t.identity[:, :]).then_inc(maxT_ready, 1)

                def turn_heads(g, s):
                    pe.wait_ge(heads_ready, g * 4 + (s + 1))
                    if ahead(g, s, 1):
                        pe.wait_ge(shift_ready, g * 4 + (s + 2))
                    else:
                        pe.wait_ge(written, g * 4 + s)
                    for c in range(4):
                        last = pe.transpose(turned[:, c * P:(c + 1) * P], heads[s % 2][:, c * P:(c + 1) * P], t.identity[:, :])
                    last.then_inc(turned_ready, 1)

                def score(g, s, k, j):
                    x, half = divmod(j, 2)
                    rows, e = slice(0, SHIFTS + 4), s * 32 + 4 * k + j
                    if (k, j) == (0, 0):
                        pe.wait_ge(shift_in[s % STACKS], g * 64 + (s // STACKS + 1) * 64)
                    if not isinstance(g, int) or 32 * 4 * g + e >= 2:
                        pe.wait_ge(prob_ready, g * (4 * 32) + (e - 1))
                    pe.matmul(score_bank[j % 2][:, :], k_stack[s % STACKS][x][rows, k * P:(k + 1) * P],
                              q_stack[s % STACKS][rows, half * CH:(half + 1) * CH], start=True, stop=True).then_inc(score_ready, 1)

                def use(g, s, k):
                    if k == 0:
                        pe.wait_ge(staged, g * 8 + (2 * s + 2))
                        if not first(g, s):
                            pe.wait_ge(heads_ready, g * 4 + s)
                    pe.wait_ge(prob_ready, g * (4 * 32) + (s * 32 + 4 * k + 4))
                    for j in range(4):
                        last = pe.matmul(summed[VW * j:VW * (j + 1), :], v_tile[s % 2][:, j // 2, k, :], probs[:, k % PROB_STEPS, j, :],
                                         start=(k == 0), stop=(k == TB - 1), tile_position=(0, VW * j))
                    last.then_inc(used, 1)

                pe.wait_ge(rows_set, 2 * STACKS)
                for m in range(MAX_LEAD):
                    if m == TILES + 2:
                        turn_maxima(0, 0)
                    search(0, 0, *divmod(m, TILES))

                def body(g, s):
                    for k in range(TB):
                        tiles = [tile for tile in searched_at(k) if ahead(g, s, tile[0])]
                        for j in range(2):
                            score(g, s, k, j)
                        if k == 0 and tiles:
                            search(g, s, *tiles.pop(0))
                        if k > 0:
                            use(g, s, k - 1)
                        if k == 2 and not first(g, s):
                            turn_heads(g, s - 1)
                        if k == TURN_AT and ahead(g, s, 1):
                            turn_maxima(g, s + 1)
                        for j in range(2, 4):
                            score(g, s, k, j)
                        for tile in tiles:
                            search(g, s, *tile)
                    use(g, s, TB - 1)

                each_pair(pe, body)
                turn_heads(NPAIR // 4 - 1, 3)


def choose(dve, chain, padded, experts, chosen, top, wanted, marked):
    for tile in range(NT):
        last = dve.max(out=top[:, tile, :], in_=padded[:, tile, 0:experts])
    chain.after(last)
    chain.after(dve.tensor_copy(wanted[:, :, 0:chosen], top[:, :, 0:chosen]))
    for tile in range(NT):
        last = dve.match_replace(out=marked[:, tile, :], in_to_replace=wanted[:, tile, :],
                                 in_values=padded[:, tile, :], imm_value=HIGH)
    chain.after(last)
    chain.after(dve.tensor_scalar(marked[:, :, 0:experts], marked[:, :, 0:experts], HIGH, None, ALU.is_equal))


def split_weights(dve, chain, weight, parts, rest):
    chain.after(dve.tensor_copy(parts[:, :, 0, :], weight))
    chain.after(dve.tensor_tensor(rest[0], weight, parts[:, :, 0, :], ALU.subtract))
    chain.after(dve.tensor_copy(parts[:, :, 1, :], rest[0]))
    return dve.tensor_tensor(parts[:, :, 2, :], rest[0], parts[:, :, 1, :], ALU.subtract)


def layer0_mixture(nc, t, d):
    NP0 = E0 * F0 // P
    NU = NP0 + 1
    pad = E0 + 8 - K0
    ctx = ExitStack()
    with ctx:
        def sb(name, shape, dt=F32):
            return ctx.enter_context(nc.sbuf_tensor(name, shape, dt))

        def ps(name, shape, dt=F32):
            return ctx.enter_context(nc.psum_tensor(name, shape, dt))

        def sem(name):
            return ctx.enter_context(nc.semaphore(name))

        normed = sb("m0_normed", [P, NT, D])
        centred = sb("m0_centred", [P, NT, D])
        squares = sb("m0_squares", [P, NT, D])
        inT = sb("m0_inT", [P, T])
        stat = sb("m0_stat", [P, 5, NT])
        gate_w = sb("m0_gate_w", [P, E0])
        route = sb("m0_route", [P, 1])
        w1 = sb("m0_w1", [P, NP0, 2, F0])
        ws1 = sb("m0_ws1", [P, P])
        w2 = sb("m0_w2", [P, NP0, D])
        ws2 = sb("m0_ws2", [P, D])
        b1 = sb("m0_b1", [P, NU])
        b2x3 = sb("m0_b2x3", [3 * E0, D])
        bs2 = sb("m0_bs2", [P, 1])
        spread32 = sb("m0_spread32", [3 * E0, NP0, P])
        spread = sb("m0_spread", [3 * E0, NP0, P], BF16)
        padded = sb("m0_padded", [P, NT, pad])
        marked = sb("m0_marked", [P, NT, pad])
        top, wanted = sb("m0_top", [P, NT, 8]), sb("m0_wanted", [P, NT, 8])
        weight = sb("m0_weight", [P, NT, E0])
        rest = sb("m0_rest", [P, NT, E0])
        total = sb("m0_total", [P, 2, NT])
        parts = sb("m0_parts", [P, NT, 3, E0], BF16)
        weightT = sb("m0_weightT", [3 * E0, T], BF16)
        weightT32 = sb("m0_weightT32", [3 * E0, T])
        hidden = sb("m0_hidden", [P, NU, CH])
        weighed = sb("m0_weighed", [P, NP0, CH])
        outT = sb("m0_outT", [P, CH])
        identity16 = sb("m0_identity16", [P, P], BF16)
        hid_bank = [ps(f"m0_hid{i}", [P, CH]) for i in range(2)]
        wgt_bank = [ps(f"m0_wgt{i}", [P, CH]) for i in range(2)]
        sum_bank, turn_bank = ps("m0_sum", [P, CH]), ps("m0_turn", [P, NT // 4, D])
        gate_bank = ps("m0_gate", [P, NT, E0])
        part_bank = ps("m0_part", [3 * E0, CH], BF16)

        w_in, dve_step, root_asked, root_given = sem("w_in"), sem("dve_step"), sem("root_asked"), sem("root_given")
        low_set, normed_ready, tr_ready, tr_out = sem("low_set"), sem("normed_ready"), sem("tr_ready"), sem("tr_out")
        gate_ready, prob_ready, cast_ready = sem("gate_ready"), sem("prob_ready"), sem("cast_ready")
        parts_ready, partT_ready, partT_out = sem("parts_ready"), sem("partT_ready"), sem("partT_out")
        hid_ready, act_ready, wgt_ready, weighed_ready = sem("hid_ready"), sem("act_ready"), sem("wgt_ready"), sem("weighed_ready")
        sum_ready, out_ready, turn_ready, added = sem("sum_ready"), sem("out_ready"), sem("turn_ready"), sem("added")
        NW = 15

        with nc.Block() as block:
            @block.sync
            def _(sp):
                def load(dst, src):
                    sp.dma_start(dst, src).then_inc(w_in, 16)

                sp.wait_ge(low_set, 5)
                load(gate_w[:, :], d["L0_ffn_gate_W"])
                load(route[:, :], d["L0_ffn_route_scale"].partition_broadcast(P))
                load(w1[:, :, :, :].rearrange("p m e f -> p (m e) f"), d["L0_ffn_W1"].rearrange("e d f -> d e f"))
                load(ws1[:, 0:F0], d["L0_ffn_Ws1"])
                load(w2[:, :, :], d["L0_ffn_W2"].rearrange("(m e) f d -> (e f) m d", e=2))
                load(ws2[0:F0, :], d["L0_ffn_Ws2"])
                load(b1[:, 0:NP0], d["L0_ffn_b1"])
                load(b1[0:F0, NP0:NU], d["L0_ffn_bs1"])
                for i in range(3):
                    load(b2x3[i * E0:(i + 1) * E0, :], d["L0_ffn_b2"])
                load(bs2[:, :], d["L0_ffn_bs2"])
                load(spread32[:, :, :], d["spread0"])
                load(t.mask32[:, :], d["mask"])
                load(t.seen[:, :], d["seen"])

            @block.gpsimd
            def _(pool):
                pool.memset(padded[:, :, E0:pad], LOW).then_inc(low_set, 1)
                pool.memset(wanted[:, :, K0:8], LOW).then_inc(low_set, 1)
                pool.memset(ws1[:, F0:P], 0.0).then_inc(low_set, 1)
                pool.wait_ge(low_set, 3)
                pool.memset(ws2[F0:P, :], 0.0).then_inc(low_set, 1)
                pool.memset(b1[F0:P, NP0:NU], 0.0).then_inc(low_set, 1)
                pool.wait_ge(w_in, 16 * NW)
                pool.tensor_copy(spread[:, :, :], spread32[:, :, :]).then_inc(cast_ready, 1)
                pool.tensor_copy(identity16[:, :], t.identity[:, :]).then_inc(cast_ready, 1)

            @block.vector
            def _(dve):
                chain = Chain(dve, dve_step)
                for b in range(B):
                    half = t.x[:, b * TB:(b + 1) * TB, :].rearrange("p t (h w) -> p h t w", w=HD0)
                    src = t.attn0[:, b * S:(b + 1) * S].rearrange("p (h t w) -> p h t w", h=H0, w=HD0)
                    last = dve.tensor_tensor(half, half, src, ALU.add)
                chain.after(last)
                normalise(dve, chain, normed[:, :, :], t.x[:, :, :], (centred[:, :, :], squares[:, :, :]), stat, 1e-5,
                          root_asked, root_given, 0)
                dve.engine_nop().then_inc(normed_ready, 1)
                for c in range(NCH):
                    dve.wait_ge(tr_ready, c + 1)
                    bank = (hid_bank + wgt_bank)[c]
                    dve.tensor_copy(inT[:, c * CH:(c + 1) * CH], bank[:, :]).then_inc(tr_out, 1)
                dve.wait_ge(w_in, 16 * NW)
                dve.wait_ge(low_set, 2)
                dve.wait_ge(prob_ready, 1)
                chain.after(dve.tensor_scalar(padded[:, :, 0:E0], weight[:, :, :], route[:, 0:1], None, ALU.mult))
                choose(dve, chain, padded, E0, K0, top, wanted, marked)
                chain.after(dve.tensor_tensor(weight[:, :, :], padded[:, :, 0:E0], marked[:, :, 0:E0], ALU.mult))
                chain.after(dve.tensor_tensor(total[:, 0, :], top[:, :, 0], top[:, :, 1], ALU.add))
                chain.after(dve.reciprocal(total[:, 1, :], total[:, 0, :]))
                chain.after(dve.tensor_tensor(weight[:, :, :], weight[:, :, :],
                                              total[:, 1, :].unsqueeze(2).broadcast_to([P, NT, E0]), ALU.mult))
                split_weights(dve, chain, weight[:, :, :], parts, [rest[:, :, :]]).then_inc(parts_ready, 1)
                for c in range(NCH):
                    cols = slice(c * CH, (c + 1) * CH)
                    dve.wait_ge(partT_ready, c + 1)
                    chain.after(dve.tensor_copy(weightT[:, cols], part_bank[:, :]))
                    dve.tensor_copy(weightT32[:, cols], weightT[:, cols]).then_inc(partT_out, 1)
                with dve.Fori(0, NCH) as c:
                    for m in range(NP0):
                        dve.wait_ge(act_ready, c * NU + (m + 1))
                        dve.wait_ge(wgt_ready, c * NP0 + (m + 1))
                        dve.wait_ge(sum_ready, c)
                        dve.tensor_tensor(weighed[:, m, :], hidden[:, m, :], wgt_bank[m % 2][:, :], ALU.mult).then_inc(weighed_ready, 1)
                    dve.wait_ge(turn_ready, c + 1)
                    xs = t.x[:, :, :].rearrange("p t d -> p (t d)")[:, bass.ds(c * CH, CH)]
                    dve.tensor_tensor(xs, turn_bank[:, :, :].rearrange("p t d -> p (t d)"), xs, ALU.add).then_inc(added, 1)

            @block.scalar
            def _(act):
                take_root(act, stat, root_asked, root_given, 0)
                act.wait_ge(gate_ready, 1)
                act.activation(weight[:, :, :], gate_bank[:, :, :], ACT.Sigmoid).then_inc(prob_ready, 1)
                act.wait_ge(w_in, 16 * NW)
                with act.Fori(0, NCH) as c:
                    for m in range(NU):
                        act.wait_ge(hid_ready, c * NU + (m + 1))
                        if m < NP0:
                            act.wait_ge(weighed_ready, c * NP0)
                        else:
                            act.wait_ge(sum_ready, c)
                        act.activation(hidden[:, m, :], hid_bank[m % 2][:, :], ACT.Gelu, bias=b1[:, m:m + 1]).then_inc(act_ready, 1)
                    act.wait_ge(sum_ready, c + 1)
                    act.wait_ge(turn_ready, c)
                    act.activation(outT[:, :], sum_bank[:, :], ACT.Identity, bias=bs2[:, 0:1]).then_inc(out_ready, 1)

            @block.tensor
            def _(pe):
                pe.wait_ge(normed_ready, 1)
                for c in range(NCH):
                    transpose_tiles(pe, (hid_bank + wgt_bank)[c], normed, t.identity[:, :], c).then_inc(tr_ready, 1)
                pe.wait_ge(w_in, 16 * NW)
                pe.wait_ge(tr_out, NCH)
                for tile in range(NT):
                    last = pe.matmul(gate_bank[:, tile, :], inT[:, tile * P:(tile + 1) * P], gate_w[:, :], start=True, stop=True)
                last.then_inc(gate_ready, 1)
                pe.wait_ge(cast_ready, 2)
                pe.wait_ge(parts_ready, 1)
                for c in range(NCH):
                    if c:
                        pe.wait_ge(partT_out, c)
                    for k in range(4):
                        last = pe.transpose(part_bank[:, k * P:(k + 1) * P],
                                            parts[:, 4 * c + k, :, :].rearrange("p a e -> p (a e)"), identity16[:, :])
                    last.then_inc(partT_ready, 1)
                pe.wait_ge(partT_out, NCH)
                with pe.Fori(0, NCH) as c:
                    cols = bass.ds(c * CH, CH)

                    def up(m):
                        if m < NP0:
                            pe.wait_ge(weighed_ready, c * NP0 + max(m - 1, 0))
                        pe.wait_ge(act_ready, c * NU + max(m - 1, 0))
                        w = w1[:, m, :, :].rearrange("p e f -> p (e f)") if m < NP0 else ws1[:, :]
                        pe.matmul(hid_bank[m % 2][:, :], w, inT[:, cols], start=True, stop=True).then_inc(hid_ready, 1)
                        if m < NP0:
                            pe.matmul(wgt_bank[m % 2][:, :], spread[:, m, :], weightT[:, cols], start=True, stop=True).then_inc(wgt_ready, 1)

                    pe.wait_ge(out_ready, c)
                    up(0)
                    up(1)
                    pe.matmul(sum_bank[:, :], b2x3[:, :], weightT32[:, cols], start=True, stop=False)
                    for m in range(NU):
                        if m + 2 < NU:
                            up(m + 2)
                        if m < NP0:
                            pe.wait_ge(weighed_ready, c * NP0 + (m + 1))
                            pe.matmul(sum_bank[:, :], w2[:, m, :], weighed[:, m, :], start=False, stop=False)
                        else:
                            pe.wait_ge(act_ready, c * NU + NU)
                            pe.matmul(sum_bank[:, :], ws2[:, :], hidden[:, m, :], start=False, stop=True).then_inc(sum_ready, 1)
                    pe.wait_ge(out_ready, c + 1)
                    pe.wait_ge(added, c)
                    for k in range(4):
                        last = pe.transpose(turn_bank[:, k, :], outT[:, k * P:(k + 1) * P], t.identity[:, :])
                    last.then_inc(turn_ready, 1)


QB = 4
BLOCKS = [(b, q, half) for b in range(B) for q in range(GQ) for half in range(TB // QB)]
NB = len(BLOCKS)
NS = NB * QB
TURNS = [(k, j) for k in range(NB) for j in range(QB * (BLOCKS[k][2] + 1))]
NTURN = len(TURNS)
TURNED_BY = [sum(1 for k, _ in TURNS if k <= block) for block in range(NB)]
NPROJ = 2 + 2 * GQ + 2
NROT = NPROJ - 2


def attention_order(last):
    units = []
    for k in range(NB):
        width = QB * (BLOCKS[k][2] + 1)
        ahead = [QB * (k + 1) + c for c in range(QB)] if k + 1 < NB or not last else []
        scores_at = [0, 0, 1, 2] if width == QB else [0, 1, 3, 5]
        if k == 0:
            units = [(1, u) for u in range(NPROJ)]
        if k == NB // 2:
            units = [] if last else [(0, u) for u in range(NPROJ)]
        placed = None
        for j in range(width + 1):
            if j < width:
                yield "turn", (k, j)
            if placed:
                yield "place", placed
                placed = None
            for n in (n for at, n in zip(scores_at, ahead) if at == j):
                yield "score", n
            if j >= 1:
                yield "use", (k, j - 1)
            if j == 2 and k:
                yield "output", k - 1
            if j == 3 and k:
                yield "close", k - 1
            if units and j % 2 and j < width:
                placed = units.pop(0)
                yield "project", placed
        if placed:
            yield "place", placed
        yield "take", k
    yield "output", NB - 1
    yield "close", NB - 1


def bank_before(last, step):
    users = [e for e in attention_order(last) if e[0] in ("project", "output")]
    i = users.index(step)
    return users[i - 1] if i else None


def layer1_attention(nc, t, d):
    SLOTS = 4
    ctx = ExitStack()
    with ctx:
        def sb(name, shape, dt=F32):
            return ctx.enter_context(nc.sbuf_tensor(name, shape, dt))

        def ps(name, shape):
            return ctx.enter_context(nc.psum_tensor(name, shape, F32))

        def sem(name):
            return ctx.enter_context(nc.semaphore(name))

        normed = sb("a1_normed", [P, NT, D])
        centred = sb("a1_centred", [P, NT, D])
        stat = sb("a1_stat", [P, 5, NT])
        inT = sb("a1_inT", [P, T])
        w_q, w_k, w_v = sb("a1_wq", [P, GQ, D1]), sb("a1_wk", [P, D1]), sb("a1_wv", [P, D1])
        w_o = sb("a1_wo", [P, GQ, D])
        kT = sb("a1_kT", [P, B, S])
        qT = sb("a1_qT", [P, B, GQ, S])
        v = sb("a1_v", [P, B, TB, D1])
        straight, crossed = sb("a1_straight", [P, 2, CH]), sb("a1_crossed", [P, 2, CH])
        probs = sb("a1_probs", [P, 2, QB, S])
        turned = sb("a1_turned", [P, SLOTS, CH])
        headsT = sb("a1_headsT", [P, 2, CH])
        lowest = sb("a1_lowest", [P, 2 * QB])
        weight = sb("a1_weight", [P, 4, QB])
        inverse = sb("a1_inverse", [P, 4, QB])
        part = sb("a1_part", [P, 2, QB, D])
        mask16, identity16 = sb("a1_mask16", [P, P], BF16), sb("a1_identity16", [P, P], BF16)
        scores = [ps(f"a1_scores{i}", [P, S]) for i in range(2)]
        turn_bank = [ps(f"a1_turn{i}", [P, CH]) for i in range(2)]
        sum_bank, proj_bank = ps("a1_sum", [P, CH]), ps("a1_proj", [P, CH])
        first_banks = [proj_bank] + turn_bank

        dve_step, root_asked, root_given = sem("dve_step"), sem("root_asked"), sem("root_given")
        normed_ready, tr_ready, tr_out = sem("normed_ready"), sem("tr_ready"), sem("tr_out")
        w_in, wo_in, cast_ready = sem("w_in"), sem("wo_in"), sem("cast_ready")
        rot_ready, rot_taken, rotated = sem("rot_ready"), sem("rot_taken"), sem("rotated")
        v_ready, v_taken = sem("v_ready"), sem("v_taken")
        score_ready, lowest_ready, prob_ready = sem("score_ready"), sem("lowest_ready"), sem("prob_ready")
        turn_ready, used = sem("turn_ready"), sem("used")
        taken = [sem("taken_by_vector"), sem("taken_by_scalar")]
        heads_ready, out_ready, out_taken, added = sem("heads_ready"), sem("out_ready"), sem("out_taken"), sem("added")
        inverse_ready = sem("inverse_ready")

        def from_one(n):
            return n + 1

        def place_of(b, u):
            half = slice(u % 2 * CH, (u % 2 + 1) * CH)
            if u < 2:
                return kT[:, b, half]
            if u < NROT:
                return qT[:, b, (u - 2) // 2, half]
            return v[:, b, u % 2 * QB:(u % 2 + 1) * QB, :].rearrange("p t d -> p (t d)")

        def rotations(g, b, u):
            return (g * (2 * NROT) + (NROT + u + 1)) if b else (g * (2 * NROT) + (2 * NROT + u + 1))

        def copies(g, b, u):
            return (g * 4 + (2 + u - NROT + 1)) if b else (g * 4 + (4 + u - NROT + 1))

        def project(pe, bank, b, u):
            if u < NROT:
                w = w_k[:, :] if u < 2 else w_q[:, (u - 2) // 2, :]
                first = b * S + u % 2 * CH
                pe.matmul(bank[:, :], w, inT[:, first:first + CH], start=True, stop=True).then_inc(rot_ready, 1)
            else:
                for c in range(QB):
                    first = b * S + (u % 2 * QB + c) * P
                    last = pe.matmul(bank[:, c * P:(c + 1) * P], inT[:, first:first + P], w_v[:, :], start=True, stop=True)
                last.then_inc(v_ready, 1)

        def rotate(dve, bank, u, r):
            table, cols = 2 if u < 2 else 0, slice(u % 2 * CH, (u % 2 + 1) * CH)
            dve.tensor_tensor(straight[:, r % 2, :], bank[:, :], t.rope[:, table, cols], ALU.mult)
            for half in range(2):
                to, of = slice(half * 64, half * 64 + 64), slice(64 - half * 64, 128 - half * 64)
                last = dve.tensor_tensor(crossed[to, r % 2, :], bank[of, :], t.rope[to, table + 1, cols], ALU.mult)
            last.then_inc(rot_taken, 1)

        def score(pe, n):
            k, c = divmod(n, QB)
            b, q, half = BLOCKS[k % NB]
            tile = half * QB + c
            width = (tile + 1) * P
            for first in range(0, width, CH):
                cols = min(CH, width - first)
                pe.matmul(scores[n % 2][:, first:first + cols], qT[:, b, q, tile * P:(tile + 1) * P], kT[:, b, first:first + cols],
                          start=True, stop=first + cols < width)
            pe.matmul(scores[n % 2][:, width - P:width], identity16[:, :], mask16[:, :], start=False, stop=True).then_inc(score_ready, 1)

        def row_width(n):
            return (BLOCKS[n // QB % NB][2] * QB + n % QB + 1) * P

        def find_lowest(dve, n):
            dve.tensor_reduce(out=lowest[:, n % 8:n % 8 + 1], in_=scores[n % 2][:, 0:row_width(n)], op=ALU.max, axis=AX_X,
                              negate=True).then_inc(lowest_ready, 1)

        def exponentiate(act, n):
            k, c = divmod(n, QB)
            act.activation(probs[:, k % 2, c, 0:row_width(n)], scores[n % 2][:, 0:row_width(n)], ACT.Exp,
                           bias=lowest[:, n % 8:n % 8 + 1], accum_out=weight[:, k % 4, c:c + 1]).then_inc(prob_ready, 1)

        def skipped(k, j):
            return max(0, j - BLOCKS[k][2] * QB) * P

        def copy_turned(m):
            k, j = TURNS[m]
            return turned[:, m % SLOTS, skipped(k, j):CH], turn_bank[m % 2][:, skipped(k, j):CH]

        def each_head(engine, body):
            with engine.Fori(0, KV1 - 1) as g:
                body(g, False)
            body(KV1 - 1, True)

        with nc.Block() as block:
            @block.sync
            def _(sp):
                def load(g):
                    sp.dma_start(w_q[:, :, :].rearrange("p q d -> p (q d)"), d["L1_attn_Wq"][:, bass.ds(g * (GQ * D1), GQ * D1)]).then_inc(w_in, 16)
                    sp.dma_start(w_k[:, :], d["L1_attn_Wk"][:, bass.ds(g * D1, D1)]).then_inc(w_in, 16)
                    sp.dma_start(w_v[:, :], d["L1_attn_Wv"][:, bass.ds(g * D1, D1)]).then_inc(w_in, 16)

                def load_out(g):
                    for q in range(GQ):
                        sp.dma_start(w_o[:, q, :], d["L1_attn_Wo"][bass.ds(g * (GQ * D1) + q * D1, D1), :]).then_inc(wo_in, 16)

                load(0)
                load_out(0)
                with sp.Fori(0, KV1 - 1) as g:
                    sp.wait_ge(v_ready, from_one(g * 4 + 4))
                    load(g + 1)
                    sp.wait_ge(out_ready, from_one(g * NB + NB))
                    load_out(g + 1)

            @block.gpsimd
            def _(pool):
                pool.sem_inc(rotated, 1)
                pool.sem_inc(added, 1)
                pool.tensor_copy(mask16[:, :], t.mask32[:, :]).then_inc(cast_ready, 1)
                pool.tensor_copy(identity16[:, :], t.identity[:, :]).then_inc(cast_ready, 1)

                def add_rotation(b, u, count):
                    pool.wait_ge(rot_taken, from_one(count))
                    pool.tensor_tensor(place_of(b, u), straight[:, u % 2, :], crossed[:, u % 2, :], ALU.add).then_inc(rotated, 1)

                for u in range(NROT):
                    add_rotation(0, u, u + 1)

                def body(g, last):
                    for what, n in attention_order(last):
                        if what == "place" and n[1] < NROT:
                            add_rotation(*n, rotations(g, *n))
                        if what == "close":
                            b, _, half = BLOCKS[n]
                            xs = t.x[:, b * TB + half * QB:b * TB + half * QB + QB, :]
                            pool.wait_ge(out_taken, from_one(g * NB + (n + 1)))
                            pool.wait_ge(added, from_one(g * NB + n))
                            pool.tensor_tensor(xs, xs, part[:, n % 2, :, :], ALU.add).then_inc(added, 1)

                each_head(pool, body)

            @block.vector
            def _(dve):
                chain = Chain(dve, dve_step)
                for s in (rot_taken, lowest_ready, taken[0], out_taken, inverse_ready):
                    dve.sem_inc(s, 1)
                normalise(dve, chain, normed[:, :, :], t.x[:, :, :], (centred[:, :, :], normed[:, :, :]), stat, 1e-5,
                          root_asked, root_given, 0)
                dve.engine_nop().then_inc(normed_ready, 1)
                for c in range(NCH):
                    dve.wait_ge(tr_ready, c + 1)
                    dve.tensor_copy(inT[:, c * CH:(c + 1) * CH], scores[c // 2][:, c % 2 * CH:(c % 2 + 1) * CH]).then_inc(tr_out, 1)
                for u in range(NROT):
                    dve.wait_ge(rot_ready, from_one(u + 1))
                    if u >= 2:
                        dve.wait_ge(rotated, from_one(u - 1))
                    rotate(dve, first_banks[u % 3], u, u)
                for n in range(QB):
                    dve.wait_ge(score_ready, from_one(n + 1))
                    find_lowest(dve, n)

                def body(g, last):
                    for what, n in attention_order(last):
                        if what == "turn" and TURNS.index(n) % 2 == 0:
                            m = TURNS.index(n)
                            dve.wait_ge(turn_ready, from_one(g * NTURN + (m + 1)))
                            dve.wait_ge(used, from_one(g * NTURN + max(m - SLOTS + 1, 0)))
                            dve.tensor_copy(*copy_turned(m)).then_inc(taken[0], 1)
                        if what == "place" and n[1] < NROT:
                            dve.wait_ge(rot_ready, from_one(rotations(g, *n)))
                            dve.wait_ge(rotated, from_one(rotations(g, *n) - 2))
                            rotate(dve, proj_bank, n[1], n[1])
                        if what == "score":
                            dve.wait_ge(score_ready, from_one(g * NS + (n + 1)))
                            find_lowest(dve, n)
                        if what == "close":
                            dve.wait_ge(prob_ready, from_one(g * NS + (QB * n + QB)))
                            dve.reciprocal(inverse[:, n % 4, :], weight[:, n % 4, :]).then_inc(inverse_ready, 1)
                            dve.wait_ge(inverse_ready, from_one(g * NB + (n + 1)))
                            dve.wait_ge(out_ready, from_one(g * NB + (n + 1)))
                            dve.wait_ge(added, from_one(g * NB + max(n - 1, 0)))
                            dve.tensor_tensor(part[:, n % 2, :, :], proj_bank[:, :].rearrange("p (t d) -> p t d", d=D),
                                              inverse[:, n % 4, :].unsqueeze(2).broadcast_to([P, QB, D]), ALU.mult).then_inc(out_taken, 1)

                each_head(dve, body)

            @block.scalar
            def _(act):
                for s in (v_taken, prob_ready, taken[1], heads_ready):
                    act.sem_inc(s, 1)
                take_root(act, stat, root_asked, root_given, 0)
                for i in range(2):
                    act.wait_ge(v_ready, from_one(i + 1))
                    act.activation(place_of(0, NROT + i), first_banks[(NROT + i) % 3][:, :], ACT.Copy).then_inc(v_taken, 1)
                for n in range(QB):
                    act.wait_ge(lowest_ready, from_one(n + 1))
                    exponentiate(act, n)

                def body(g, last):
                    for what, n in attention_order(last):
                        if what == "turn" and TURNS.index(n) % 2 == 1:
                            m = TURNS.index(n)
                            act.wait_ge(turn_ready, from_one(g * NTURN + (m + 1)))
                            act.wait_ge(used, from_one(g * NTURN + max(m - SLOTS + 1, 0)))
                            act.activation(*copy_turned(m), ACT.Copy).then_inc(taken[1], 1)
                        if what == "place" and n[1] >= NROT:
                            act.wait_ge(v_ready, from_one(copies(g, *n)))
                            act.activation(place_of(*n), proj_bank[:, :], ACT.Copy).then_inc(v_taken, 1)
                        if what == "score":
                            k = n // QB
                            act.wait_ge(lowest_ready, from_one(g * NS + (n + 1)))
                            act.wait_ge(turn_ready, from_one(g * NTURN + (TURNED_BY[k - 2] if k >= 2 else 0)))
                            exponentiate(act, n)
                        if what == "take":
                            act.wait_ge(used, from_one(g * NTURN + TURNED_BY[n]))
                            act.wait_ge(out_ready, from_one(g * NB + max(n - 1, 0)))
                            act.activation(headsT[:, n % 2, :], sum_bank[:, :], ACT.Copy).then_inc(heads_ready, 1)

                each_head(act, body)

            @block.tensor
            def _(pe):
                for s in (rot_ready, v_ready, score_ready, turn_ready, used, out_ready):
                    pe.sem_inc(s, 1)
                pe.wait_ge(normed_ready, 1)
                for c in range(NCH):
                    transpose_tiles(pe, scores[c // 2][:, c % 2 * CH:(c % 2 + 1) * CH], normed, t.identity[:, :], c).then_inc(tr_ready, 1)
                pe.wait_ge(w_in, 48)
                pe.wait_ge(cast_ready, 2)
                pe.wait_ge(tr_out, NCH)
                for u in range(NPROJ):
                    if u >= 3:
                        pe.wait_ge(rot_taken, from_one(u - 2))
                    project(pe, first_banks[u % 3], 0, u)
                pe.wait_ge(rotated, from_one(NROT))
                for n in range(QB):
                    if n >= 2:
                        pe.wait_ge(prob_ready, from_one(n - 1))
                    score(pe, n)
                pe.wait_ge(rot_taken, from_one(NROT))
                pe.wait_ge(v_taken, from_one(2))

                def body(g, last):
                    for what, n in attention_order(last):
                        if what in ("project", "output"):
                            before = bank_before(last, (what, n))
                            if before is None or before[0] == "output":
                                pe.wait_ge(out_taken, from_one(g * NB + (before[1] + 1 if before else 0)))
                            elif before[1][1] < NROT:
                                pe.wait_ge(rot_taken, from_one(rotations(g, *before[1])))
                            else:
                                pe.wait_ge(v_taken, from_one(copies(g, *before[1])))
                        if what == "project":
                            if n == (0, 0):
                                pe.wait_ge(w_in, (g + 2) * 48)
                            project(pe, proj_bank, *n)
                        if what == "score":
                            k = n // QB
                            if n % QB == 0 and k % (NB // B) == 0:
                                pe.wait_ge(rotated, from_one(rotations(g, 1 if k < NB else 0, NROT - 1)))
                            pe.wait_ge(prob_ready, from_one(g * NS + (n - 1)))
                            score(pe, n)
                        if what == "turn":
                            k, j = n
                            m = TURNS.index(n)
                            if j == 0:
                                pe.wait_ge(prob_ready, from_one(g * NS + QB * (k + 1)))
                            pe.wait_ge(taken[m % 2], from_one(g * (NTURN // 2) + m // 2))
                            for c in range(skipped(k, j) // P, QB):
                                last_turn = pe.transpose(turn_bank[m % 2][:, c * P:(c + 1) * P], probs[:, k % 2, c, j * P:(j + 1) * P], t.identity[:, :])
                            last_turn.then_inc(turn_ready, 1)
                        if what == "use":
                            k, j = n
                            m = TURNS.index(n)
                            if j == 0:
                                pe.wait_ge(heads_ready, from_one(g * NB + k))
                                pe.wait_ge(v_taken, from_one(g * 4 + (2 if k < NB // B else 4)))
                            pe.wait_ge(taken[m % 2], from_one(g * (NTURN // 2) + (m // 2 + 1)))
                            pe.matmul(sum_bank[:, skipped(k, j):CH], v[:, BLOCKS[k][0], j, :], turned[:, m % SLOTS, skipped(k, j):CH],
                                      start=(j == 0), stop=(TURNED_BY[k] == m + 1)).then_inc(used, 1)
                        if what == "output":
                            pe.wait_ge(heads_ready, from_one(g * NB + (n + 1)))
                            if n == 0:
                                pe.wait_ge(wo_in, (g + 1) * 32)
                            for c in range(QB):
                                last_out = pe.matmul(proj_bank[:, c * P:(c + 1) * P], headsT[:, n % 2, c * P:(c + 1) * P],
                                                     w_o[:, BLOCKS[n][1], :], start=True, stop=True)
                            last_out.then_inc(out_ready, 1)

                each_head(pe, body)


def layer1_mixture(nc, t, d, out):
    pad = E1 + 8 - K1
    SIDE = LIMIT + 1.0
    ctx = ExitStack()
    with ctx:
        def sb(name, shape, dt=F32):
            return ctx.enter_context(nc.sbuf_tensor(name, shape, dt))

        def ps(name, shape, dt=F32):
            return ctx.enter_context(nc.psum_tensor(name, shape, dt))

        def sem(name):
            return ctx.enter_context(nc.semaphore(name))

        normed = sb("m1_normed", [P, NT, D])
        centred = sb("m1_centred", [P, NT, D])
        squares = sb("m1_squares", [P, NT, D])
        inT = sb("m1_inT", [P, T])
        stat = sb("m1_stat", [P, 5, NT])
        scale = sb("m1_scale", [P, D])
        gate_w, gate_b = sb("m1_gate_w", [P, E1]), sb("m1_gate_b", [P, E1])
        w1 = [sb(f"m1_w1_{i}", [P, F1]) for i in range(2)]
        w2 = [sb(f"m1_w2_{i}", [P, D]) for i in range(2)]
        b1 = sb("m1_b1", [P, E1])
        b2x3 = sb("m1_b2x3", [3 * E1, D])
        spread32 = sb("m1_spread32", [3 * E1, E1 * P])
        spread = [sb(f"m1_spread{i}", [3 * E1, P], BF16) for i in range(2)]
        padded = sb("m1_padded", [P, NT, pad])
        marked = sb("m1_marked", [P, NT, pad])
        top, wanted = sb("m1_top", [P, NT, 8]), sb("m1_wanted", [P, NT, 8])
        weight = sb("m1_weight", [P, NT, E1])
        rest = sb("m1_rest", [P, NT, E1])
        total = sb("m1_total", [P, 2, NT])
        parts = sb("m1_parts", [P, NT, 3, E1], BF16)
        weightT = sb("m1_weightT", [3 * E1, T], BF16)
        weightT32 = sb("m1_weightT32", [3 * E1, T])
        identity16 = sb("m1_identity16", [P, P], BF16)
        linear, sigm = sb("m1_linear", [P, 4, CH]), sb("m1_sigm", [P, 4, CH])
        gated, weighed = sb("m1_gated", [P, 4, CH]), sb("m1_weighed", [P, 4, CH])
        outT = sb("m1_outT", [P, T])
        hid_bank = [ps(f"m1_hid{i}", [P, CH]) for i in range(2)]
        wgt_bank = [ps(f"m1_wgt{i}", [P, CH]) for i in range(2)]
        sum_bank = [ps(f"m1_sum{i}", [P, CH]) for i in range(NCH)]
        gate_bank = hid_bank[0][:, 0:NT * E1].rearrange("p (t e) -> p t e", e=E1)

        w_in, dve_step, root_asked, root_given = sem("w_in"), sem("dve_step"), sem("root_asked"), sem("root_given")
        low_set, normed_ready, tr_ready, tr_out = sem("low_set"), sem("normed_ready"), sem("tr_ready"), sem("tr_out")
        gate_ready, exp_asked, exp_given, cast_ready = sem("gate_ready"), sem("exp_asked"), sem("exp_given"), sem("cast_ready")
        parts_ready, partT_ready, partT_out = sem("parts_ready"), sem("partT_ready"), sem("partT_out")
        expert_in = [sem(f"expert_in{i}") for i in range(2)]
        spread_ready = sem("spread_ready")
        hid_ready, linear_ready, sigm_ready, gated_ready = sem("hid_ready"), sem("linear_ready"), sem("sigm_ready"), sem("gated_ready")
        wgt_ready, weighed_ready, summed = sem("wgt_ready"), sem("weighed_ready"), sem("summed")
        sum_out, turn_ready, added, stored = sem("sum_out"), sem("turn_ready"), sem("added"), sem("stored")
        NW = 8
        N = 2 * NCH

        with nc.Block() as block:
            @block.sync
            def _(sp):
                def load(dst, src):
                    sp.dma_start(dst, src).then_inc(w_in, 16)

                def load_expert(e, par):
                    sp.dma_start(w1[par][:, :], d["L1_ffn_mlp1_w"][bass.ds(e * P, P), :]).then_inc(expert_in[par], 16)
                    sp.dma_start(w2[par][:, :], d["L1_ffn_mlp2_w"][bass.ds(e * P, P), :]).then_inc(expert_in[par], 16)

                load(scale[:, :], d["L1_ffn_scale"].partition_broadcast(P))
                load(gate_w[:, :], d["L1_ffn_gate_w"])
                load(gate_b[:, :], d["L1_ffn_gate_b"].partition_broadcast(P))
                load(b1[:, :], d["L1_ffn_mlp1_b"])
                for i in range(3):
                    load(b2x3[i * E1:(i + 1) * E1, :], d["L1_ffn_mlp2_b"])
                load(spread32[:, :], d["spread1"])
                for par in range(2):
                    load_expert(par, par)
                with sp.Fori(0, E1 // 2 - 1) as i:
                    for par in range(2):
                        sp.wait_ge(summed, i * N + (par + 1) * NCH)
                        load_expert(i * 2 + (par + 2), par)
                for c in range(NCH):
                    sp.wait_ge(added, c + 1)
                    b, first = c // (NCH // B), c % (NCH // B) * CH
                    sp.dma_start(out[b, first:first + CH, :].rearrange("(t p) d -> p t d", p=P), t.x[:, 4 * c:4 * c + 4, :]).then_inc(stored, 16)
                sp.wait_ge(stored, 16 * NCH)

            @block.gpsimd
            def _(pool):
                pool.memset(padded[:, :, E1:pad], LOW).then_inc(low_set, 1)
                pool.memset(wanted[:, :, K1:8], LOW).then_inc(low_set, 1)
                pool.tensor_copy(identity16[:, :], t.identity[:, :]).then_inc(cast_ready, 1)
                with pool.Fori(0, E1 // 2) as i:
                    for n in range(N):
                        pool.wait_ge(sigm_ready, i * N + (n + 1))
                        pool.wait_ge(weighed_ready, i * N + max(n - 3, 0))
                        pool.tensor_tensor(gated[:, n % 4, :], linear[:, n % 4, :], sigm[:, n % 4, :], ALU.mult).then_inc(gated_ready, 1)

            @block.vector
            def _(dve):
                chain = Chain(dve, dve_step)
                normalise(dve, chain, normed[:, :, :], t.x[:, :, :], (centred[:, :, :], squares[:, :, :]), stat, 1e-5,
                          root_asked, root_given, 0)
                chain.after(dve.tensor_tensor(t.x[:, :, :], t.x[:, :, :], normed[:, :, :], ALU.add))
                chain.after(dve.tensor_tensor(squares[:, :, :], normed[:, :, :], normed[:, :, :], ALU.mult))
                chain.after(dve.reduce_sum(stat[:, 1, :], squares[:, :, :], AX_X))
                dve.tensor_scalar(stat[:, 2, :], stat[:, 1, :], 1.0 / D, 1e-5, ALU.mult, ALU.add).then_inc(root_asked, 1)
                dve.wait_ge(root_given, 2)
                chain.after(dve.reciprocal(stat[:, 4, :], stat[:, 3, :]))
                chain.after(dve.tensor_tensor(centred[:, :, :], normed[:, :, :], over_features(stat[:, 4, :]), ALU.mult))
                dve.wait_ge(w_in, 16 * NW)
                dve.tensor_tensor(normed[:, :, :], centred[:, :, :], scale[:, :].unsqueeze(1).broadcast_to([P, NT, D]),
                                  ALU.mult).then_inc(normed_ready, 1)
                for c in range(NCH):
                    dve.wait_ge(tr_ready, c + 1)
                    dve.tensor_copy(inT[:, c * CH:(c + 1) * CH], sum_bank[c][:, :]).then_inc(tr_out, 1)
                dve.wait_ge(low_set, 2)
                dve.wait_ge(gate_ready, 1)
                chain.after(dve.tensor_tensor(padded[:, :, 0:E1], gate_bank, gate_b[:, :].unsqueeze(1).broadcast_to([P, NT, E1]), ALU.add))
                choose(dve, chain, padded, E1, K1, top, wanted, marked)
                dve.tensor_tensor(weight[:, :, :], padded[:, :, 0:E1], top[:, :, 0].unsqueeze(2).broadcast_to([P, NT, E1]),
                                  ALU.subtract).then_inc(exp_asked, 1)
                dve.wait_ge(exp_given, 1)
                chain.after(dve.tensor_tensor(weight[:, :, :], rest[:, :, :], marked[:, :, 0:E1], ALU.mult))
                chain.after(dve.reduce_sum(total[:, 0, :], weight[:, :, :], AX_X))
                chain.after(dve.reciprocal(total[:, 1, :], total[:, 0, :]))
                chain.after(dve.tensor_tensor(weight[:, :, :], weight[:, :, :],
                                              total[:, 1, :].unsqueeze(2).broadcast_to([P, NT, E1]), ALU.mult))
                split_weights(dve, chain, weight[:, :, :], parts, [rest[:, :, :]]).then_inc(parts_ready, 1)
                for c in range(NCH):
                    cols = slice(c * CH, (c + 1) * CH)
                    dve.wait_ge(partT_ready, c + 1)
                    chain.after(dve.tensor_copy(weightT[:, cols], wgt_bank[c % 2][0:3 * E1, 0:CH // 2].bitcast(BF16)))
                    dve.tensor_copy(weightT32[:, cols], weightT[:, cols]).then_inc(partT_out, 1)
                with dve.Fori(0, E1 // 2) as i:
                    dve.wait_ge(wgt_ready, i * N)
                    for par in range(2):
                        dve.tensor_scalar(spread[par][:, :], spread32[:, bass.ds(i * (2 * P) + par * P, P)], 1.0, None,
                                          ALU.mult).then_inc(spread_ready, 1)
                    for n in range(N + 1):
                        if n < N:
                            dve.wait_ge(hid_ready, i * N + (n + 1))
                            dve.wait_ge(gated_ready, i * N + max(n - 3, 0))
                            dve.tensor_scalar(linear[:, n % 4, :], hid_bank[n % 2][:, :], b1[:, bass.ds(i * 2 + n // NCH, 1)], LIMIT,
                                              ALU.add, ALU.min).then_inc(linear_ready, 1)
                        if n:
                            m = n - 1
                            dve.wait_ge(gated_ready, i * N + (m + 1))
                            dve.wait_ge(wgt_ready, i * N + (m + 1))
                            dve.wait_ge(summed, i * N + max(m - 3, 0))
                            dve.scalar_tensor_tensor(out=weighed[:, m % 4, :], in0=gated[:, m % 4, :], scalar=SIDE, in1=wgt_bank[m % 2][:, :],
                                                     op0=ALU.mult, op1=ALU.mult).then_inc(weighed_ready, 1)
                for c in range(NCH):
                    dve.wait_ge(summed, E1 * NCH - NCH + c + 1)
                    dve.tensor_copy(outT[:, c * CH:(c + 1) * CH], sum_bank[c][:, :]).then_inc(sum_out, 1)
                for c in range(NCH):
                    dve.wait_ge(turn_ready, c + 1)
                    xs = t.x[:, 4 * c:4 * c + 4, :]
                    dve.tensor_tensor(xs, (hid_bank + wgt_bank)[c][:, :].rearrange("p (t d) -> p t d", d=D), xs, ALU.add).then_inc(added, 1)

            @block.scalar
            def _(act):
                take_root(act, stat, root_asked, root_given, 0)
                take_root(act, stat, root_asked, root_given, 1)
                act.wait_ge(exp_asked, 1)
                act.activation(rest[:, :, :], weight[:, :, :], ACT.Exp).then_inc(exp_given, 1)
                with act.Fori(0, E1 // 2) as i:
                    for n in range(N):
                        act.wait_ge(linear_ready, i * N + (n + 1))
                        act.wait_ge(gated_ready, i * N + max(n - 3, 0))
                        act.activation(sigm[:, n % 4, :], linear[:, n % 4, :], ACT.Sigmoid, scale=ALPHA).then_inc(sigm_ready, 1)

            @block.tensor
            def _(pe):
                pe.wait_ge(normed_ready, 1)
                for c in range(NCH):
                    transpose_tiles(pe, sum_bank[c], normed, t.identity[:, :], c).then_inc(tr_ready, 1)
                pe.wait_ge(w_in, 16 * NW)
                pe.wait_ge(tr_out, NCH)
                for tile in range(NT):
                    last = pe.matmul(gate_bank[:, tile, :], inT[:, tile * P:(tile + 1) * P], gate_w[:, :], start=True, stop=True)
                last.then_inc(gate_ready, 1)
                pe.wait_ge(cast_ready, 1)
                pe.wait_ge(parts_ready, 1)
                for c in range(NCH):
                    if c >= 2:
                        pe.wait_ge(partT_out, c - 1)
                    half = wgt_bank[c % 2][0:3 * E1, 0:CH // 2].bitcast(BF16)
                    for k in range(4):
                        last = pe.transpose(half[:, k * P:(k + 1) * P], parts[:, 4 * c + k, :, :].rearrange("p a e -> p (a e)"), identity16[:, :])
                    last.then_inc(partT_ready, 1)
                pe.wait_ge(partT_out, NCH)
                for c in range(NCH):
                    pe.matmul(sum_bank[c][:, :], b2x3[:, :], weightT32[:, c * CH:(c + 1) * CH], start=True, stop=True)
                with pe.Fori(0, E1 // 2) as i:
                    def up(n):
                        par, c = divmod(n, NCH)
                        cols = slice(c * CH, (c + 1) * CH)
                        if c == 0:
                            pe.wait_ge(expert_in[par], (i + 1) * 32)
                            pe.wait_ge(spread_ready, i * 2 + 2)
                        pe.wait_ge(linear_ready, i * N + max(n - 1, 0))
                        pe.matmul(hid_bank[n % 2][:, :], w1[par][:, :], inT[:, cols], start=True, stop=True).then_inc(hid_ready, 1)
                        pe.wait_ge(weighed_ready, i * N + max(n - 1, 0))
                        pe.matmul(wgt_bank[n % 2][:, :], spread[par][:, :], weightT[:, cols], start=True, stop=True).then_inc(wgt_ready, 1)

                    up(0)
                    up(1)
                    for n in range(N):
                        if n + 2 < N:
                            up(n + 2)
                        par, c = divmod(n, NCH)
                        pe.wait_ge(weighed_ready, i * N + (n + 1))
                        pe.matmul(sum_bank[c][:, :], w2[par][:, :], weighed[:, n % 4, :], start=False, stop=True,
                                  skip_group_check=True).then_inc(summed, 1)
                for c in range(NCH):
                    pe.wait_ge(sum_out, c + 1)
                    for k in range(4):
                        last = pe.transpose((hid_bank + wgt_bank)[c][:, k * P:(k + 1) * P], outT[:, (4 * c + k) * P:(4 * c + k + 1) * P],
                                            t.identity[:, :])
                    last.then_inc(turn_ready, 1)


def two_layers(nc, d, out):
    t = Tensors()
    ctx = ExitStack()
    with ctx:
        def sb(name, shape, dt=F32):
            return ctx.enter_context(nc.sbuf_tensor(name, shape, dt))

        t.x = sb("x", [P, NT, D])
        t.identity = sb("identity", [P, P])
        t.mask32 = sb("mask32", [P, P])
        t.seen = sb("seen", [P, P])
        t.rope = sb("rope", [P, 4, S])
        t.values0 = sb("values0", [P, B * H0 * TB * HD0])
        t.attn0 = sb("attn0", [P, B * H0 * TB * HD0])
        t.parts_dram = [nc.dram_tensor(f"{name}_parts", (3, B * P, S), BF16, kind="Internal").ap() for name in ("q", "k")]
        layer0_project(nc, t, d)
        layer0_attention(nc, t)
        layer0_mixture(nc, t, d)
        layer1_attention(nc, t, d)
        layer1_mixture(nc, t, d, out)


def shape_constants():
    import numpy as np
    f32 = np.float32
    half = (np.arange(0, D1, 2, dtype=f32) / f32(D1)).astype(f32)
    inverse_frequency = (f32(1.0) / np.power(f32(10000.0), half)).astype(f32)
    angle = np.outer(np.arange(S, dtype=f32), inverse_frequency).astype(f32)
    cos, sin = np.cos(angle).T, np.sin(angle).T
    cos, sin = np.concatenate([cos, cos]), np.concatenate([-sin, sin])
    scale = f32(1.0) / np.sqrt(f32(D1))
    rope = np.stack([cos * scale, sin * scale, cos, sin]).astype(f32)
    spread0 = np.zeros((3, E0, E0 * F0 // P, P), f32)
    for e in range(E0):
        m, side = divmod(e, 2)
        spread0[:, e, m, side * F0:(side + 1) * F0] = 1.0
    spread1 = np.zeros((3, E1, E1, P), f32)
    for e in range(E1):
        spread1[:, e, e, :] = 1.0
    later = np.triu(np.ones((P, P), bool), 1)
    return {"identity": np.eye(P, dtype=f32), "mask": np.where(later, f32(LOW), f32(0.0)).astype(f32),
            "seen": np.triu(np.ones((P, P), f32)), "rope": rope,
            "spread0": spread0.reshape(3 * E0, -1, P), "spread1": spread1.reshape(3 * E1, -1)}


def kernel(**inputs):
    import numpy as np
    import concourse.bacc as bacc
    from concourse import mybir as my
    from concourse.bass_utils import run_bass_kernel_spmd as run

    arrays = {name: np.asarray(a) for name, a in inputs.items()}
    arrays["L1_ffn_gate_w"] = arrays["L1_ffn_gate_w"].T
    arrays["L1_ffn_mlp1_w"] = arrays["L1_ffn_mlp1_w"][:, ::2, :].transpose(0, 2, 1).reshape(E1 * P, F1)
    arrays["L1_ffn_mlp1_b"] = arrays["L1_ffn_mlp1_b"][:, ::2].T
    arrays["L1_ffn_mlp2_w"] = arrays["L1_ffn_mlp2_w"].transpose(0, 2, 1).reshape(E1 * F1, D)
    arrays["L0_ffn_b1"] = arrays["L0_ffn_b1"].reshape(E0 * F0 // P, P).T
    arrays["L0_ffn_bs1"] = arrays["L0_ffn_bs1"].reshape(F0, 1)
    arrays["L0_ffn_bs2"] = arrays["L0_ffn_bs2"].reshape(D, 1)
    arrays["L0_ffn_route_scale"] = arrays["L0_ffn_route_scale"].reshape(1)
    arrays.update(shape_constants())

    nc = bacc.Bacc("TRN2", target_bir_lowering=False, num_devices=1)
    given, d = {}, {}
    for name, a in arrays.items():
        a = np.ascontiguousarray(a)
        given[f"in_{name}"] = a
        d[name] = nc.dram_tensor(f"in_{name}", a.shape, my.dt.from_np(a.dtype), kind="ExternalInput").ap()
    out = nc.dram_tensor("out_0", (B, S, D), F32, kind="ExternalOutput").ap()
    two_layers(nc, d, out)
    r = run(nc, [given], core_ids=[0])
    return r.results[0]["out_0"]
```

```python
from contextlib import ExitStack

import concourse.bass as bass
from concourse import mybir

F32 = mybir.dt.float32
BF16 = mybir.dt.bfloat16
ALU = mybir.AluOpType
ACT = mybir.ActivationFunctionType
AX_X = mybir.AxisListType.X

P = 128
B, S, D = 2, 1024, 128
T = B * S
NT = T // P
TB = S // P
CH = 512
NCH = T // CH

H0, HD0 = 16, 8
NPAIR = B * H0 // 2
NST = 6 * HD0
SHIFTS = 2 * NST
VW = 32

H1, KV1, D1 = 8, 4, 128
GQ = H1 // KV1

E0, K0, F0 = 8, 2, 64
E1, K1, F1 = 16, 4, 128
ALPHA, LIMIT = 1.702, 7.0
LOW, HIGH = -3.0e38, 3.0e38
SCALE0 = 1.0 / 128.0 ** 0.5


def wait_from(engine, sem, count):
    if not isinstance(count, int) or count > 0:
        engine.wait_ge(sem, count)


class Tensors:
    pass


class Chain:

    def __init__(self, engine, sem):
        self.engine, self.sem, self.n = engine, sem, 0

    def after(self, instruction):
        self.n += 1
        instruction.then_inc(self.sem, 1)
        self.engine.wait_ge(self.sem, self.n)


class Moments:

    def __init__(self, sb, name):
        self.raw = sb(f"{name}_raw", [P, NT, 6])
        self.both = sb(f"{name}_both", [P, NT, 2])
        self.of_root = sb(f"{name}_of_root", [P, NT])
        self.root = sb(f"{name}_root", [P, NT])
        self.inverse = sb(f"{name}_inverse", [P, NT])
        self.mean, self.variance = self.both[:, :, 0], self.both[:, :, 1]


def find_moments(dve, chain, src, moments):
    for tile in range(NT):
        last = dve.bn_stats(moments.raw[:, tile, :], src[:, tile, :])
    chain.after(last)
    for tile in range(NT):
        last = dve.bn_aggr(moments.both[:, tile, :], moments.raw[:, tile, :])
    chain.after(last)


def normalise(dve, chain, dst, src, moments, eps, root_asked, root_given, turn, ready=None):
    find_moments(dve, chain, src, moments)
    dve.tensor_scalar(moments.of_root[:, :], moments.variance, eps, None, ALU.add).then_inc(root_asked, 1)
    dve.wait_ge(root_given, turn + 1)
    chain.after(dve.reciprocal(moments.inverse[:, :], moments.root[:, :]))
    for tile in range(NT):
        last = dve.tensor_scalar(dst[:, tile, :], src[:, tile, :], moments.both[:, tile, 0:1], moments.inverse[:, tile:tile + 1],
                                 ALU.subtract, ALU.mult)
        if ready is not None and tile % 4 == 3:
            last.then_inc(ready, 1)
    if ready is None:
        chain.after(last)


def take_root(act, moments, root_asked, root_given, turn):
    act.wait_ge(root_asked, turn + 1)
    act.activation(moments.root[:, :], moments.of_root[:, :], ACT.Sqrt).then_inc(root_given, 1)


def transpose_tiles(pe, dst_bank, src, identity, chunk):
    for c in range(CH // P):
        last = pe.transpose(dst_bank[:, c * P:(c + 1) * P], src[:, chunk * (CH // P) + c, :], identity)
    return last


STACKS = 4


def load_pair(sp, t, pair, stack, loaded):
    q_dram, k_dram = t.parts_dram
    for x in range(2):
        head = bass.ds(pair * (2 * HD0) + x * HD0, HD0)
        first = x * NST
        for part in range(3):
            rows = slice(first, first + (3 - part) * HD0)
            first += (3 - part) * HD0
            sp.dma_start(t.q_stack[stack][rows, :], q_dram[part, head, :].unsqueeze(0).broadcast_to([3 - part, HD0, S])).then_inc(loaded, 16)
            sp.dma_start(t.k_stack[stack][x][rows, :], k_dram[0:3 - part, head, :]).then_inc(loaded, 16)


def layer0_project(nc, t, d):
    ctx = ExitStack()
    with ctx:
        def sb(name, shape, dt=F32):
            return ctx.enter_context(nc.sbuf_tensor(name, shape, dt))

        def sem(name):
            return ctx.enter_context(nc.semaphore(name))

        normedT = sb("l0_normedT", [P, T])
        moments = Moments(sb, "l0_token")
        first_inverse = sb("l0_first_inverse", [P, NT])
        w_qkv = sb("l0_w_qkv", [P, 3, D])
        affineT = sb("l0_affineT", [P, 2])
        parts = [sb("l0_q_parts", [P, 3, T], BF16), sb("l0_k_parts", [P, 3, T], BF16)]
        rest = sb("l0_rest", [P, 4, CH])
        tr_bank = [ctx.enter_context(nc.psum_tensor(f"l0_tr{i}", [P, CH], F32)) for i in range(4)]
        banks = [ctx.enter_context(nc.psum_tensor(f"l0_bank{i}", [P, CH], F32)) for i in range(4)]

        x_in, w_in = sem("x_in"), sem("w_in")
        dve_step, root_asked, root_given = sem("dve_step"), sem("root_asked"), sem("root_given")
        normed_ready, tr_ready, tr_out = sem("normed_ready"), sem("tr_ready"), sem("tr_out")
        qk_ready, hi_ready, rest_ready = sem("qk_ready"), sem("hi_ready"), sem("rest_ready")
        mid_ready, lo_ready = sem("mid_ready"), sem("lo_ready")
        v_ready, v_out, pair_in = sem("v_ready"), sem("v_out"), sem("pair_in")
        parts_out = [sem(f"parts_out{b}") for b in range(B)]
        consts_in, zeros_set = sem("consts_in"), sem("zeros_set")
        NW = 8

        with nc.Block() as block:
            def send_parts(engine, b):
                for which in range(2):
                    engine.wait_ge(lo_ready, (2 * b + which + 1) * (NCH // B))
                    engine.dma_start(t.parts_dram[which][:, b * P:(b + 1) * P, :].rearrange("a r s -> r a s"),
                                     parts[which][:, :, b * S:(b + 1) * S]).then_inc(parts_out[b], 16)

            @block.sync
            def _(sp):
                sp.dma_start(t.x[:, :, :], d["L0_attn_x"].rearrange("b (t p) d -> p (b t) d", p=P)).then_inc(x_in, 16)
                sp.dma_start(t.identity[:, :], d["identity"]).then_inc(w_in, 16)
                for i, name in enumerate(("L0_attn_ln_scale", "L0_attn_ln_bias")):
                    sp.dma_start(affineT[:, i:i + 1], d[name].rearrange("(p a) -> p a", a=1)).then_inc(w_in, 16)
                    sp.dma_start(t.affine0[:, i, :], d[name].partition_broadcast(P)).then_inc(w_in, 16)
                for i, name in enumerate(("L0_attn_wq", "L0_attn_wk", "L0_attn_wv")):
                    sp.dma_start(w_qkv[:, i, :], d[name]).then_inc(w_in, 16)
                send_parts(sp, 0)
                sp.wait_ge(parts_out[0], 16 * 2)
                sp.wait_ge(zeros_set, 2 * STACKS)
                load_pair(sp, t, 0, 0, pair_in)
                sp.wait_ge(pair_in, 12 * 16)
                sp.wait_ge(parts_out[1], 16 * 2)

            def unit(u):
                b, which, half = u // NCH, u // (NCH // B) % 2, u % (NCH // B)
                c = b * (NCH // B) + half
                return which, c, slice(c * CH, (c + 1) * CH)

            @block.gpsimd
            def _(pool):
                pool.dma_start(t.rope[:, :, :], d["rope"].rearrange("a p s -> p a s")).then_inc(consts_in, 16)
                for stack in t.k_stack:
                    for x in range(2):
                        pool.memset(stack[x][0:SHIFTS, :], 0.0).then_inc(zeros_set, 1)
                pool.wait_ge(zeros_set, 2 * STACKS)
                for u in range(2 * NCH):
                    which, c, cols = unit(u)
                    pool.wait_ge(mid_ready, u + 1)
                    pool.tensor_tensor(parts[which][:, 2, cols], rest[:, u % 4, :], parts[which][:, 1, cols],
                                       ALU.subtract).then_inc(lo_ready, 1)
                pool.wait_ge(consts_in, 16)

            @block.vector
            def _(dve):
                chain = Chain(dve, dve_step)
                dve.wait_ge(x_in, 16)
                find_moments(dve, chain, t.x, moments)
                dve.tensor_scalar(moments.of_root[:, :], moments.variance, 1e-5, None, ALU.add).then_inc(root_asked, 1)
                dve.wait_ge(root_given, 1)
                chain.after(dve.reciprocal(first_inverse[:, :], moments.root[:, :]))
                chain.after(dve.tensor_tensor(moments.of_root[:, :], first_inverse[:, :], first_inverse[:, :], ALU.mult))
                chain.after(dve.tensor_tensor(moments.of_root[:, :], moments.of_root[:, :], moments.variance, ALU.mult))
                chain.after(dve.tensor_scalar(moments.of_root[:, :], moments.of_root[:, :], 1e-6, None, ALU.add))
                dve.engine_nop().then_inc(root_asked, 1)
                dve.wait_ge(root_given, 2)
                chain.after(dve.reciprocal(moments.inverse[:, :], moments.root[:, :]))
                chain.after(dve.tensor_tensor(moments.inverse[:, :], moments.inverse[:, :], first_inverse[:, :], ALU.mult))
                for tile in range(NT):
                    last = dve.tensor_scalar(t.normed0[:, tile, :], t.x[:, tile, :], moments.both[:, tile, 0:1],
                                             moments.inverse[:, tile:tile + 1], ALU.subtract, ALU.mult)
                    if tile % 4 == 3:
                        last.then_inc(normed_ready, 1)
                for u in range(2 * NCH):
                    which, c, cols = unit(u)
                    dve.wait_ge(hi_ready, u + 1)
                    if u >= 4:
                        dve.wait_ge(lo_ready, u - 3)
                    dve.tensor_tensor(rest[:, u % 4, :], banks[u % 4][:, :], parts[which][:, 0, cols],
                                      ALU.subtract).then_inc(rest_ready, 1)
                for c in range(NCH):
                    b, first = c // (NCH // B), c % (NCH // B) * 4
                    dve.wait_ge(v_ready, c + 1)
                    dst = t.values0[:, b * H0 * S // P * HD0:(b + 1) * H0 * S // P * HD0].rearrange(
                        "p (h t w) -> p t h w", h=H0, w=HD0)[:, first:first + 4, :, :]
                    dve.tensor_copy(dst, tr_bank[c][:, :].rearrange("p (t h w) -> p t h w", t=4, w=HD0)).then_inc(v_out, 1)

            @block.scalar
            def _(act):
                take_root(act, moments, root_asked, root_given, 0)
                take_root(act, moments, root_asked, root_given, 1)
                act.wait_ge(w_in, 16 * NW)
                for c in range(NCH):
                    act.wait_ge(tr_ready, c + 1)
                    act.activation(normedT[:, c * CH:(c + 1) * CH], tr_bank[c][:, :], ACT.Identity, scale=affineT[:, 0:1],
                                   bias=affineT[:, 1:2]).then_inc(tr_out, 1)

                def split(u):
                    which, c, cols = unit(u)
                    act.wait_ge(rest_ready, u + 1)
                    act.activation(parts[which][:, 1, cols], rest[:, u % 4, :], ACT.Copy).then_inc(mid_ready, 1)

                for u in range(2 * NCH):
                    which, c, cols = unit(u)
                    act.wait_ge(qk_ready, u + 1)
                    act.activation(parts[which][:, 0, cols], banks[u % 4][:, :], ACT.Copy).then_inc(hi_ready, 1)
                    if u >= 1:
                        split(u - 1)
                split(2 * NCH - 1)
                send_parts(act, 1)

            @block.tensor
            def _(pe):
                pe.wait_ge(w_in, 16 * NW)
                for c in range(NCH):
                    pe.wait_ge(normed_ready, c + 1)
                    transpose_tiles(pe, tr_bank[c], t.normed0, t.identity[:, :], c).then_inc(tr_ready, 1)
                for u in range(2 * NCH):
                    which, c, cols = unit(u)
                    pe.wait_ge(tr_out, c + 1)
                    if u >= 4:
                        pe.wait_ge(rest_ready, u - 3)
                    pe.matmul(banks[u % 4][:, :], w_qkv[:, which, :], normedT[:, cols], start=True, stop=True).then_inc(qk_ready, 1)
                for c in range(NCH):
                    for k in range(4):
                        tile = 4 * c + k
                        last = pe.matmul(tr_bank[c][:, k * P:(k + 1) * P], normedT[:, tile * P:(tile + 1) * P],
                                         w_qkv[:, 2, :], start=True, stop=True)
                    last.then_inc(v_ready, 1)


MAX_LEAD = 22
PROB_STEPS = 4


def layer0_attention(nc, t):
    assert 20 <= MAX_LEAD <= 26 and MAX_LEAD % 2 == 0
    TILES = 2 * TB
    TURN_AT = (2 * TILES - MAX_LEAD) // 2 + 1
    ctx = ExitStack()
    with ctx:
        def sb(name, shape, dt=F32):
            return ctx.enter_context(nc.sbuf_tensor(name, shape, dt))

        def ps(name, shape):
            return ctx.enter_context(nc.psum_tensor(name, shape, F32))

        def sem(name):
            return ctx.enter_context(nc.semaphore(name))

        q_stack, k_stack = t.q_stack, t.k_stack
        v_tile = [sb(f"v_tile{i}", [P, 2, TB, VW]) for i in range(2)]
        probs = sb("probs", [P, PROB_STEPS, 4, CH])
        heads = [sb(f"heads{i}", [P, CH]) for i in range(2)]
        inverse = sb("inverse", [P, 2, P // 8])
        maxima = sb("maxima", [P, 2, TILES])
        shift = sb("shift", [TILES, 2, P], BF16)
        score_bank = [ps(f"score_bank{i}", [P, CH]) for i in range(2)]
        max_bank = [ps(f"max_bank{i}", [P, S]) for i in range(2)]
        summed = ps("summed", [P, CH])
        turned = ps("turned", [P, CH])

        loaded = [sem(f"loaded{i}") for i in range(STACKS)]
        shift_in = [sem(f"shift_in{i}") for i in range(STACKS)]
        staged, ones_set = sem("staged"), sem("ones_set")
        rows_set, residual_step = sem("rows_set"), sem("residual_step")
        score_ready, prob_ready, used = sem("score_ready"), sem("prob_ready"), sem("used")
        plain_ready, max_ready = sem("plain_ready"), sem("max_ready")
        maxT_ready, high_ready, shift_ready = sem("maxT_ready"), sem("high_ready"), sem("shift_ready")
        heads_ready, turned_ready = sem("heads_ready"), sem("turned_ready")
        inverse_ready, written = sem("inverse_ready"), sem("written")

        def each_pair(engine, body):
            body(0, 0)
            with engine.Fori(0, NPAIR // 4 - 1) as g:
                for s in range(1, 5):
                    body(g, s)
            for s in range(1, 4):
                body(NPAIR // 4 - 1, s)

        def ahead(g, s, n):
            return not isinstance(g, int) or 4 * g + s + n < NPAIR

        def first(g, s):
            return isinstance(g, int) and 4 * g + s == 0

        def searched_at(k):
            return [divmod(MAX_LEAD + 2 * k + i, TILES) for i in range(2)]

        with nc.Block() as block:
            @block.sync
            def _(sp):
                def subtract(stack):
                    for part in range(2):
                        row = SHIFTS + 2 * part
                        sp.dma_start(q_stack[stack][row:row + 2, :], shift[:, part, :]).then_inc(shift_in[stack], 16)

                for pair in range(1, 3):
                    load_pair(sp, t, pair, pair, loaded[pair])
                sp.wait_ge(shift_ready, 1)
                subtract(0)

                def body(g, s):
                    if ahead(g, s, 1):
                        sp.wait_ge(shift_ready, g * 4 + (s + 2))
                        subtract((s + 1) % STACKS)
                    if ahead(g, s, 3):
                        if not first(g, s):
                            sp.wait_ge(score_ready, g * (4 * 32) + s * 32)
                        load_pair(sp, t, g * 4 + (s + 3), (s + 3) % STACKS, loaded[(s + 3) % STACKS])

                each_pair(sp, body)

            @block.gpsimd
            def _(pool):
                for i in range(2):
                    pool.memset(v_tile[i][:, :, :, :], 0.0).then_inc(ones_set, 1)
                pool.wait_ge(ones_set, 2)
                for i in range(2):
                    pool.memset(v_tile[i][:, :, :, HD0:HD0 + 1], 1.0).then_inc(ones_set, 1)
                pool.wait_ge(ones_set, 4)
                for i in range(STACKS):
                    for x in range(2):
                        own = [t.identity[SHIFTS:P, SHIFTS + 2 * part + x:SHIFTS + 2 * part + x + 1].broadcast_to([P - SHIFTS, S])
                               for part in range(2)]
                        pool.tensor_tensor(k_stack[i][x][SHIFTS:P, :], own[0], own[1], ALU.add).then_inc(rows_set, 1)
                pool.wait_ge(rows_set, 2 * STACKS)
                scale, bias = (t.affine0[:, i, :].unsqueeze(1).broadcast_to([P, NT, D]) for i in range(2))
                pool.tensor_tensor(t.normed0[:, :, :], t.normed0[:, :, :], scale, ALU.mult).then_inc(residual_step, 1)
                pool.wait_ge(residual_step, 1)
                pool.tensor_tensor(t.normed0[:, :, :], t.normed0[:, :, :], bias, ALU.add).then_inc(residual_step, 1)
                pool.wait_ge(residual_step, 2)
                pool.tensor_tensor(t.x[:, :, :], t.x[:, :, :], t.normed0[:, :, :], ALU.add).then_inc(residual_step, 1)

            @block.vector
            def _(dve):
                def search(g, s, away, n):
                    m = (s + away) * TILES + n
                    dve.wait_ge(plain_ready, g * (4 * TILES) + (m + 1))
                    dve.reduce_max(maxima[:, (s + away) % 2, n:n + 1], max_bank[n % 2][:, :], AX_X).then_inc(max_ready, 1)

                def split(g, s):
                    dve.wait_ge(maxT_ready, g * 4 + (s + 1))
                    if not first(g, s):
                        dve.wait_ge(shift_in[(s - 1) % STACKS], g * 32 + ((s - 1) // STACKS + 1) * 32)
                    mT = turned[0:TILES, 0:P]
                    dve.tensor_scalar(shift[:, 0, :], mT, -1.0, None, ALU.mult).then_inc(high_ready, 1)
                    dve.wait_ge(high_ready, g * 4 + (s + 1))
                    dve.scalar_tensor_tensor(out=shift[:, 1, :], in0=mT, scalar=-1.0, in1=shift[:, 0, :],
                                             op0=ALU.mult, op1=ALU.subtract).then_inc(shift_ready, 1)

                def stage(g, s):
                    for x in range(2):
                        src = t.values0[:, bass.ds(g * (8 * TB * HD0) + (2 * s + x) * TB * HD0, TB * HD0)]
                        dve.tensor_scalar(v_tile[s % 2][:, x, :, 0:HD0], src.rearrange("p (t w) -> p t w", w=HD0), 1.0, None,
                                          ALU.mult).then_inc(staged, 1)

                def divide(g, s):
                    dve.wait_ge(turned_ready, g * 4 + (s + 1))
                    tv = turned[:, :].rearrange("p (c h w) -> p c h w", c=4, w=VW)
                    inv = inverse[:, s % 2, :].rearrange("p (c h) -> p c h", c=4)
                    dve.reciprocal(inv, tv[:, :, :, HD0]).then_inc(inverse_ready, 1)
                    dve.wait_ge(inverse_ready, g * 4 + (s + 1))
                    dst = t.attn0[:, bass.ds(g * (4 * P) + s * P, P)].rearrange("p (h c w) -> p c h w", h=4, w=HD0)
                    dve.tensor_tensor(dst, tv[:, :, :, 0:HD0], inv.unsqueeze(3).broadcast_to([P, 4, 4, HD0]),
                                      ALU.mult).then_inc(written, 1)

                dve.wait_ge(ones_set, 4)
                stage(0, 0)
                for m in range(MAX_LEAD):
                    if m == TILES + 2:
                        split(0, 0)
                    search(0, 0, *divmod(m, TILES))

                def body(g, s):
                    for k in range(TB):
                        if k == TURN_AT and ahead(g, s, 1):
                            split(g, s + 1)
                        for away, n in searched_at(k):
                            if ahead(g, s, away):
                                search(g, s, away, n)
                        if k == 3 and not first(g, s):
                            divide(g, s - 1)
                        if k == TB - 1 and ahead(g, s, 1):
                            if not first(g, s):
                                dve.wait_ge(used, g * (4 * TB) + s * TB)
                            stage(g, s + 1)

                each_pair(dve, body)
                divide(NPAIR // 4 - 1, 3)

            @block.scalar
            def _(act):
                def take(g, s):
                    act.wait_ge(used, g * (4 * TB) + (s + 1) * TB)
                    act.activation(heads[s % 2][:, :], summed[:, :], ACT.Copy).then_inc(heads_ready, 1)

                def body(g, s):
                    for k in range(TB):
                        for j in range(4):
                            act.wait_ge(score_ready, g * (4 * 32) + (s * 32 + 4 * k + j + 1))
                            if j == 0 and (k >= PROB_STEPS or not first(g, s)):
                                act.wait_ge(used, g * (4 * TB) + (s * TB + k - PROB_STEPS + 1))
                            act.activation(probs[:, k % PROB_STEPS, j, :], score_bank[j % 2][:, :], ACT.Exp, scale=SCALE0).then_inc(prob_ready, 1)
                            if k == 0 and j == 1 and not first(g, s):
                                take(g, s - 1)

                each_pair(act, body)
                take(NPAIR // 4 - 1, 3)

            @block.tensor
            def _(pe):
                def search(g, s, away, n):
                    m = (s + away) * TILES + n
                    x, qt = divmod(n, TB)
                    stack = (s + away) % STACKS
                    if n == 0:
                        turn = (s + away) // STACKS + (1 if stack else 0)
                        wait_from(pe, loaded[stack], g * (12 * 16) + turn * (12 * 16))
                    if m >= 2:
                        pe.wait_ge(max_ready, g * (4 * TILES) + (m - 1))
                    for half in range(2):
                        last = pe.matmul(max_bank[n % 2][:, half * CH:(half + 1) * CH], q_stack[stack][0:SHIFTS, qt * P:(qt + 1) * P],
                                         k_stack[stack][x][0:SHIFTS, half * CH:(half + 1) * CH], start=True, stop=True)
                    last.then_inc(plain_ready, 1)

                def turn_maxima(g, s):
                    pe.wait_ge(max_ready, g * (4 * TILES) + (s + 1) * TILES)
                    if 4 * (g if isinstance(g, int) else 1) + s >= 2:
                        pe.wait_ge(written, g * 4 + (s - 1))
                    pe.transpose(turned[0:TILES, 0:P], maxima[:, s % 2, :], t.identity[:, :]).then_inc(maxT_ready, 1)

                def turn_heads(g, s):
                    pe.wait_ge(heads_ready, g * 4 + (s + 1))
                    if ahead(g, s, 1):
                        pe.wait_ge(shift_ready, g * 4 + (s + 2))
                    else:
                        pe.wait_ge(written, g * 4 + s)
                    for c in range(4):
                        last = pe.transpose(turned[:, c * P:(c + 1) * P], heads[s % 2][:, c * P:(c + 1) * P], t.identity[:, :])
                    last.then_inc(turned_ready, 1)

                def score(g, s, k, j):
                    x, half = divmod(j, 2)
                    rows, e = slice(0, SHIFTS + 4), s * 32 + 4 * k + j
                    if (k, j) == (0, 0):
                        if isinstance(g, int) and g == 0:
                            pe.wait_ge(rows_set, 2)
                        elif s <= STACKS - 1 and not isinstance(g, int):
                            pe.wait_ge(rows_set, 2 * (s + 1))
                        pe.wait_ge(shift_in[s % STACKS], g * 32 + (s // STACKS + 1) * 32)
                    if not isinstance(g, int) or 32 * 4 * g + e >= 2:
                        pe.wait_ge(prob_ready, g * (4 * 32) + (e - 1))
                    pe.matmul(score_bank[j % 2][:, :], k_stack[s % STACKS][x][rows, k * P:(k + 1) * P],
                              q_stack[s % STACKS][rows, half * CH:(half + 1) * CH], start=True, stop=True).then_inc(score_ready, 1)

                def use(g, s, k):
                    if k == 0:
                        pe.wait_ge(staged, g * 8 + (2 * s + 2))
                        if not first(g, s):
                            pe.wait_ge(heads_ready, g * 4 + s)
                    pe.wait_ge(prob_ready, g * (4 * 32) + (s * 32 + 4 * k + 4))
                    for j in range(4):
                        last = pe.matmul(summed[VW * j:VW * (j + 1), :], v_tile[s % 2][:, j // 2, k, :], probs[:, k % PROB_STEPS, j, :],
                                         start=(k == 0), stop=(k == TB - 1), tile_position=(0, VW * j))
                    last.then_inc(used, 1)

                for m in range(MAX_LEAD):
                    if m == TILES + 2:
                        turn_maxima(0, 0)
                    search(0, 0, *divmod(m, TILES))

                def body(g, s):
                    for k in range(TB):
                        tiles = [tile for tile in searched_at(k) if ahead(g, s, tile[0])]
                        for j in range(2):
                            score(g, s, k, j)
                        if first(g, s) and k == 0:
                            search(g, s, *tiles.pop(0))
                        if k > 0:
                            use(g, s, k - 1)
                        elif not first(g, s):
                            use(g, s - 1, TB - 1)
                        if k == 2 and not first(g, s):
                            turn_heads(g, s - 1)
                        if k == TURN_AT and ahead(g, s, 1):
                            turn_maxima(g, s + 1)
                        for j in range(2, 4):
                            score(g, s, k, j)
                        for tile in tiles:
                            search(g, s, *tile)

                each_pair(pe, body)
                use(NPAIR // 4 - 1, 3, TB - 1)
                turn_heads(NPAIR // 4 - 1, 3)


def choose(dve, chain, padded, experts, chosen, top, wanted, marked):
    for tile in range(NT):
        last = dve.max(out=top[:, tile, :], in_=padded[:, tile, 0:experts])
    chain.after(last)
    chain.after(dve.tensor_copy(wanted[:, :, 0:chosen], top[:, :, 0:chosen]))
    for tile in range(NT):
        last = dve.match_replace(out=marked[:, tile, :], in_to_replace=wanted[:, tile, :],
                                 in_values=padded[:, tile, :], imm_value=HIGH)
    chain.after(last)
    chain.after(dve.tensor_scalar(marked[:, :, 0:experts], marked[:, :, 0:experts], HIGH, None, ALU.is_equal))


def split_weights(dve, chain, weight, parts, rest):
    chain.after(dve.tensor_copy(parts[:, :, 0, :], weight))
    chain.after(dve.tensor_tensor(rest[0], weight, parts[:, :, 0, :], ALU.subtract))
    chain.after(dve.tensor_copy(parts[:, :, 1, :], rest[0]))
    return dve.tensor_tensor(parts[:, :, 2, :], rest[0], parts[:, :, 1, :], ALU.subtract)


def layer0_mixture(nc, t, d):
    NP0 = E0 * F0 // P
    NU = NP0 + 1
    pad = E0 + 8 - K0
    ctx = ExitStack()
    with ctx:
        def sb(name, shape, dt=F32):
            return ctx.enter_context(nc.sbuf_tensor(name, shape, dt))

        def ps(name, shape, dt=F32):
            return ctx.enter_context(nc.psum_tensor(name, shape, dt))

        def sem(name):
            return ctx.enter_context(nc.semaphore(name))

        normed = sb("m0_normed", [P, NT, D])
        inT = sb("m0_inT", [P, T])
        moments = Moments(sb, "m0_token")
        gate_w = sb("m0_gate_w", [P, E0])
        route = sb("m0_route", [P, 1])
        w1 = sb("m0_w1", [P, NP0, 2, F0])
        ws1 = sb("m0_ws1", [P, P])
        w2 = sb("m0_w2", [P, NP0, D])
        ws2 = sb("m0_ws2", [P, D])
        b1 = sb("m0_b1", [P, NU])
        b2x3 = sb("m0_b2x3", [3 * E0, D])
        bs2 = sb("m0_bs2", [P, 1])
        spread32 = sb("m0_spread32", [3 * E0, NP0, P])
        spread = sb("m0_spread", [3 * E0, NP0, P], BF16)
        padded = sb("m0_padded", [P, NT, pad])
        marked = sb("m0_marked", [P, NT, pad])
        top, wanted = sb("m0_top", [P, NT, 8]), sb("m0_wanted", [P, NT, 8])
        weight = sb("m0_weight", [P, NT, E0])
        rest = sb("m0_rest", [P, NT, E0])
        total = sb("m0_total", [P, 2, NT])
        parts = sb("m0_parts", [P, NT, 3, E0], BF16)
        weightT = sb("m0_weightT", [3 * E0, T], BF16)
        weightT32 = sb("m0_weightT32", [3 * E0, T])
        hidden = sb("m0_hidden", [P, NU, CH])
        weighed = sb("m0_weighed", [P, NP0, CH])
        outT = sb("m0_outT", [P, CH])
        identity16 = sb("m0_identity16", [P, P], BF16)
        hid_bank = [ps(f"m0_hid{i}", [P, CH]) for i in range(2)]
        wgt_bank = [ps(f"m0_wgt{i}", [P, CH]) for i in range(2)]
        sum_bank, turn_bank = ps("m0_sum", [P, CH]), ps("m0_turn", [P, NT // 4, D])
        gate_bank = ps("m0_gate", [P, NT, E0])
        part_bank = ps("m0_part", [3 * E0, CH], BF16)

        w_in, dve_step, root_asked, root_given = sem("w_in"), sem("dve_step"), sem("root_asked"), sem("root_given")
        low_set, normed_ready, tr_ready, tr_out = sem("low_set"), sem("normed_ready"), sem("tr_ready"), sem("tr_out")
        gate_ready, prob_ready, cast_ready = sem("gate_ready"), sem("prob_ready"), sem("cast_ready")
        parts_ready, partT_ready, partT_out = sem("parts_ready"), sem("partT_ready"), sem("partT_out")
        hid_ready, act_ready, wgt_ready, weighed_ready = sem("hid_ready"), sem("act_ready"), sem("wgt_ready"), sem("weighed_ready")
        shared_used = sem("shared_used")
        sum_ready, out_ready, turn_ready, added = sem("sum_ready"), sem("out_ready"), sem("turn_ready"), sem("added")
        NW = 14

        ORDER = [NP0] + list(range(NP0))

        def each_chunk(engine, body):
            body(0)
            with engine.Fori(1, NCH - 1) as c:
                body(c)
            body(NCH - 1)

        def is_first(c):
            return isinstance(c, int) and c == 0

        def is_last(c):
            return isinstance(c, int) and c == NCH - 1

        with nc.Block() as block:
            @block.sync
            def _(sp):
                def load(dst, src):
                    sp.dma_start(dst, src).then_inc(w_in, 16)

                sp.wait_ge(low_set, 5)
                load(gate_w[:, :], d["L0_ffn_gate_W"])
                load(route[:, :], d["L0_ffn_route_scale"].partition_broadcast(P))
                load(w1[:, :, :, :].rearrange("p m e f -> p (m e) f"), d["L0_ffn_W1"].rearrange("e d f -> d e f"))
                load(ws1[:, 0:F0], d["L0_ffn_Ws1"])
                load(w2[:, :, :], d["L0_ffn_W2"].rearrange("(m e) f d -> (e f) m d", e=2))
                load(ws2[0:F0, :], d["L0_ffn_Ws2"])
                load(b1[:, 0:NP0], d["L0_ffn_b1"])
                load(b1[0:F0, NP0:NU], d["L0_ffn_bs1"])
                for i in range(3):
                    load(b2x3[i * E0:(i + 1) * E0, :], d["L0_ffn_b2"])
                load(bs2[:, :], d["L0_ffn_bs2"])
                load(spread32[:, :, :], d["spread0"])
                load(t.mask32[:, :], d["mask"])

            @block.gpsimd
            def _(pool):
                pool.memset(padded[:, :, E0:pad], LOW).then_inc(low_set, 1)
                pool.memset(wanted[:, :, K0:8], LOW).then_inc(low_set, 1)
                pool.memset(ws1[:, F0:P], 0.0).then_inc(low_set, 1)
                pool.wait_ge(low_set, 3)
                pool.memset(ws2[F0:P, :], 0.0).then_inc(low_set, 1)
                pool.memset(b1[F0:P, NP0:NU], 0.0).then_inc(low_set, 1)
                pool.wait_ge(w_in, 16 * NW)
                pool.tensor_copy(spread[:, :, :], spread32[:, :, :]).then_inc(cast_ready, 1)
                pool.tensor_copy(identity16[:, :], t.identity[:, :]).then_inc(cast_ready, 1)

            @block.vector
            def _(dve):
                chain = Chain(dve, dve_step)
                for b in range(B):
                    half = t.x[:, b * TB:(b + 1) * TB, :].rearrange("p t (h w) -> p h t w", w=HD0)
                    src = t.attn0[:, b * S:(b + 1) * S].rearrange("p (h t w) -> p h t w", h=H0, w=HD0)
                    last = dve.tensor_tensor(half, half, src, ALU.add)
                chain.after(last)
                normalise(dve, chain, normed, t.x, moments, 1e-5, root_asked, root_given, 0, normed_ready)
                dve.wait_ge(w_in, 16 * NW)
                dve.wait_ge(low_set, 2)
                dve.wait_ge(prob_ready, 1)
                chain.after(dve.tensor_scalar(padded[:, :, 0:E0], weight[:, :, :], route[:, 0:1], None, ALU.mult))
                choose(dve, chain, padded, E0, K0, top, wanted, marked)
                chain.after(dve.tensor_tensor(weight[:, :, :], padded[:, :, 0:E0], marked[:, :, 0:E0], ALU.mult))
                chain.after(dve.tensor_tensor(total[:, 0, :], top[:, :, 0], top[:, :, 1], ALU.add))
                chain.after(dve.reciprocal(total[:, 1, :], total[:, 0, :]))
                chain.after(dve.tensor_tensor(weight[:, :, :], weight[:, :, :],
                                              total[:, 1, :].unsqueeze(2).broadcast_to([P, NT, E0]), ALU.mult))
                split_weights(dve, chain, weight[:, :, :], parts, [rest[:, :, :]]).then_inc(parts_ready, 1)

                def take_parts(c):
                    cols = slice(c * CH, (c + 1) * CH)
                    dve.wait_ge(partT_ready, c + 1)
                    chain.after(dve.tensor_copy(weightT[:, cols], part_bank[:, :]))
                    dve.tensor_copy(weightT32[:, cols], weightT[:, cols]).then_inc(partT_out, 1)

                def add(c):
                    dve.wait_ge(turn_ready, c + 1)
                    xs = t.x[:, :, :].rearrange("p t d -> p (t d)")[:, bass.ds(c * CH, CH)]
                    dve.tensor_tensor(xs, turn_bank[:, :, :].rearrange("p t d -> p (t d)"), xs, ALU.add).then_inc(added, 1)

                take_parts(0)

                def body(c):
                    for m in range(NP0):
                        dve.wait_ge(act_ready, c * NU + (m + 2))
                        dve.wait_ge(wgt_ready, c * NP0 + (m + 1))
                        wait_from(dve, sum_ready, c)
                        dve.tensor_tensor(weighed[:, m, :], hidden[:, m, :], wgt_bank[m % 2][:, :], ALU.mult).then_inc(weighed_ready, 1)
                        if is_first(c) and m + 1 < NCH:
                            take_parts(m + 1)
                        if m == NP0 - 1 and not is_first(c):
                            add(c - 1)

                each_chunk(dve, body)
                add(NCH - 1)

            @block.scalar
            def _(act):
                take_root(act, moments, root_asked, root_given, 0)
                for c in range(NCH):
                    act.wait_ge(tr_ready, c + 1)
                    act.activation(inT[:, c * CH:(c + 1) * CH], (hid_bank + wgt_bank)[c][:, :], ACT.Copy).then_inc(tr_out, 1)
                act.wait_ge(gate_ready, 1)
                act.activation(weight[:, :, :], gate_bank[:, :, :], ACT.Sigmoid).then_inc(prob_ready, 1)
                act.wait_ge(w_in, 16 * NW)

                def activate(c, j):
                    m = ORDER[j]
                    act.wait_ge(hid_ready, c * NU + (j + 1))
                    if m < NP0:
                        wait_from(act, weighed_ready, c * NP0 + (m + 1 - NP0))
                    else:
                        wait_from(act, shared_used, c)
                    act.activation(hidden[:, m, :], hid_bank[j % 2][:, :], ACT.Gelu, bias=b1[:, m:m + 1]).then_inc(act_ready, 1)

                def leave(c):
                    act.wait_ge(sum_ready, c + 1)
                    wait_from(act, turn_ready, c)
                    act.activation(outT[:, :], sum_bank[:, :], ACT.Identity, bias=bs2[:, 0:1]).then_inc(out_ready, 1)

                for j in range(NU):
                    activate(0, j)

                def body(c):
                    if not is_first(c):
                        leave(c - 1)
                    if not is_last(c):
                        for j in range(NU):
                            activate(c + 1, j)

                each_chunk(act, body)
                leave(NCH - 1)

            @block.tensor
            def _(pe):
                for c in range(NCH):
                    pe.wait_ge(normed_ready, c + 1)
                    transpose_tiles(pe, (hid_bank + wgt_bank)[c], normed, t.identity[:, :], c).then_inc(tr_ready, 1)
                pe.wait_ge(w_in, 16 * NW)
                for tile in range(NT):
                    if tile % 4 == 0:
                        pe.wait_ge(tr_out, tile // 4 + 1)
                    last = pe.matmul(gate_bank[:, tile, :], inT[:, tile * P:(tile + 1) * P], gate_w[:, :], start=True, stop=True)
                last.then_inc(gate_ready, 1)

                def up(c, j):
                    m = ORDER[j]
                    wait_from(pe, act_ready, c * NU + (j - 1 if j else 0))
                    w = w1[:, m, :, :].rearrange("p e f -> p (e f)") if m < NP0 else ws1[:, :]
                    pe.matmul(hid_bank[j % 2][:, :], w, inT[:, bass.ds(c * CH, CH)], start=True, stop=True).then_inc(hid_ready, 1)

                def spread_weights(c, m):
                    pe.matmul(wgt_bank[m % 2][:, :], spread[:, m, :], weightT[:, bass.ds(c * CH, CH)], start=True, stop=True).then_inc(wgt_ready, 1)

                def turn_parts(c):
                    wait_from(pe, partT_out, c)
                    for k in range(4):
                        last = pe.transpose(part_bank[:, k * P:(k + 1) * P],
                                            parts[:, 4 * c + k, :, :].rearrange("p a e -> p (a e)"), identity16[:, :])
                    last.then_inc(partT_ready, 1)

                def turn_sum(c):
                    pe.wait_ge(out_ready, c + 1)
                    wait_from(pe, added, c)
                    for k in range(4):
                        last = pe.transpose(turn_bank[:, k, :], outT[:, k * P:(k + 1) * P], t.identity[:, :])
                    last.then_inc(turn_ready, 1)

                for j in range(NU):
                    up(0, j)
                pe.wait_ge(cast_ready, 2)
                pe.wait_ge(parts_ready, 1)
                turn_parts(0)

                def body(c):
                    if isinstance(c, int):
                        pe.wait_ge(partT_out, c + 1)
                    for m in range(2):
                        spread_weights(c, m)
                    if not is_last(c):
                        up(c + 1, 0)
                    wait_from(pe, out_ready, c)
                    pe.wait_ge(act_ready, c * NU + 1)
                    pe.matmul(sum_bank[:, :], ws2[:, :], hidden[:, NP0, :], start=True, stop=False).then_inc(shared_used, 1)
                    pe.matmul(sum_bank[:, :], b2x3[:, :], weightT32[:, bass.ds(c * CH, CH)], start=False, stop=False)
                    for m in range(NP0):
                        pe.wait_ge(weighed_ready, c * NP0 + (m + 1))
                        last = pe.matmul(sum_bank[:, :], w2[:, m, :], weighed[:, m, :], start=False, stop=(m == NP0 - 1))
                        if m == NP0 - 1:
                            last.then_inc(sum_ready, 1)
                        if m + 2 < NP0:
                            spread_weights(c, m + 2)
                        if not is_last(c):
                            up(c + 1, m + 1)
                        if is_first(c) and m + 1 < NCH:
                            turn_parts(m + 1)
                        if m == 0 and not is_first(c):
                            turn_sum(c - 1)
                    if is_first(c):
                        pe.wait_ge(partT_out, NCH)

                each_chunk(pe, body)
                turn_sum(NCH - 1)


QB = 4
BLOCKS = [(b, q, half) for b in range(B) for half in reversed(range(TB // QB)) for q in range(GQ)]
NB = len(BLOCKS)
NS = NB * QB
TURNS = [(k, j) for k in range(NB) for j in range(QB * (BLOCKS[k][2] + 1))]
NTURN = len(TURNS)
TURNED_BY = [sum(1 for k, _ in TURNS if k <= block) for block in range(NB)]
NPROJ = 2 + 2 * GQ + 2
NROT = NPROJ - 2


USE_LAG = 2


def use(tile):
    k, j = tile
    yield "use", tile
    if j == QB * (BLOCKS[k][2] + 1) - 1:
        yield "take", k


def attention_order(last):
    units, turned = [], []
    for k in range(NB):
        width = QB * (BLOCKS[k][2] + 1)
        ahead = [QB * (k + 1) + c for c in range(QB)] if k + 1 < NB or not last else []
        scores_at = [0, 0, 2, 2] if width == QB else [0, 2, 4, 6]
        if k == 0:
            units = [(1, u) for u in range(NPROJ)]
        if k == NB // 2:
            units = [] if last else [(0, u) for u in range(NPROJ)]
        placed = None
        for j in range(width):
            if placed:
                yield "place", placed
                placed = None
            yield "turn", (k, j)
            turned.append((k, j))
            for n in (n for at, n in zip(scores_at, ahead) if at == j):
                yield "score", n
            if len(turned) > USE_LAG:
                yield from use(turned.pop(0))
            if j == 2 and k:
                yield "output", k - 1
            if j == 3 and k:
                yield "close", k - 1
            if units and j % 2:
                placed = units.pop(0)
                yield "project", placed
        if placed:
            yield "place", placed
    for tile in turned:
        yield from use(tile)
    yield "output", NB - 1
    yield "close", NB - 1


def bank_before(last, step):
    users = [e for e in attention_order(last) if e[0] in ("project", "output")]
    i = users.index(step)
    return users[i - 1] if i else None


def layer1_attention(nc, t, d):
    SLOTS = 4
    ctx = ExitStack()
    with ctx:
        def sb(name, shape, dt=F32):
            return ctx.enter_context(nc.sbuf_tensor(name, shape, dt))

        def ps(name, shape):
            return ctx.enter_context(nc.psum_tensor(name, shape, F32))

        def sem(name):
            return ctx.enter_context(nc.semaphore(name))

        normed = sb("a1_normed", [P, NT, D])
        moments = Moments(sb, "a1_token")
        inT = sb("a1_inT", [P, T])
        w_q, w_k, w_v = sb("a1_wq", [P, GQ, D1]), sb("a1_wk", [P, D1]), sb("a1_wv", [P, D1])
        w_o = sb("a1_wo", [P, GQ, D])
        kT = sb("a1_kT", [P, B, S])
        qT = sb("a1_qT", [P, B, GQ, S])
        v = sb("a1_v", [P, B, TB, D1])
        straight, swapped = sb("a1_straight", [P, 2, CH]), sb("a1_swapped", [P, 2, CH])
        crossed = sb("a1_crossed", [P, CH])
        probs = sb("a1_probs", [P, 2, QB, S])
        turned = sb("a1_turned", [P, SLOTS, CH])
        headsT = sb("a1_headsT", [P, 2, CH])
        lowest = sb("a1_lowest", [P, 2 * QB])
        weight = sb("a1_weight", [P, 4, QB])
        inverse = sb("a1_inverse", [P, 4, QB])
        part = sb("a1_part", [P, 2, QB, D])
        mask16, identity16 = sb("a1_mask16", [P, P], BF16), sb("a1_identity16", [P, P], BF16)
        scores = [ps(f"a1_scores{i}", [P, S]) for i in range(2)]
        turn_bank = [ps(f"a1_turn{i}", [P, CH]) for i in range(2)]
        sum_bank, proj_bank = ps("a1_sum", [P, CH]), ps("a1_proj", [P, CH])
        first_banks = [proj_bank] + turn_bank + [sum_bank]
        DIRECT = 4

        dve_step, root_asked, root_given = sem("dve_step"), sem("root_asked"), sem("root_given")
        normed_ready, tr_ready, tr_out = sem("normed_ready"), sem("tr_ready"), sem("tr_out")
        w_in, wo_in, cast_ready = sem("w_in"), sem("wo_in"), sem("cast_ready")
        rot_ready, straight_ready, swapped_ready = sem("rot_ready"), sem("straight_ready"), sem("swapped_ready")
        crossed_ready, rotated = sem("crossed_ready"), sem("rotated")
        v_ready, v_taken = sem("v_ready"), sem("v_taken")
        score_ready, lowest_ready, prob_ready = sem("score_ready"), sem("lowest_ready"), sem("prob_ready")
        turn_ready, used = sem("turn_ready"), sem("used")
        taken = [sem("taken_by_vector"), sem("taken_by_scalar")]
        heads_ready, out_ready, out_taken, added = sem("heads_ready"), sem("out_ready"), sem("out_taken"), sem("added")
        inverse_ready = sem("inverse_ready")

        def from_one(n):
            return n + 1

        def place_of(b, u):
            half = slice(u % 2 * CH, (u % 2 + 1) * CH)
            if u < 2:
                return kT[:, b, half]
            if u < NROT:
                return qT[:, b, (u - 2) // 2, half]
            return v[:, b, u % 2 * QB:(u % 2 + 1) * QB, :].rearrange("p t d -> p (t d)")

        def rotations(g, b, u):
            return (g * (2 * NROT) + (NROT + u + 1)) if b else (g * (2 * NROT) + (2 * NROT + u + 1))

        def copies(g, b, u):
            return (g * 4 + (2 + u - NROT + 1)) if b else (g * 4 + (4 + u - NROT + 1))

        def project(pe, bank, b, u):
            if u < NROT:
                w = w_k[:, :] if u < 2 else w_q[:, (u - 2) // 2, :]
                first = b * S + u % 2 * CH
                pe.matmul(bank[:, :], w, inT[:, first:first + CH], start=True, stop=True).then_inc(rot_ready, 1)
            else:
                for c in range(QB):
                    first = b * S + (u % 2 * QB + c) * P
                    last = pe.matmul(bank[:, c * P:(c + 1) * P], inT[:, first:first + P], w_v[:, :], start=True, stop=True)
                last.then_inc(v_ready, 1)

        def table_of(u, of):
            return t.rope[:, (2 if u < 2 else 0) + of, u % 2 * CH:(u % 2 + 1) * CH]

        def straighten(dve, bank, u, count):
            dve.wait_ge(rot_ready, from_one(count))
            if not isinstance(count, int) or count > 2:
                dve.wait_ge(rotated, from_one(count - 2))
            dve.tensor_tensor(straight[:, u % 2, :], bank[:, :], table_of(u, 0), ALU.mult).then_inc(straight_ready, 1)

        def swap(act, bank, u, count):
            act.wait_ge(straight_ready, from_one(count))
            if not isinstance(count, int) or count > 2:
                act.wait_ge(rotated, from_one(count - 2))
            for half in range(2):
                to, of = slice(half * 64, half * 64 + 64), slice(64 - half * 64, 128 - half * 64)
                last = act.activation(swapped[to, u % 2, :], bank[of, :], ACT.Copy)
            last.then_inc(swapped_ready, 1)

        def cross(dve, bank, u):
            if u >= 2:
                dve.wait_ge(rotated, from_one(u - 1))
            for half in range(2):
                to, of = slice(half * 64, half * 64 + 64), slice(64 - half * 64, 128 - half * 64)
                last = dve.tensor_tensor(swapped[to, u % 2, :], bank[of, :], table_of(u, 1)[to, :], ALU.mult)
            last.then_inc(swapped_ready, 1)

        def score(pe, n):
            k, c = divmod(n, QB)
            b, q, half = BLOCKS[k % NB]
            tile = half * QB + c
            width = (tile + 1) * P
            for first in range(0, width, CH):
                cols = min(CH, width - first)
                pe.matmul(scores[n % 2][:, first:first + cols], qT[:, b, q, tile * P:(tile + 1) * P], kT[:, b, first:first + cols],
                          start=True, stop=first + cols < width)
            pe.matmul(scores[n % 2][:, width - P:width], identity16[:, :], mask16[:, :], start=False, stop=True).then_inc(score_ready, 1)

        def row_width(n):
            return (BLOCKS[n // QB % NB][2] * QB + n % QB + 1) * P

        def find_lowest(dve, n):
            dve.tensor_reduce(out=lowest[:, n % 8:n % 8 + 1], in_=scores[n % 2][:, 0:row_width(n)], op=ALU.max, axis=AX_X,
                              negate=True).then_inc(lowest_ready, 1)

        def exponentiate(act, n):
            k, c = divmod(n, QB)
            act.activation(probs[:, k % 2, c, 0:row_width(n)], scores[n % 2][:, 0:row_width(n)], ACT.Exp,
                           bias=lowest[:, n % 8:n % 8 + 1], accum_out=weight[:, k % 4, c:c + 1]).then_inc(prob_ready, 1)

        def skipped(k, j):
            return max(0, j - BLOCKS[k][2] * QB) * P

        def copy_turned(m):
            k, j = TURNS[m]
            return turned[:, m % SLOTS, skipped(k, j):CH], turn_bank[m % 2][:, skipped(k, j):CH]

        def each_head(engine, body):
            with engine.Fori(0, KV1 - 1) as g:
                body(g, False)
            body(KV1 - 1, True)

        with nc.Block() as block:
            @block.sync
            def _(sp):
                def load(g):
                    sp.dma_start(w_q[:, :, :].rearrange("p q d -> p (q d)"), d["L1_attn_Wq"][:, bass.ds(g * (GQ * D1), GQ * D1)]).then_inc(w_in, 16)
                    sp.dma_start(w_k[:, :], d["L1_attn_Wk"][:, bass.ds(g * D1, D1)]).then_inc(w_in, 16)
                    sp.dma_start(w_v[:, :], d["L1_attn_Wv"][:, bass.ds(g * D1, D1)]).then_inc(w_in, 16)

                def load_out(g):
                    for q in range(GQ):
                        sp.dma_start(w_o[:, q, :], d["L1_attn_Wo"][bass.ds(g * (GQ * D1) + q * D1, D1), :]).then_inc(wo_in, 16)

                load(0)
                load_out(0)
                with sp.Fori(0, KV1 - 1) as g:
                    sp.wait_ge(v_ready, from_one(g * 4 + 4))
                    load(g + 1)
                    sp.wait_ge(out_ready, from_one(g * NB + NB))
                    load_out(g + 1)

            @block.gpsimd
            def _(pool):
                pool.sem_inc(rotated, 1)
                pool.sem_inc(crossed_ready, 1 + DIRECT)
                pool.sem_inc(added, 1)
                pool.tensor_copy(mask16[:, :], t.mask32[:, :]).then_inc(cast_ready, 1)
                pool.tensor_copy(identity16[:, :], t.identity[:, :]).then_inc(cast_ready, 1)

                def add_rotation(b, u, count):
                    pool.wait_ge(swapped_ready, from_one(count))
                    if not isinstance(count, int) or count > 1:
                        pool.wait_ge(rotated, from_one(count - 1))
                    pool.tensor_tensor(crossed[:, :], swapped[:, u % 2, :], table_of(u, 1), ALU.mult).then_inc(crossed_ready, 1)
                    pool.wait_ge(crossed_ready, from_one(count))
                    pool.tensor_tensor(place_of(b, u), straight[:, u % 2, :], crossed[:, :], ALU.add).then_inc(rotated, 1)

                for u in range(DIRECT):
                    pool.wait_ge(swapped_ready, from_one(u + 1))
                    pool.tensor_tensor(place_of(0, u), straight[:, u % 2, :], swapped[:, u % 2, :], ALU.add).then_inc(rotated, 1)
                for u in range(DIRECT, NROT):
                    add_rotation(0, u, u + 1)

                def body(g, last):
                    for what, n in attention_order(last):
                        if what == "place" and n[1] < NROT:
                            add_rotation(*n, rotations(g, *n))
                        if what == "close":
                            b, _, half = BLOCKS[n]
                            xs = t.x[:, b * TB + half * QB:b * TB + half * QB + QB, :]
                            pool.wait_ge(out_taken, from_one(g * NB + (n + 1)))
                            pool.wait_ge(added, from_one(g * NB + n))
                            pool.tensor_tensor(xs, xs, part[:, n % 2, :, :], ALU.add).then_inc(added, 1)

                each_head(pool, body)

            @block.vector
            def _(dve):
                chain = Chain(dve, dve_step)
                for s in (straight_ready, lowest_ready, taken[0], out_taken, inverse_ready):
                    dve.sem_inc(s, 1)
                normalise(dve, chain, normed, t.x, moments, 1e-5, root_asked, root_given, 0, normed_ready)
                for u in range(NROT):
                    straighten(dve, first_banks[u % 4], u, u + 1)
                    if u < DIRECT:
                        cross(dve, first_banks[u % 4], u)
                for n in range(QB):
                    dve.wait_ge(score_ready, from_one(n + 1))
                    find_lowest(dve, n)

                def body(g, last):
                    for what, n in attention_order(last):
                        if what == "turn" and TURNS.index(n) % 2 == 0:
                            m = TURNS.index(n)
                            dve.wait_ge(turn_ready, from_one(g * NTURN + (m + 1)))
                            dve.wait_ge(used, from_one(g * NTURN + max(m - SLOTS + 1, 0)))
                            dve.tensor_copy(*copy_turned(m)).then_inc(taken[0], 1)
                        if what == "place" and n[1] < NROT:
                            straighten(dve, proj_bank, n[1], rotations(g, *n))
                        if what == "score":
                            dve.wait_ge(score_ready, from_one(g * NS + (n + 1)))
                            find_lowest(dve, n)
                        if what == "close":
                            dve.wait_ge(prob_ready, from_one(g * NS + (QB * n + QB)))
                            dve.reciprocal(inverse[:, n % 4, :], weight[:, n % 4, :]).then_inc(inverse_ready, 1)
                            dve.wait_ge(inverse_ready, from_one(g * NB + (n + 1)))
                            dve.wait_ge(out_ready, from_one(g * NB + (n + 1)))
                            dve.wait_ge(added, from_one(g * NB + max(n - 1, 0)))
                            dve.tensor_tensor(part[:, n % 2, :, :], proj_bank[:, :].rearrange("p (t d) -> p t d", d=D),
                                              inverse[:, n % 4, :].unsqueeze(2).broadcast_to([P, QB, D]), ALU.mult).then_inc(out_taken, 1)

                each_head(dve, body)

            @block.scalar
            def _(act):
                for s in (swapped_ready, v_taken, prob_ready, taken[1], heads_ready):
                    act.sem_inc(s, 1)
                take_root(act, moments, root_asked, root_given, 0)
                for c in range(NCH):
                    act.wait_ge(tr_ready, c + 1)
                    act.activation(inT[:, c * CH:(c + 1) * CH], scores[c // 2][:, c % 2 * CH:(c % 2 + 1) * CH], ACT.Copy).then_inc(tr_out, 1)
                for u in range(DIRECT, NROT):
                    swap(act, first_banks[u % 4], u, u + 1)
                for i in range(2):
                    act.wait_ge(v_ready, from_one(i + 1))
                    act.activation(place_of(0, NROT + i), first_banks[(NROT + i) % 4][:, :], ACT.Copy).then_inc(v_taken, 1)
                for n in range(QB):
                    act.wait_ge(lowest_ready, from_one(n + 1))
                    exponentiate(act, n)

                def body(g, last):
                    for what, n in attention_order(last):
                        if what == "turn" and TURNS.index(n) % 2 == 1:
                            m = TURNS.index(n)
                            act.wait_ge(turn_ready, from_one(g * NTURN + (m + 1)))
                            act.wait_ge(used, from_one(g * NTURN + max(m - SLOTS + 1, 0)))
                            act.activation(*copy_turned(m), ACT.Copy).then_inc(taken[1], 1)
                        if what == "place" and n[1] < NROT:
                            swap(act, proj_bank, n[1], rotations(g, *n))
                        if what == "place" and n[1] >= NROT:
                            act.wait_ge(v_ready, from_one(copies(g, *n)))
                            act.activation(place_of(*n), proj_bank[:, :], ACT.Copy).then_inc(v_taken, 1)
                        if what == "score":
                            k = n // QB
                            act.wait_ge(lowest_ready, from_one(g * NS + (n + 1)))
                            act.wait_ge(turn_ready, from_one(g * NTURN + (TURNED_BY[k - 2] if k >= 2 else 0)))
                            exponentiate(act, n)
                        if what == "take":
                            act.wait_ge(used, from_one(g * NTURN + TURNED_BY[n]))
                            act.wait_ge(out_ready, from_one(g * NB + max(n - 1, 0)))
                            act.activation(headsT[:, n % 2, :], sum_bank[:, :], ACT.Copy).then_inc(heads_ready, 1)

                each_head(act, body)

            @block.tensor
            def _(pe):
                for s in (rot_ready, v_ready, score_ready, turn_ready, used, out_ready):
                    pe.sem_inc(s, 1)
                for c in range(NCH):
                    pe.wait_ge(normed_ready, c + 1)
                    transpose_tiles(pe, scores[c // 2][:, c % 2 * CH:(c % 2 + 1) * CH], normed, t.identity[:, :], c).then_inc(tr_ready, 1)
                pe.wait_ge(w_in, 48)
                pe.wait_ge(cast_ready, 2)
                for u in range(NPROJ):
                    if u < 2:
                        pe.wait_ge(tr_out, u + 1)
                    if u >= 4:
                        pe.wait_ge(swapped_ready, from_one(u - 3))
                    project(pe, first_banks[u % 4], 0, u)
                pe.wait_ge(rotated, from_one(DIRECT))
                pe.wait_ge(tr_out, NCH)
                for n in range(QB):
                    if n >= 2:
                        pe.wait_ge(prob_ready, from_one(n - 1))
                    score(pe, n)
                pe.wait_ge(rotated, from_one(NROT))
                pe.wait_ge(v_taken, from_one(2))

                def body(g, last):
                    for what, n in attention_order(last):
                        if what in ("project", "output"):
                            before = bank_before(last, (what, n))
                            if before is None or before[0] == "output":
                                pe.wait_ge(out_taken, from_one(g * NB + (before[1] + 1 if before else 0)))
                            elif before[1][1] < NROT:
                                pe.wait_ge(swapped_ready, from_one(rotations(g, *before[1])))
                            else:
                                pe.wait_ge(v_taken, from_one(copies(g, *before[1])))
                        if what == "project":
                            if n == (0, 0):
                                pe.wait_ge(w_in, (g + 2) * 48)
                            project(pe, proj_bank, *n)
                        if what == "score":
                            k = n // QB
                            if n % QB == 0 and k % (NB // B) == 0:
                                pe.wait_ge(rotated, from_one(rotations(g, 1 if k < NB else 0, NROT - 1)))
                            pe.wait_ge(prob_ready, from_one(g * NS + (n - 1)))
                            score(pe, n)
                        if what == "turn":
                            k, j = n
                            m = TURNS.index(n)
                            if j == 0:
                                pe.wait_ge(prob_ready, from_one(g * NS + QB * (k + 1)))
                            pe.wait_ge(taken[m % 2], from_one(g * (NTURN // 2) + m // 2))
                            for c in range(skipped(k, j) // P, QB):
                                last_turn = pe.transpose(turn_bank[m % 2][:, c * P:(c + 1) * P], probs[:, k % 2, c, j * P:(j + 1) * P], t.identity[:, :])
                            last_turn.then_inc(turn_ready, 1)
                        if what == "use":
                            k, j = n
                            m = TURNS.index(n)
                            if j == 0:
                                pe.wait_ge(heads_ready, from_one(g * NB + k))
                                pe.wait_ge(v_taken, from_one(g * 4 + (2 if k < NB // B else 4)))
                            pe.wait_ge(taken[m % 2], from_one(g * (NTURN // 2) + (m // 2 + 1)))
                            pe.matmul(sum_bank[:, skipped(k, j):CH], v[:, BLOCKS[k][0], j, :], turned[:, m % SLOTS, skipped(k, j):CH],
                                      start=(j == 0), stop=(TURNED_BY[k] == m + 1)).then_inc(used, 1)
                        if what == "output":
                            pe.wait_ge(heads_ready, from_one(g * NB + (n + 1)))
                            if n == 0:
                                pe.wait_ge(wo_in, (g + 1) * 32)
                            for c in range(QB):
                                last_out = pe.matmul(proj_bank[:, c * P:(c + 1) * P], headsT[:, n % 2, c * P:(c + 1) * P],
                                                     w_o[:, BLOCKS[n][1], :], start=True, stop=True)
                            last_out.then_inc(out_ready, 1)

                each_head(pe, body)


def layer1_mixture(nc, t, d, out):
    pad = E1 + 8 - K1
    SIDE = LIMIT + 1.0
    ctx = ExitStack()
    with ctx:
        def sb(name, shape, dt=F32):
            return ctx.enter_context(nc.sbuf_tensor(name, shape, dt))

        def ps(name, shape, dt=F32):
            return ctx.enter_context(nc.psum_tensor(name, shape, dt))

        def sem(name):
            return ctx.enter_context(nc.semaphore(name))

        normed = sb("m1_normed", [P, NT, D])
        layer_in = sb("m1_layer_in", [P, NT, D])
        inT = sb("m1_inT", [P, T])
        moments = Moments(sb, "m1_token")
        first_inverse = sb("m1_first_inverse", [P, NT])
        scaleT = sb("m1_scaleT", [P, 1])
        gate_w, gate_b = sb("m1_gate_w", [P, E1]), sb("m1_gate_b", [P, E1])
        w1 = [sb(f"m1_w1_{i}", [P, F1]) for i in range(2)]
        w2 = [sb(f"m1_w2_{i}", [P, D]) for i in range(2)]
        b1, b2 = sb("m1_b1", [P, E1]), sb("m1_b2", [E1, D])
        padded = sb("m1_padded", [P, NT, pad])
        marked = sb("m1_marked", [P, NT, pad])
        top, wanted = sb("m1_top", [P, NT, 8]), sb("m1_wanted", [P, NT, 8])
        weight = sb("m1_weight", [P, NT, E1])
        powers = sb("m1_powers", [P, NT, E1])
        total = sb("m1_total", [P, 2, NT])
        weightT = sb("m1_weightT", [E1, T])
        column = [sb(f"m1_column{i}", [P, NT, 1]) for i in range(2)]
        linear, sigm = sb("m1_linear", [P, 4, CH]), sb("m1_sigm", [P, 4, CH])
        gated = sb("m1_gated", [P, 4, CH])
        scaled = sb("m1_scaled", [P, 2, 4, D])
        AHEAD, AHEAD_LOW = 3, 4
        hid_bank = [ps(f"m1_hid{i}", [P, CH]) for i in range(4)]
        down_bank = [ps(f"m1_down{i}", [P, 4, D]) for i in range(2)]
        spare_bank = [ps(f"m1_spare{i}", [P, CH]) for i in range(2)]
        gate_bank = down_bank[0][:, 0:NT * E1 // D, :].rearrange("p k d -> p (k d)").rearrange("p (t e) -> p t e", e=E1)

        w_in, dve_step, root_asked, root_given = sem("w_in"), sem("dve_step"), sem("root_asked"), sem("root_given")
        low_set, normed_ready, tr_ready, tr_out = sem("low_set"), sem("normed_ready"), sem("tr_ready"), sem("tr_out")
        input_ready, residual_ready = sem("input_ready"), sem("residual_ready")
        gate_taken = sem("gate_taken")
        gate_ready, exp_asked, exp_given, weight_ready = sem("gate_ready"), sem("exp_asked"), sem("exp_given"), sem("weight_ready")
        wT_ready, wT_out, bias_ready, bias_added = sem("wT_ready"), sem("wT_out"), sem("bias_ready"), sem("bias_added")
        up_in = [sem(f"up_in{i}") for i in range(2)]
        down_in = [sem(f"down_in{i}") for i in range(2)]
        column_ready = sem("column_ready")
        hid_ready, linear_ready, sigm_ready, gated_ready = sem("hid_ready"), sem("linear_ready"), sem("sigm_ready"), sem("gated_ready")
        down_ready, scaled_ready, added, stored = sem("down_ready"), sem("scaled_ready"), sem("added"), sem("stored")
        NW = 5
        N = 2 * NCH
        PAIRS = E1 // 2

        def each_pair(engine, body):
            body(0)
            with engine.Fori(1, PAIRS - 1) as i:
                body(i)
            body(PAIRS - 1)

        def is_last(i):
            return isinstance(i, int) and i == PAIRS - 1

        def is_first(i):
            return isinstance(i, int) and i == 0

        with nc.Block() as block:
            @block.sync
            def _(sp):
                def load(dst, src):
                    sp.dma_start(dst, src).then_inc(w_in, 16)

                def load_up(e, par):
                    sp.dma_start(w1[par][:, :], d["L1_ffn_mlp1_w"][bass.ds(e * P, P), :]).then_inc(up_in[par], 16)

                def load_down(e, par):
                    sp.dma_start(w2[par][:, :], d["L1_ffn_mlp2_w"][bass.ds(e * P, P), :]).then_inc(down_in[par], 16)

                load(scaleT[:, :], d["L1_ffn_scale"].rearrange("(p a) -> p a", a=1))
                load(gate_w[:, :], d["L1_ffn_gate_w"])
                load(gate_b[:, :], d["L1_ffn_gate_b"].partition_broadcast(P))
                load(b1[:, :], d["L1_ffn_mlp1_b"])
                load(b2[:, :], d["L1_ffn_mlp2_b"])
                for par in range(2):
                    load_up(par, par)
                    load_down(par, par)
                with sp.Fori(0, PAIRS - 1) as i:
                    for par in range(2):
                        sp.wait_ge(hid_ready, i * N + (par + 1) * NCH)
                        load_up(i * 2 + (par + 2), par)
                        sp.wait_ge(down_ready, i * N + (par + 1) * NCH)
                        load_down(i * 2 + (par + 2), par)
                for c in range(NCH):
                    sp.wait_ge(added, (E1 - 1) * NCH + c + 1)
                    b, first = c // (NCH // B), c % (NCH // B) * CH
                    sp.dma_start(out[b, first:first + CH, :].rearrange("(t p) d -> p t d", p=P), t.x[:, 4 * c:4 * c + 4, :]).then_inc(stored, 16)
                sp.wait_ge(stored, 16 * NCH)

            @block.gpsimd
            def _(pool):
                pool.memset(padded[:, :, E1:pad], LOW).then_inc(low_set, 1)
                pool.memset(wanted[:, :, K1:8], LOW).then_inc(low_set, 1)
                pool.wait_ge(input_ready, NCH)
                pool.tensor_tensor(t.x[:, :, :], t.x[:, :, :], layer_in[:, :, :], ALU.add).then_inc(residual_ready, 1)

                def body(i):
                    for n in range(N):
                        pool.wait_ge(sigm_ready, i * N + (n + 1))
                        wait_from(pool, down_ready, i * N + (n - 3))
                        pool.tensor_tensor(gated[:, n % 4, :], linear[:, n % 4, :], sigm[:, n % 4, :], ALU.mult).then_inc(gated_ready, 1)

                each_pair(pool, body)

            @block.vector
            def _(dve):
                chain = Chain(dve, dve_step)
                find_moments(dve, chain, t.x, moments)
                dve.tensor_scalar(moments.of_root[:, :], moments.variance, 1e-5, None, ALU.add).then_inc(root_asked, 1)
                dve.wait_ge(root_given, 1)
                chain.after(dve.reciprocal(first_inverse[:, :], moments.root[:, :]))
                chain.after(dve.tensor_tensor(moments.of_root[:, :], first_inverse[:, :], first_inverse[:, :], ALU.mult))
                chain.after(dve.tensor_tensor(moments.of_root[:, :], moments.of_root[:, :], moments.variance, ALU.mult))
                dve.tensor_scalar(moments.of_root[:, :], moments.of_root[:, :], 1e-5, None, ALU.add).then_inc(root_asked, 1)
                dve.wait_ge(root_given, 2)
                chain.after(dve.reciprocal(moments.inverse[:, :], moments.root[:, :]))
                chain.after(dve.tensor_tensor(moments.inverse[:, :], moments.inverse[:, :], first_inverse[:, :], ALU.mult))
                for dst, inverse, ready in ((normed, moments.inverse, normed_ready), (layer_in, first_inverse, input_ready)):
                    for tile in range(NT):
                        last = dve.tensor_scalar(dst[:, tile, :], t.x[:, tile, :], moments.both[:, tile, 0:1], inverse[:, tile:tile + 1],
                                                 ALU.subtract, ALU.mult)
                        if tile % 4 == 3:
                            last.then_inc(ready, 1)

                def lower(i, n):
                    dve.wait_ge(hid_ready, i * N + (n + 1))
                    wait_from(dve, gated_ready, i * N + (n - 3))
                    dve.tensor_scalar(linear[:, n % 4, :], hid_bank[n % 4][:, :], b1[:, bass.ds(i * 2 + n // NCH, 1)], LIMIT,
                                      ALU.add, ALU.min).then_inc(linear_ready, 1)

                def fetch(i, par):
                    dve.tensor_scalar(column[par][:, :, :], weight[:, :, bass.ds(i * 2 + par, 1)], SIDE, None, ALU.mult).then_inc(column_ready, 1)

                dve.wait_ge(w_in, 16 * NW)
                for n in range(AHEAD_LOW):
                    lower(0, n)
                dve.wait_ge(low_set, 2)
                dve.wait_ge(gate_ready, 1)
                dve.tensor_tensor(padded[:, :, 0:E1], gate_bank, gate_b[:, :].unsqueeze(1).broadcast_to([P, NT, E1]),
                                  ALU.add).then_inc(gate_taken, 1)
                dve.wait_ge(gate_taken, 1)
                choose(dve, chain, padded, E1, K1, top, wanted, marked)
                dve.tensor_tensor(weight[:, :, :], padded[:, :, 0:E1], top[:, :, 0].unsqueeze(2).broadcast_to([P, NT, E1]),
                                  ALU.subtract).then_inc(exp_asked, 1)
                dve.wait_ge(exp_given, 1)
                chain.after(dve.tensor_tensor(weight[:, :, :], powers[:, :, :], marked[:, :, 0:E1], ALU.mult))
                chain.after(dve.reduce_sum(total[:, 0, :], weight[:, :, :], AX_X))
                chain.after(dve.reciprocal(total[:, 1, :], total[:, 0, :]))
                dve.tensor_tensor(weight[:, :, :], weight[:, :, :], total[:, 1, :].unsqueeze(2).broadcast_to([P, NT, E1]),
                                  ALU.mult).then_inc(weight_ready, 1)
                dve.wait_ge(weight_ready, 1)
                for par in range(2):
                    fetch(0, par)
                dve.wait_ge(residual_ready, 1)

                def body(i):
                    for n in range(N):
                        if n + AHEAD_LOW < N or not is_last(i):
                            lower(i, n + AHEAD_LOW)
                        if is_first(i) and n >= N - NCH:
                            c = n - (N - NCH)
                            xs = t.x[:, 4 * c:4 * c + 4, :]
                            dve.wait_ge(bias_ready, c + 1)
                            dve.wait_ge(added, n - NCH + 1)
                            dve.tensor_tensor(xs, spare_bank[c % 2][:, :].rearrange("p (t d) -> p t d", d=D), xs, ALU.add).then_inc(bias_added, 1)
                            dve.wait_ge(bias_added, c + 1)
                        c = n % NCH
                        xs = t.x[:, 4 * c:4 * c + 4, :]
                        dve.wait_ge(scaled_ready, i * N + (n + 1))
                        wait_from(dve, added, i * N + (n + 1 - NCH))
                        dve.tensor_tensor(xs, xs, scaled[:, n % 2, :, :], ALU.add).then_inc(added, 1)
                        if n in (NCH - 1, N - 1) and not is_last(i):
                            fetch(i + 1, n // NCH)

                each_pair(dve, body)

            @block.scalar
            def _(act):
                take_root(act, moments, root_asked, root_given, 0)
                take_root(act, moments, root_asked, root_given, 1)
                act.wait_ge(w_in, 16 * NW)
                for c in range(NCH):
                    act.wait_ge(tr_ready, c + 1)
                    act.activation(inT[:, c * CH:(c + 1) * CH], spare_bank[c % 2][:, :], ACT.Copy, scale=scaleT[:, 0:1]).then_inc(tr_out, 1)

                def sigmoid(i, n):
                    act.wait_ge(linear_ready, i * N + (n + 1))
                    wait_from(act, gated_ready, i * N + (n - 3))
                    act.activation(sigm[:, n % 4, :], linear[:, n % 4, :], ACT.Sigmoid, scale=ALPHA).then_inc(sigm_ready, 1)

                for n in range(AHEAD):
                    sigmoid(0, n)
                act.wait_ge(exp_asked, 1)
                act.activation(powers[:, :, :], weight[:, :, :], ACT.Exp).then_inc(exp_given, 1)

                def body(i):
                    for n in range(N):
                        if n + AHEAD < N or not is_last(i):
                            sigmoid(i, n + AHEAD)
                        if is_first(i) and n >= N - NCH:
                            c = n - (N - NCH)
                            act.wait_ge(wT_ready, c + 1)
                            act.activation(weightT[:, c * CH:(c + 1) * CH], spare_bank[c % 2][0:E1, :], ACT.Copy).then_inc(wT_out, 1)
                        act.wait_ge(down_ready, i * N + (n + 1))
                        act.wait_ge(column_ready, i * 2 + (n // NCH + 1))
                        wait_from(act, added, i * N + (n - 1))
                        for k in range(4):
                            tile = n % NCH * 4 + k
                            last = act.activation(scaled[:, n % 2, k, :], down_bank[n % 2][:, k, :], ACT.Copy,
                                                  scale=column[n // NCH][:, tile, :])
                        last.then_inc(scaled_ready, 1)

                each_pair(act, body)

            @block.tensor
            def _(pe):
                for c in range(NCH):
                    pe.wait_ge(normed_ready, c + 1)
                    if c >= 2:
                        pe.wait_ge(tr_out, c - 1)
                    transpose_tiles(pe, spare_bank[c % 2], normed, t.identity[:, :], c).then_inc(tr_ready, 1)
                pe.wait_ge(w_in, 16 * NW)

                def up(i, n):
                    par, c = n // NCH % 2, n % NCH
                    if c == 0:
                        pe.wait_ge(up_in[par], i * 16 + (n // N + 1) * 16)
                    if is_first(i) and n < NCH:
                        pe.wait_ge(tr_out, c + 1)
                    wait_from(pe, linear_ready, i * N + (n - 3))
                    pe.matmul(hid_bank[n % 4][:, :], w1[par][:, :], inT[:, c * CH:(c + 1) * CH], start=True, stop=True).then_inc(hid_ready, 1)

                for n in range(AHEAD):
                    up(0, n)
                pe.wait_ge(tr_out, NCH)
                for tile in range(NT):
                    last = pe.matmul(gate_bank[:, tile, :], inT[:, tile * P:(tile + 1) * P], gate_w[:, :], start=True, stop=True)
                last.then_inc(gate_ready, 1)

                def body(i):
                    for n in range(N):
                        if n + AHEAD < N or not is_last(i):
                            up(i, n + AHEAD)
                        par = n // NCH
                        if is_first(i) and n >= N - NCH:
                            c = n - (N - NCH)
                            pe.wait_ge(weight_ready, 1)
                            if c >= 2:
                                pe.wait_ge(bias_added, c - 1)
                            for k in range(4):
                                last = pe.transpose(spare_bank[c % 2][0:E1, k * P:(k + 1) * P], weight[:, 4 * c + k, :], t.identity[:, :])
                            last.then_inc(wT_ready, 1)
                        if n % NCH == 0:
                            pe.wait_ge(down_in[par], i * 16 + 16)
                        if is_first(i) and n == 0:
                            pe.wait_ge(gate_taken, 1)
                        pe.wait_ge(gated_ready, i * N + (n + 1))
                        wait_from(pe, scaled_ready, i * N + (n - 1))
                        for k in range(4):
                            last = pe.matmul(down_bank[n % 2][:, k, :], gated[:, n % 4, k * P:(k + 1) * P], w2[par][:, :], start=True, stop=True)
                        last.then_inc(down_ready, 1)
                        if is_first(i) and n >= N - NCH:
                            pe.wait_ge(wT_out, c + 1)
                            for k in range(4):
                                last = pe.matmul(spare_bank[c % 2][:, k * P:(k + 1) * P], weightT[:, (4 * c + k) * P:(4 * c + k + 1) * P],
                                                 b2[:, :], start=True, stop=True)
                            last.then_inc(bias_ready, 1)

                each_pair(pe, body)


def two_layers(nc, d, out):
    t = Tensors()
    ctx = ExitStack()
    with ctx:
        def sb(name, shape, dt=F32):
            return ctx.enter_context(nc.sbuf_tensor(name, shape, dt))

        t.x = sb("x", [P, NT, D])
        t.identity = sb("identity", [P, P])
        t.mask32 = sb("mask32", [P, P])
        t.rope = sb("rope", [P, 4, S])
        t.values0 = sb("values0", [P, B * H0 * TB * HD0])
        t.attn0 = sb("attn0", [P, B * H0 * TB * HD0])
        t.parts_dram = [nc.dram_tensor(f"{name}_parts", (3, B * P, S), BF16, kind="Internal").ap() for name in ("q", "k")]
        with ExitStack() as early:
            def early_sb(name, shape, dt=F32):
                return early.enter_context(nc.sbuf_tensor(name, shape, dt))

            t.normed0 = early_sb("normed0", [P, NT, D])
            t.affine0 = early_sb("affine0", [P, 2, D])
            t.q_stack = [early_sb(f"q_stack{i}", [P, S], BF16) for i in range(STACKS)]
            t.k_stack = [[early_sb(f"k_stack{i}_{x}", [P, S], BF16) for x in range(2)] for i in range(STACKS)]
            layer0_project(nc, t, d)
            layer0_attention(nc, t)
        layer0_mixture(nc, t, d)
        layer1_attention(nc, t, d)
        layer1_mixture(nc, t, d, out)


def shape_constants():
    import numpy as np
    f32 = np.float32
    half = (np.arange(0, D1, 2, dtype=f32) / f32(D1)).astype(f32)
    inverse_frequency = (f32(1.0) / np.power(f32(10000.0), half)).astype(f32)
    angle = np.outer(np.arange(S, dtype=f32), inverse_frequency).astype(f32)
    cos, sin = np.cos(angle).T, np.sin(angle).T
    cos, sin = np.concatenate([cos, cos]), np.concatenate([-sin, sin])
    scale = f32(1.0) / np.sqrt(f32(D1))
    rope = np.stack([cos * scale, sin * scale, cos, sin]).astype(f32)
    spread0 = np.zeros((3, E0, E0 * F0 // P, P), f32)
    for e in range(E0):
        m, side = divmod(e, 2)
        spread0[:, e, m, side * F0:(side + 1) * F0] = 1.0
    later = np.triu(np.ones((P, P), bool), 1)
    return {"identity": np.eye(P, dtype=f32), "mask": np.where(later, f32(LOW), f32(0.0)).astype(f32),
            "rope": rope, "spread0": spread0.reshape(3 * E0, -1, P)}


def kernel(**inputs):
    import numpy as np
    import concourse.bacc as bacc
    from concourse import mybir as my
    from concourse.bass_utils import run_bass_kernel_spmd as run

    arrays = {name: np.asarray(a) for name, a in inputs.items()}
    arrays["L1_ffn_gate_w"] = arrays["L1_ffn_gate_w"].T
    arrays["L1_ffn_mlp1_w"] = arrays["L1_ffn_mlp1_w"][:, ::2, :].transpose(0, 2, 1).reshape(E1 * P, F1)
    arrays["L1_ffn_mlp1_b"] = arrays["L1_ffn_mlp1_b"][:, ::2].T
    arrays["L1_ffn_mlp2_w"] = arrays["L1_ffn_mlp2_w"].transpose(0, 2, 1).reshape(E1 * F1, D)
    arrays["L0_ffn_b1"] = arrays["L0_ffn_b1"].reshape(E0 * F0 // P, P).T
    arrays["L0_ffn_bs1"] = arrays["L0_ffn_bs1"].reshape(F0, 1)
    arrays["L0_ffn_bs2"] = arrays["L0_ffn_bs2"].reshape(D, 1)
    arrays["L0_ffn_route_scale"] = arrays["L0_ffn_route_scale"].reshape(1)
    arrays.update(shape_constants())

    nc = bacc.Bacc("TRN2", target_bir_lowering=False, num_devices=1)
    given, d = {}, {}
    for name, a in arrays.items():
        a = np.ascontiguousarray(a)
        given[f"in_{name}"] = a
        d[name] = nc.dram_tensor(f"in_{name}", a.shape, my.dt.from_np(a.dtype), kind="ExternalInput").ap()
    out = nc.dram_tensor("out_0", (B, S, D), F32, kind="ExternalOutput").ap()
    two_layers(nc, d, out)
    r = run(nc, [given], core_ids=[0])
    return r.results[0]["out_0"]
```
